# Optimizing a Trainium2 kernel written in Bass

```python
import numpy as np
import jax
import jax.numpy as jnp

def _softmax(x, axis=-1):
    return jax.nn.softmax(x, axis=axis)

def _gelu(x):
    return jax.nn.gelu(x, approximate=True)

def _silu(x):
    return jax.nn.silu(x)

def _sigmoid(x):
    return jax.nn.sigmoid(x)

def _layernorm(x, axis=-1, eps=1e-05):
    m = jnp.mean(x, axis=axis, keepdims=True)
    v = jnp.var(x, axis=axis, keepdims=True)
    return (x - m) / jnp.sqrt(v + eps)

def _scatter_add(tgt, idx, src, axis=0):
    return tgt.at[idx].add(src)

def _segment_sum(src, seg, n):
    return jax.ops.segment_sum(src, seg, n)
kernel_name = 'mk_decoder_preln_d4_seqx_r8_9ecb3f'

def setup_inputs(seed: int=0):
    np.random.seed(seed)
    _w = jnp.asarray

    def _rec_inputs():
        import jax
        import jax.numpy as jnp
        _rk = jax.random.key(seed)
        x = -0.0002928 + 1 * jax.random.normal(jax.random.fold_in(_rk, 1), (32, 128, 128), jnp.float32)
        _lenS = 128 - jax.random.randint(jax.random.fold_in(_rk, 7), (32,), 0, max(1, 128 // 4) + 1, jnp.int32)
        _lenS2 = 120 - jax.random.randint(jax.random.fold_in(_rk, 8), (32,), 0, max(1, 120 // 4) + 1, jnp.int32)
        _ctx_768P = jax.random.normal(jax.random.fold_in(_rk, 11), (32, 16, 96), jnp.float32)
        _ctx_768c = jax.random.dirichlet(jax.random.fold_in(_rk, 511), 0.3 * jnp.ones((16,), jnp.float32), (32, 120))
        _ctx_768t = jnp.einsum('bsk,bkd->bsd', _ctx_768c, _ctx_768P)
        _ctx_768t = _ctx_768t * jax.lax.rsqrt(jnp.mean(jnp.square(_ctx_768t)) + 1e-12) * 0.953939
        ctx_768 = 2.09791e-05 + 1.00001 * (_ctx_768t + 0.3 * jax.random.normal(jax.random.fold_in(_rk, 611), (32, 120, 96), jnp.float32))
        _validS = jnp.arange(128)[None, :] < _lenS[:, None]
        _validS2 = jnp.arange(120)[None, :] < _lenS2[:, None]
        _causal = jnp.tril(jnp.ones((128, 128), dtype=bool))
        mask_BxS2_bk0 = jnp.logical_not(jnp.broadcast_to(_validS2[:, :], (32, 120)))
        mask_BxS_bf1 = jnp.ones((32, 128), dtype=bool)
        mask_BxS2_bf1 = jnp.ones((32, 120), dtype=bool)
        return (x, ctx_768, mask_BxS2_bk0, mask_BxS_bf1, mask_BxS2_bf1)
    x, ctx_768, mask_BxS2_bk0, mask_BxS_bf1, mask_BxS2_bf1 = _rec_inputs()

    def _L0_attn_setup():
        import jax, jax.numpy as jnp
        import numpy as np
        SCALING = 1.0
        H, N = (128, 64)
        B, L = (4, 256)
        key = jax.random.key(seed)
        ks = jax.random.split(key, 10)
        x = jax.random.normal(ks[0], (B, L, H), dtype=jnp.float32)
        in_proj = jax.random.normal(ks[1], (H, N), dtype=jnp.float32)
        out_proj = jax.random.normal(ks[2], (N, H), dtype=jnp.float32)
        lo, hi = (np.log(0.01), np.log(100.0))
        frequencies = jnp.exp(jax.random.uniform(ks[3], (N,)) * (hi - lo) + lo) / SCALING
        decays = jnp.full((N,), np.log(0.5), dtype=jnp.float32)
        s = 1.0 / np.sqrt(H)
        ss_W = jax.random.uniform(ks[4], (H, H), minval=-s, maxval=s)
        ss_b = jax.random.uniform(ks[5], (H,), minval=-s, maxval=s)
        gate_W = jax.random.uniform(ks[6], (H, H), minval=-s, maxval=s)
        gate_b = jax.random.uniform(ks[7], (H,), minval=-s, maxval=s)
        fin_W = jax.random.uniform(ks[8], (H, H), minval=-s, maxval=s)
        fin_b = jax.random.uniform(ks[9], (H,), minval=-s, maxval=s)
        return {'x': x, 'in_proj': in_proj, 'out_proj': out_proj, 'frequencies': frequencies, 'decays': decays, 'ss_W': ss_W, 'ss_b': ss_b, 'gate_W': gate_W, 'gate_b': gate_b, 'fin_W': fin_W, 'fin_b': fin_b}
    _L0_attn_all = _L0_attn_setup()
    _L0_attn_in = {k: v for k, v in _L0_attn_all.items() if k in ('in_proj', 'out_proj', 'frequencies', 'decays', 'ss_W', 'ss_b', 'gate_W', 'gate_b', 'fin_W', 'fin_b')}
    del _L0_attn_all

    def _L0_xattn_setup():
        import jax, jax.numpy as jnp
        import numpy as np
        QUERY_DIM, KV_DIM, EMBED_DIM, NUM_HEADS = (128, 96, 128, 16)
        HEAD_DIM = EMBED_DIM // NUM_HEADS
        SCALE = HEAD_DIM ** (-0.5)
        LN_EPS = 1e-05

        def _l2norm(x, eps=1e-12):
            n = jnp.sqrt(jnp.sum(x * x, axis=-1, keepdims=True))
            return x / jnp.maximum(n, eps)
        key = jax.random.key(seed)
        ks = jax.random.split(key, 12)
        B, Nq, Nk = (2, 256, 256)
        s = lambda d: 1.0 / np.sqrt(d)
        return {'query': jax.random.normal(ks[0], (B, Nq, QUERY_DIM), jnp.float32), 'key': jax.random.normal(ks[1], (B, Nk, KV_DIM), jnp.float32), 'value': jax.random.normal(ks[2], (B, Nk, KV_DIM), jnp.float32), 'Wq': jax.random.normal(ks[3], (QUERY_DIM, EMBED_DIM), jnp.float32) * s(QUERY_DIM), 'bq': jnp.zeros((EMBED_DIM,), jnp.float32), 'Wk': jax.random.normal(ks[4], (KV_DIM, EMBED_DIM), jnp.float32) * s(KV_DIM), 'bk': jnp.zeros((EMBED_DIM,), jnp.float32), 'Wv': jax.random.normal(ks[5], (KV_DIM, EMBED_DIM), jnp.float32) * s(KV_DIM), 'bv': jnp.zeros((EMBED_DIM,), jnp.float32), 'Wo': jax.random.normal(ks[6], (EMBED_DIM, EMBED_DIM), jnp.float32) * s(EMBED_DIM), 'bo': jnp.zeros((EMBED_DIM,), jnp.float32), 'ln_gamma': jnp.ones((EMBED_DIM,), jnp.float32), 'ln_beta': jnp.zeros((EMBED_DIM,), jnp.float32)}
    _L0_xattn_all = _L0_xattn_setup()
    _L0_xattn_in = {k: v for k, v in _L0_xattn_all.items() if k in ('Wq', 'bq', 'Wk', 'bk', 'Wv', 'bv', 'Wo', 'bo', 'ln_gamma', 'ln_beta')}
    del _L0_xattn_all

    def _L0_ffn_setup():
        import jax, jax.numpy as jnp
        import numpy as np
        D_MODEL = 128
        D_FF = 512
        N_EXPERTS = 8
        TOP_K = 2
        B, T = (4, 256)
        key = jax.random.key(seed)
        ks = jax.random.split(key, 5)
        x = jax.random.normal(ks[0], (B, T, D_MODEL), dtype=jnp.float32)

        def lin(k, shape, fan_in):
            return jax.random.normal(k, shape, dtype=jnp.float32) / np.float32(np.sqrt(fan_in))
        return {'x': x, 'router_w': lin(ks[1], (N_EXPERTS, D_MODEL), D_MODEL), 'w_gate': lin(ks[2], (N_EXPERTS, D_MODEL, D_FF), D_MODEL), 'w_up': lin(ks[3], (N_EXPERTS, D_MODEL, D_FF), D_MODEL), 'w_down': lin(ks[4], (N_EXPERTS, D_FF, D_MODEL), D_FF)}
    _L0_ffn_all = _L0_ffn_setup()
    _L0_ffn_in = {k: v for k, v in _L0_ffn_all.items() if k in ('router_w', 'w_gate', 'w_up', 'w_down')}
    del _L0_ffn_all

    def _L1_attn_setup():
        import jax, jax.numpy as jnp
        import numpy as np
        B, S, D, H = (4, 128, 128, 16)
        d = D // H
        EPS = 1e-05

        def _ln(z, g, b):
            mu = jnp.mean(z, axis=-1, keepdims=True)
            var = jnp.mean((z - mu) ** 2, axis=-1, keepdims=True)
            return (z - mu) * jax.lax.rsqrt(var + EPS) * g + b
        key = jax.random.key(seed)
        ks = jax.random.split(key, 6)
        x = jax.random.normal(ks[0], (B, S, D), dtype=jnp.float32)
        Wproj = jax.random.normal(ks[1], (D, 3 * D), dtype=jnp.float32) / np.sqrt(D)
        bproj = jax.random.normal(ks[2], (3 * D,), dtype=jnp.float32) * 0.02
        W0 = jax.random.normal(ks[3], (d, d), dtype=jnp.float32) / np.sqrt(d)
        ln_g = jnp.ones((d,), dtype=jnp.float32)
        ln_b = jnp.zeros((d,), dtype=jnp.float32)
        gn_g = jnp.ones((D,), dtype=jnp.float32)
        gn_b = jnp.zeros((D,), dtype=jnp.float32)
        Wout = jax.random.normal(ks[4], (D, D), dtype=jnp.float32) / np.sqrt(D)
        bout = jax.random.normal(ks[5], (D,), dtype=jnp.float32) * 0.02
        return {'x': x, 'Wproj': Wproj, 'bproj': bproj, 'W0': W0, 'ln_g': ln_g, 'ln_b': ln_b, 'gn_g': gn_g, 'gn_b': gn_b, 'Wout': Wout, 'bout': bout}
    _L1_attn_all = _L1_attn_setup()
    _L1_attn_in = {k: v for k, v in _L1_attn_all.items() if k in ('Wproj', 'bproj', 'W0', 'ln_g', 'ln_b', 'gn_g', 'gn_b', 'Wout', 'bout')}
    del _L1_attn_all

    def _L1_xattn_setup():
        import jax, jax.numpy as jnp
        import numpy as np
        DIM_IN, DIM_LAT, DIM_HEAD = (96, 128, 64)
        INNER = max(DIM_LAT, DIM_IN)
        HEADS = INNER // DIM_HEAD
        SCALE = DIM_HEAD ** (-0.5)
        RMS_EPS = 1e-08
        LN_EPS = 1e-05

        def layernorm(x, g, b):
            mu = jnp.mean(x, axis=-1, keepdims=True)
            var = jnp.mean((x - mu) ** 2, axis=-1, keepdims=True)
            return (x - mu) * jax.lax.rsqrt(var + LN_EPS) * g + b

        def rmsnorm(x, gamma):
            norm = jnp.sqrt(jnp.sum(x * x, axis=-1, keepdims=True)) * x.shape[-1] ** (-0.5)
            return x / jnp.maximum(norm, RMS_EPS) * gamma
        key = jax.random.key(seed)
        ks = jax.random.split(key, 12)
        b, n, m = (4, 512, 64)
        x = jax.random.normal(ks[0], (b, n, DIM_IN), jnp.float32)
        latents = jax.random.normal(ks[1], (b, m, DIM_LAT), jnp.float32)
        mask = jax.random.randint(ks[2], (b, n), 0, 2).astype(bool)
        s = lambda k, sh, fan: jax.random.normal(k, sh, jnp.float32) * fan ** (-0.5)
        return {'x': x, 'latents': latents, 'mask': mask, 'ln_x_g': jnp.ones((DIM_IN,), jnp.float32), 'ln_x_b': jnp.zeros((DIM_IN,), jnp.float32), 'ln_l_g': jnp.ones((DIM_LAT,), jnp.float32), 'ln_l_b': jnp.zeros((DIM_LAT,), jnp.float32), 'qn_g': jnp.ones((DIM_HEAD,), jnp.float32), 'kn_g': jnp.ones((DIM_HEAD,), jnp.float32), 'Wq': s(ks[3], (INNER, DIM_LAT), DIM_LAT), 'Wkv': s(ks[4], (2 * INNER, DIM_IN), DIM_IN), 'Wlkv': s(ks[5], (2 * INNER, DIM_LAT), DIM_LAT), 'Wo': s(ks[6], (DIM_LAT, INNER), INNER), 'bo': jnp.zeros((DIM_LAT,), jnp.float32)}
    _L1_xattn_all = _L1_xattn_setup()
    _L1_xattn_in = {k: v for k, v in _L1_xattn_all.items() if k in ('ln_x_g', 'ln_x_b', 'ln_l_g', 'ln_l_b', 'qn_g', 'kn_g', 'Wq', 'Wkv', 'Wlkv', 'Wo', 'bo')}
    del _L1_xattn_all

    def _L1_ffn_setup():
        import jax, jax.numpy as jnp
        import numpy as np
        E = 64
        K = 6
        CAP = 64
        ROUTE_SCALE = 1.0
        key = jax.random.key(seed)
        ks = jax.random.split(key, 9)
        B, S, D, I = (2, 128, 128, 88)
        SI = 2 * I
        s = 0.02
        return {'x': jax.random.normal(ks[0], (B, S, D), jnp.float32), 'gate_w': jax.random.normal(ks[1], (E, D), jnp.float32) * s, 'gate_b': jnp.zeros((E,), jnp.float32), 'w1': jax.random.normal(ks[2], (E, I, D), jnp.float32) * s, 'w2': jax.random.normal(ks[3], (E, D, I), jnp.float32) * s, 'w3': jax.random.normal(ks[4], (E, I, D), jnp.float32) * s, 'ws1': jax.random.normal(ks[5], (SI, D), jnp.float32) * s, 'ws2': jax.random.normal(ks[6], (D, SI), jnp.float32) * s, 'ws3': jax.random.normal(ks[7], (SI, D), jnp.float32) * s}
    _L1_ffn_all = _L1_ffn_setup()
    _L1_ffn_in = {k: v for k, v in _L1_ffn_all.items() if k in ('gate_w', 'gate_b', 'w1', 'w2', 'w3', 'ws1', 'ws2', 'ws3')}
    del _L1_ffn_all

    def _L2_attn_setup():
        import jax, jax.numpy as jnp
        import numpy as np
        DIM = 128
        B, N = (8, 512)
        EPS = 1e-06
        key = jax.random.key(seed)
        k1, k2, k3, k4 = jax.random.split(key, 4)
        x = jax.random.normal(k1, (B, N, DIM), dtype=jnp.float32)
        s = 1.0 / np.sqrt(DIM)
        W_qkv = jax.random.uniform(k2, (3 * DIM, DIM), jnp.float32, -s, s)
        W_out = jax.random.uniform(k3, (DIM, DIM), jnp.float32, -s, s)
        b_out = jax.random.uniform(k4, (DIM,), jnp.float32, -s, s)
        return {'x': x, 'W_qkv': W_qkv, 'W_out': W_out, 'b_out': b_out}
    _L2_attn_all = _L2_attn_setup()
    _L2_attn_in = {k: v for k, v in _L2_attn_all.items() if k in ('W_qkv', 'W_out', 'b_out')}
    del _L2_attn_all

    def _L2_xattn_setup():
        import jax, jax.numpy as jnp
        import numpy as np
        B, T, DT, G, DV = (16, 64, 128, 72, 96)
        H, DH = (4, 32)
        INNER = H * DH
        HID = 4 * DT
        N_STATE = 64
        K_TOP = 32

        def layernorm(x, g, b, eps=1e-05):
            m = x.mean(-1, keepdims=True)
            v = x.var(-1, keepdims=True)
            return (x - m) * jax.lax.rsqrt(v + eps) * g + b

        def s4d(x, log_dt, A_re, A_im, C_re, C_im, D_skip):
            Bb, L, D = x.shape
            dt = jnp.exp(log_dt)
            A = A_re + 1j * A_im
            C = C_re + 1j * C_im
            dtA = dt[:, None] * A
            dC = C * (jnp.exp(dtA) - 1.0) / A
            powers = jnp.exp(dtA[:, :, None] * jnp.arange(L))
            K = 2.0 * jnp.einsum('dn,dnl->dl', dC, powers).real
            n = 2 * L
            Kf = jnp.fft.rfft(K, n=n, axis=-1)
            xf = jnp.fft.rfft(x, n=n, axis=1)
            y = jnp.fft.irfft(xf * Kf.T[None], n=n, axis=1)[:, :L]
            return y + x * D_skip
        key = jax.random.key(seed)
        ks = jax.random.split(key, 16)
        s = 0.02
        inp = {'x_text': jax.random.normal(ks[0], (B, T, DT), jnp.float32), 'x_vision': jax.random.normal(ks[1], (B, G, DV), jnp.float32), 'text_mask': jnp.ones((B, T), bool), 'vision_mask': jnp.ones((B, G), bool), 'Wq': jax.random.normal(ks[2], (DT, INNER), jnp.float32) * s, 'Wk': jax.random.normal(ks[3], (DV, INNER), jnp.float32) * s, 'Wv': jax.random.normal(ks[4], (DV, DT), jnp.float32) * s, 'W_film_in': jax.random.normal(ks[5], (DT, 2 * DT), jnp.float32) * s, 'b_film_in': jnp.zeros((2 * DT,), jnp.float32), 'W_film_out': jax.random.normal(ks[6], (DT, 2 * DT), jnp.float32) * s, 'b_film_out': jnp.zeros((2 * DT,), jnp.float32), 'g_norm_in': jnp.ones((DT,), jnp.float32), 'b_norm_in': jnp.zeros((DT,), jnp.float32), 'g_norm_out': jnp.ones((DT,), jnp.float32), 'b_norm_out': jnp.zeros((DT,), jnp.float32), 'g_ffn': jnp.ones((DT,), jnp.float32), 'b_ffn': jnp.zeros((DT,), jnp.float32), 'W1': jax.random.normal(ks[7], (DT, HID), jnp.float32) * s, 'b1': jnp.zeros((HID,), jnp.float32), 'W2': jax.random.normal(ks[8], (HID, DT), jnp.float32) * s, 'b2': jnp.zeros((DT,), jnp.float32), 'log_dt': jnp.log(0.001) + jax.random.uniform(ks[9], (DT,), jnp.float32) * (jnp.log(0.1) - jnp.log(0.001)), 'A_re': -0.5 * jnp.ones((DT, N_STATE), jnp.float32), 'A_im': jnp.tile(jnp.pi * jnp.arange(N_STATE, dtype=jnp.float32), (DT, 1)), 'C_re': jax.random.normal(ks[10], (DT, N_STATE), jnp.float32) * 0.5 ** 0.5, 'C_im': jax.random.normal(ks[11], (DT, N_STATE), jnp.float32) * 0.5 ** 0.5, 'D_skip': jax.random.normal(ks[12], (DT,), jnp.float32), 'mod_gate': jnp.array(0.5, jnp.float32)}
        return inp
    _L2_xattn_all = _L2_xattn_setup()
    _L2_xattn_in = {k: v for k, v in _L2_xattn_all.items() if k in ('Wq', 'Wk', 'Wv', 'W_film_in', 'b_film_in', 'W_film_out', 'b_film_out', 'g_norm_in', 'b_norm_in', 'g_norm_out', 'b_norm_out', 'g_ffn', 'b_ffn', 'W1', 'b1', 'W2', 'b2', 'log_dt', 'A_re', 'A_im', 'C_re', 'C_im', 'D_skip', 'mod_gate')}
    del _L2_xattn_all

    def _L2_ffn_setup():
        import jax, jax.numpy as jnp
        import numpy as np
        B, S, H, E, I, MAX_K, A_HID = (2, 256, 128, 8, 336, 6, 50)
        key = jax.random.key(seed)
        ks = jax.random.split(key, 10)
        sc = 0.02
        return {'hidden_states': jax.random.normal(ks[0], (B, S, H), dtype=jnp.float32), 'router_w': jax.random.normal(ks[1], (E, H), dtype=jnp.float32) * sc, 'actor_w1': jax.random.normal(ks[2], (A_HID, H), dtype=jnp.float32) * sc, 'actor_b1': jnp.zeros((A_HID,), dtype=jnp.float32), 'actor_w2': jax.random.normal(ks[3], (MAX_K, A_HID), dtype=jnp.float32) * sc, 'actor_b2': jnp.zeros((MAX_K,), dtype=jnp.float32), 'gate_w': jax.random.normal(ks[4], (E, I, H), dtype=jnp.float32) * sc, 'up_w': jax.random.normal(ks[5], (E, I, H), dtype=jnp.float32) * sc, 'down_w': jax.random.normal(ks[6], (E, H, I), dtype=jnp.float32) * sc}
    _L2_ffn_all = _L2_ffn_setup()
    _L2_ffn_in = {k: v for k, v in _L2_ffn_all.items() if k in ('router_w', 'actor_w1', 'actor_b1', 'actor_w2', 'actor_b2', 'gate_w', 'up_w', 'down_w')}
    del _L2_ffn_all

    def _L3_attn_setup():
        import jax, jax.numpy as jnp
        import numpy as np
        HEADS = 16
        DIM_HEAD = 64
        RMS_EPS = 1e-12
        key = jax.random.key(seed)
        k1, k2, k3 = jax.random.split(key, 3)
        b, n, dim = (2, 256, 128)
        dim_inner = HEADS * DIM_HEAD
        x = jax.random.normal(k1, (b, n, dim), dtype=jnp.float32)
        gamma = jnp.ones((dim,), dtype=jnp.float32)
        w_qkv = jax.random.normal(k2, (dim, 3 * dim_inner), dtype=jnp.float32) * dim ** (-0.5)
        w_out = jax.random.normal(k3, (dim_inner, dim), dtype=jnp.float32) * dim_inner ** (-0.5)
        return {'x': x, 'gamma': gamma, 'w_qkv': w_qkv, 'w_out': w_out}
    _L3_attn_all = _L3_attn_setup()
    _L3_attn_in = {k: v for k, v in _L3_attn_all.items() if k in ('gamma', 'w_qkv', 'w_out')}
    del _L3_attn_all

    def _L3_xattn_setup():
        import jax, jax.numpy as jnp
        import numpy as np
        NUM_HEADS = 16
        key = jax.random.key(seed)
        ks = jax.random.split(key, 8)
        dim, cond_dim = (128, 96)
        B, N, condN = (4, 256, 128)
        s = lambda k, shp, fan: jax.random.normal(k, shp, dtype=jnp.float32) * fan ** (-0.5)
        return {'x': jax.random.normal(ks[0], (B, N, dim), dtype=jnp.float32), 'cond': jax.random.normal(ks[1], (B, condN, cond_dim), dtype=jnp.float32), 'q_w': s(ks[2], (dim, dim), dim), 'q_b': jnp.zeros((dim,), jnp.float32), 'kv_w': s(ks[3], (cond_dim, 2 * dim), cond_dim), 'kv_b': jnp.zeros((2 * dim,), jnp.float32), 'proj_w': s(ks[4], (dim, dim), dim), 'proj_b': jnp.zeros((dim,), jnp.float32)}
    _L3_xattn_all = _L3_xattn_setup()
    _L3_xattn_in = {k: v for k, v in _L3_xattn_all.items() if k in ('q_w', 'q_b', 'kv_w', 'kv_b', 'proj_w', 'proj_b')}
    del _L3_xattn_all

    def _L3_ffn_setup():
        import jax, jax.numpy as jnp
        import numpy as np
        B, T, H = (2, 256, 128)
        I = 512
        HEADS = 4
        RET = 128
        NUM_EXPERTS = 512
        NUM_KEYS = 64
        K = 8
        key = jax.random.key(seed)
        ks = jax.random.split(key, 7)
        return {'hidden_states': jax.random.normal(ks[0], (B, T, H), jnp.float32), 'W_up': jax.random.normal(ks[1], (I, H), jnp.float32) * 0.02, 'W_down': jax.random.normal(ks[2], (H, I), jnp.float32) * 0.02, 'W_q': jax.random.normal(ks[3], (HEADS * RET, H), jnp.float32) * 0.02, 'keys': jax.random.normal(ks[4], (HEADS, NUM_KEYS, 2, RET // 2), jnp.float32) * 0.02, 'down_embed': jax.random.normal(ks[5], (NUM_EXPERTS, H), jnp.float32) * 0.02, 'up_embed': jax.random.normal(ks[6], (NUM_EXPERTS, H), jnp.float32) * 0.02}
    _L3_ffn_all = _L3_ffn_setup()
    _L3_ffn_in = {k: v for k, v in _L3_ffn_all.items() if k in ('W_up', 'W_down', 'W_q', 'keys', 'down_embed', 'up_embed')}
    del _L3_ffn_all
    return {'x': x, 'ctx_768': ctx_768, 'mask_BxS2_bk0': mask_BxS2_bk0, 'mask_BxS_bf1': mask_BxS_bf1, 'mask_BxS2_bf1': mask_BxS2_bf1, 'L0_attn_in_proj': _L0_attn_in['in_proj'], 'L0_attn_out_proj': _L0_attn_in['out_proj'], 'L0_attn_frequencies': _L0_attn_in['frequencies'], 'L0_attn_decays': _L0_attn_in['decays'], 'L0_attn_ss_W': _L0_attn_in['ss_W'], 'L0_attn_ss_b': _L0_attn_in['ss_b'], 'L0_attn_gate_W': _L0_attn_in['gate_W'], 'L0_attn_gate_b': _L0_attn_in['gate_b'], 'L0_attn_fin_W': _L0_attn_in['fin_W'], 'L0_attn_fin_b': _L0_attn_in['fin_b'], 'L0_xattn_Wq': _L0_xattn_in['Wq'], 'L0_xattn_bq': _L0_xattn_in['bq'], 'L0_xattn_Wk': _L0_xattn_in['Wk'], 'L0_xattn_bk': _L0_xattn_in['bk'], 'L0_xattn_Wv': _L0_xattn_in['Wv'], 'L0_xattn_bv': _L0_xattn_in['bv'], 'L0_xattn_Wo': _L0_xattn_in['Wo'], 'L0_xattn_bo': _L0_xattn_in['bo'], 'L0_xattn_ln_gamma': _L0_xattn_in['ln_gamma'], 'L0_xattn_ln_beta': _L0_xattn_in['ln_beta'], 'L0_ffn_router_w': _L0_ffn_in['router_w'], 'L0_ffn_w_gate': _L0_ffn_in['w_gate'], 'L0_ffn_w_up': _L0_ffn_in['w_up'], 'L0_ffn_w_down': _L0_ffn_in['w_down'], 'L1_attn_Wproj': _L1_attn_in['Wproj'], 'L1_attn_bproj': _L1_attn_in['bproj'], 'L1_attn_W0': _L1_attn_in['W0'], 'L1_attn_ln_g': _L1_attn_in['ln_g'], 'L1_attn_ln_b': _L1_attn_in['ln_b'], 'L1_attn_gn_g': _L1_attn_in['gn_g'], 'L1_attn_gn_b': _L1_attn_in['gn_b'], 'L1_attn_Wout': _L1_attn_in['Wout'], 'L1_attn_bout': _L1_attn_in['bout'], 'L1_xattn_ln_x_g': _L1_xattn_in['ln_x_g'], 'L1_xattn_ln_x_b': _L1_xattn_in['ln_x_b'], 'L1_xattn_ln_l_g': _L1_xattn_in['ln_l_g'], 'L1_xattn_ln_l_b': _L1_xattn_in['ln_l_b'], 'L1_xattn_qn_g': _L1_xattn_in['qn_g'], 'L1_xattn_kn_g': _L1_xattn_in['kn_g'], 'L1_xattn_Wq': _L1_xattn_in['Wq'], 'L1_xattn_Wkv': _L1_xattn_in['Wkv'], 'L1_xattn_Wlkv': _L1_xattn_in['Wlkv'], 'L1_xattn_Wo': _L1_xattn_in['Wo'], 'L1_xattn_bo': _L1_xattn_in['bo'], 'L1_ffn_gate_w': _L1_ffn_in['gate_w'], 'L1_ffn_gate_b': _L1_ffn_in['gate_b'], 'L1_ffn_w1': _L1_ffn_in['w1'], 'L1_ffn_w2': _L1_ffn_in['w2'], 'L1_ffn_w3': _L1_ffn_in['w3'], 'L1_ffn_ws1': _L1_ffn_in['ws1'], 'L1_ffn_ws2': _L1_ffn_in['ws2'], 'L1_ffn_ws3': _L1_ffn_in['ws3'], 'L2_attn_W_qkv': _L2_attn_in['W_qkv'], 'L2_attn_W_out': _L2_attn_in['W_out'], 'L2_attn_b_out': _L2_attn_in['b_out'], 'L2_xattn_Wq': _L2_xattn_in['Wq'], 'L2_xattn_Wk': _L2_xattn_in['Wk'], 'L2_xattn_Wv': _L2_xattn_in['Wv'], 'L2_xattn_W_film_in': _L2_xattn_in['W_film_in'], 'L2_xattn_b_film_in': _L2_xattn_in['b_film_in'], 'L2_xattn_W_film_out': _L2_xattn_in['W_film_out'], 'L2_xattn_b_film_out': _L2_xattn_in['b_film_out'], 'L2_xattn_g_norm_in': _L2_xattn_in['g_norm_in'], 'L2_xattn_b_norm_in': _L2_xattn_in['b_norm_in'], 'L2_xattn_g_norm_out': _L2_xattn_in['g_norm_out'], 'L2_xattn_b_norm_out': _L2_xattn_in['b_norm_out'], 'L2_xattn_g_ffn': _L2_xattn_in['g_ffn'], 'L2_xattn_b_ffn': _L2_xattn_in['b_ffn'], 'L2_xattn_W1': _L2_xattn_in['W1'], 'L2_xattn_b1': _L2_xattn_in['b1'], 'L2_xattn_W2': _L2_xattn_in['W2'], 'L2_xattn_b2': _L2_xattn_in['b2'], 'L2_xattn_log_dt': _L2_xattn_in['log_dt'], 'L2_xattn_A_re': _L2_xattn_in['A_re'], 'L2_xattn_A_im': _L2_xattn_in['A_im'], 'L2_xattn_C_re': _L2_xattn_in['C_re'], 'L2_xattn_C_im': _L2_xattn_in['C_im'], 'L2_xattn_D_skip': _L2_xattn_in['D_skip'], 'L2_xattn_mod_gate': _L2_xattn_in['mod_gate'], 'L2_ffn_router_w': _L2_ffn_in['router_w'], 'L2_ffn_actor_w1': _L2_ffn_in['actor_w1'], 'L2_ffn_actor_b1': _L2_ffn_in['actor_b1'], 'L2_ffn_actor_w2': _L2_ffn_in['actor_w2'], 'L2_ffn_actor_b2': _L2_ffn_in['actor_b2'], 'L2_ffn_gate_w': _L2_ffn_in['gate_w'], 'L2_ffn_up_w': _L2_ffn_in['up_w'], 'L2_ffn_down_w': _L2_ffn_in['down_w'], 'L3_attn_gamma': _L3_attn_in['gamma'], 'L3_attn_w_qkv': _L3_attn_in['w_qkv'], 'L3_attn_w_out': _L3_attn_in['w_out'], 'L3_xattn_q_w': _L3_xattn_in['q_w'], 'L3_xattn_q_b': _L3_xattn_in['q_b'], 'L3_xattn_kv_w': _L3_xattn_in['kv_w'], 'L3_xattn_kv_b': _L3_xattn_in['kv_b'], 'L3_xattn_proj_w': _L3_xattn_in['proj_w'], 'L3_xattn_proj_b': _L3_xattn_in['proj_b'], 'L3_ffn_W_up': _L3_ffn_in['W_up'], 'L3_ffn_W_down': _L3_ffn_in['W_down'], 'L3_ffn_W_q': _L3_ffn_in['W_q'], 'L3_ffn_keys': _L3_ffn_in['keys'], 'L3_ffn_down_embed': _L3_ffn_in['down_embed'], 'L3_ffn_up_embed': _L3_ffn_in['up_embed']}

def reference(x, ctx_768, mask_BxS2_bk0, mask_BxS_bf1, mask_BxS2_bf1, L0_attn_in_proj, L0_attn_out_proj, L0_attn_frequencies, L0_attn_decays, L0_attn_ss_W, L0_attn_ss_b, L0_attn_gate_W, L0_attn_gate_b, L0_attn_fin_W, L0_attn_fin_b, L0_xattn_Wq, L0_xattn_bq, L0_xattn_Wk, L0_xattn_bk, L0_xattn_Wv, L0_xattn_bv, L0_xattn_Wo, L0_xattn_bo, L0_xattn_ln_gamma, L0_xattn_ln_beta, L0_ffn_router_w, L0_ffn_w_gate, L0_ffn_w_up, L0_ffn_w_down, L1_attn_Wproj, L1_attn_bproj, L1_attn_W0, L1_attn_ln_g, L1_attn_ln_b, L1_attn_gn_g, L1_attn_gn_b, L1_attn_Wout, L1_attn_bout, L1_xattn_ln_x_g, L1_xattn_ln_x_b, L1_xattn_ln_l_g, L1_xattn_ln_l_b, L1_xattn_qn_g, L1_xattn_kn_g, L1_xattn_Wq, L1_xattn_Wkv, L1_xattn_Wlkv, L1_xattn_Wo, L1_xattn_bo, L1_ffn_gate_w, L1_ffn_gate_b, L1_ffn_w1, L1_ffn_w2, L1_ffn_w3, L1_ffn_ws1, L1_ffn_ws2, L1_ffn_ws3, L2_attn_W_qkv, L2_attn_W_out, L2_attn_b_out, L2_xattn_Wq, L2_xattn_Wk, L2_xattn_Wv, L2_xattn_W_film_in, L2_xattn_b_film_in, L2_xattn_W_film_out, L2_xattn_b_film_out, L2_xattn_g_norm_in, L2_xattn_b_norm_in, L2_xattn_g_norm_out, L2_xattn_b_norm_out, L2_xattn_g_ffn, L2_xattn_b_ffn, L2_xattn_W1, L2_xattn_b1, L2_xattn_W2, L2_xattn_b2, L2_xattn_log_dt, L2_xattn_A_re, L2_xattn_A_im, L2_xattn_C_re, L2_xattn_C_im, L2_xattn_D_skip, L2_xattn_mod_gate, L2_ffn_router_w, L2_ffn_actor_w1, L2_ffn_actor_b1, L2_ffn_actor_w2, L2_ffn_actor_b2, L2_ffn_gate_w, L2_ffn_up_w, L2_ffn_down_w, L3_attn_gamma, L3_attn_w_qkv, L3_attn_w_out, L3_xattn_q_w, L3_xattn_q_b, L3_xattn_kv_w, L3_xattn_kv_b, L3_xattn_proj_w, L3_xattn_proj_b, L3_ffn_W_up, L3_ffn_W_down, L3_ffn_W_q, L3_ffn_keys, L3_ffn_down_embed, L3_ffn_up_embed):
    import jax
    import jax.numpy as jnp

    def _L0_attn_ref(x, in_proj, out_proj, frequencies, decays, ss_W, ss_b, gate_W, gate_b, fin_W, fin_b):
        import jax, jax.numpy as jnp
        import numpy as np
        SCALING = 1.0
        B, L, H = x.shape
        fft_len = 2 * L - 1
        freqs = frequencies * (2.0 * jnp.pi * SCALING)
        dec = -jnp.exp(decays) * SCALING
        lam = dec + 1j * freqs
        kernel = jnp.exp(lam[None, :] * jnp.arange(L, dtype=jnp.float32)[:, None])
        k = jnp.einsum('hn,kn,nh->hk', in_proj.astype(kernel.dtype), kernel, out_proj.astype(kernel.dtype)).real
        u = jnp.transpose(x, (0, 2, 1))
        u_f = jnp.fft.fft(u, n=fft_len, axis=-1)
        k_f = jnp.fft.fft(k, n=fft_len, axis=-1)
        conv = jnp.fft.ifft(u_f * k_f[None], axis=-1)[:, :, :L].real
        ss_out = jnp.transpose(conv, (0, 2, 1))
        ss_out = jax.nn.gelu(ss_out @ ss_W.T + ss_b, approximate=False)
        gate = jax.nn.gelu(x @ gate_W.T + gate_b, approximate=False)
        return gate * ss_out @ fin_W.T + fin_b

    def _L0_xattn_ref(query, key, value, Wq, bq, Wk, bk, Wv, bv, Wo, bo, ln_gamma, ln_beta):
        import jax, jax.numpy as jnp
        import numpy as np
        QUERY_DIM, KV_DIM, EMBED_DIM, NUM_HEADS = (128, 96, 128, 16)
        HEAD_DIM = EMBED_DIM // NUM_HEADS
        SCALE = HEAD_DIM ** (-0.5)
        LN_EPS = 1e-05

        def _l2norm(x, eps=1e-12):
            n = jnp.sqrt(jnp.sum(x * x, axis=-1, keepdims=True))
            return x / jnp.maximum(n, eps)
        B, Nq, _ = query.shape
        Nk = key.shape[1]
        Qp = query @ Wq + bq
        K = _l2norm(key @ Wk + bk)
        V = value @ Wv + bv
        Q = _l2norm(Qp)
        Q = Q.reshape(B, Nq, NUM_HEADS, HEAD_DIM).transpose(0, 2, 1, 3)
        K = K.reshape(B, Nk, NUM_HEADS, HEAD_DIM).transpose(0, 2, 1, 3)
        V = V.reshape(B, Nk, NUM_HEADS, HEAD_DIM).transpose(0, 2, 1, 3)
        scores = jnp.einsum('bhqd,bhkd->bhqk', Q, K) * SCALE
        attn = jax.nn.softmax(scores, axis=-1)
        out = jnp.einsum('bhqk,bhkd->bhqd', attn, V)
        out = out.transpose(0, 2, 1, 3).reshape(B, Nq, EMBED_DIM)
        out = out @ Wo + bo
        x = out + Qp
        mu = jnp.mean(x, axis=-1, keepdims=True)
        var = jnp.mean((x - mu) ** 2, axis=-1, keepdims=True)
        return (x - mu) / jnp.sqrt(var + LN_EPS) * ln_gamma + ln_beta

    def _L0_ffn_ref(x, router_w, w_gate, w_up, w_down):
        import jax, jax.numpy as jnp
        import numpy as np
        D_MODEL = 128
        D_FF = 512
        N_EXPERTS = 8
        TOP_K = 2
        B, T = (4, 256)
        Bx, Tx, D = x.shape
        xf = x.reshape(-1, D)
        logits = xf @ router_w.T
        scores = jax.nn.softmax(logits, axis=-1)
        topk_scores, topk_ids = jax.lax.top_k(scores, TOP_K)
        topk_scores = topk_scores / topk_scores.sum(-1, keepdims=True)
        cw = (jax.nn.one_hot(topk_ids, N_EXPERTS, dtype=xf.dtype) * topk_scores[..., None]).sum(1)

        def body(acc, inputs):
            wg, wu, wd, w = inputs
            h = jax.nn.silu(xf @ wg) * (xf @ wu)
            acc = acc + w[:, None] * (h @ wd)
            return (acc, None)
        out, _ = jax.lax.scan(body, jnp.zeros_like(xf), (w_gate, w_up, w_down, cw.T))
        return out.reshape(Bx, Tx, D)

    def _L1_attn_ref(x, Wproj, bproj, W0, ln_g, ln_b, gn_g, gn_b, Wout, bout):
        import jax, jax.numpy as jnp
        import numpy as np
        B, S, D, H = (4, 128, 128, 16)
        d = D // H
        EPS = 1e-05

        def _ln(z, g, b):
            mu = jnp.mean(z, axis=-1, keepdims=True)
            var = jnp.mean((z - mu) ** 2, axis=-1, keepdims=True)
            return (z - mu) * jax.lax.rsqrt(var + EPS) * g + b
        b_, s_, dm = x.shape
        h_, hd = (H, d)
        qkv = (x @ Wproj + bproj).reshape(b_, s_, 3, h_, hd).transpose(0, 3, 2, 1, 4)
        q, k, v = (qkv[:, :, 0], qkv[:, :, 1], qkv[:, :, 2])
        ln_f = lambda z: _ln(z, ln_g, ln_b)
        mask = jnp.tril(jnp.ones((s_, s_), dtype=x.dtype))
        Z = jnp.einsum('bhsd,de->bhse', k, W0)
        y1, vjp1 = jax.vjp(ln_f, Z)
        dz1 = vjp1(y1 - v)[0]
        KK = mask * jnp.einsum('bhtd,bhsd->bhts', k, k)
        Z2 = Z - jnp.einsum('bhts,bhsd->bhtd', KK, dz1)
        y2, vjp2 = jax.vjp(ln_f, Z2)
        dz2 = vjp2(y2 - v)[0]
        A = mask * jnp.einsum('bhtd,bhsd->bhts', q, k)
        ctx = jnp.einsum('bhsd,de->bhse', q, W0) - jnp.einsum('bhts,bhsd->bhtd', A, dz1 + dz2)
        ctx = ctx.transpose(0, 2, 1, 3)
        mu = jnp.mean(ctx, axis=(1, 3), keepdims=True)
        var = jnp.mean((ctx - mu) ** 2, axis=(1, 3), keepdims=True)
        ctx = (ctx - mu) * jax.lax.rsqrt(var + EPS)
        ctx = ctx * gn_g.reshape(1, 1, h_, hd) + gn_b.reshape(1, 1, h_, hd)
        ctx = ctx.reshape(b_, s_, dm)
        return ctx @ Wout + bout

    def _L1_xattn_ref(x, latents, mask, ln_x_g, ln_x_b, ln_l_g, ln_l_b, qn_g, kn_g, Wq, Wkv, Wlkv, Wo, bo):
        import jax, jax.numpy as jnp
        import numpy as np
        DIM_IN, DIM_LAT, DIM_HEAD = (96, 128, 64)
        INNER = max(DIM_LAT, DIM_IN)
        HEADS = INNER // DIM_HEAD
        SCALE = DIM_HEAD ** (-0.5)
        RMS_EPS = 1e-08
        LN_EPS = 1e-05

        def layernorm(x, g, b):
            mu = jnp.mean(x, axis=-1, keepdims=True)
            var = jnp.mean((x - mu) ** 2, axis=-1, keepdims=True)
            return (x - mu) * jax.lax.rsqrt(var + LN_EPS) * g + b

        def rmsnorm(x, gamma):
            norm = jnp.sqrt(jnp.sum(x * x, axis=-1, keepdims=True)) * x.shape[-1] ** (-0.5)
            return x / jnp.maximum(norm, RMS_EPS) * gamma
        b, n, _ = x.shape
        m = latents.shape[1]
        xn = layernorm(x, ln_x_g, ln_x_b)
        ln = layernorm(latents, ln_l_g, ln_l_b)
        q = ln @ Wq.T
        kv = jnp.concatenate([xn @ Wkv.T, ln @ Wlkv.T], axis=1)
        k, v = (kv[..., :INNER], kv[..., INNER:])
        split_heads = lambda t: t.reshape(t.shape[0], t.shape[1], HEADS, DIM_HEAD).transpose(0, 2, 1, 3)
        q, k, v = (split_heads(q), split_heads(k), split_heads(v))
        qn = rmsnorm(q, qn_g) * SCALE
        kn = rmsnorm(k, kn_g)
        attn = jnp.einsum('bhid,bhjd->bhij', qn, kn)
        full_mask = jnp.pad(mask, ((0, 0), (0, m)), constant_values=True)
        attn = jnp.where(full_mask[:, None, None, :], attn, -jnp.finfo(attn.dtype).max)
        attn = jax.nn.softmax(attn, axis=-1)
        out = jnp.einsum('bhij,bhjd->bhid', attn, v)
        out = out.transpose(0, 2, 1, 3).reshape(b, m, INNER)
        return out @ Wo.T + bo

    def _L1_ffn_ref(x, gate_w, gate_b, w1, w2, w3, ws1, ws2, ws3):
        import jax, jax.numpy as jnp
        import numpy as np
        E = 64
        K = 6
        CAP = 64
        ROUTE_SCALE = 1.0
        shape = x.shape
        D = shape[-1]
        xf = x.reshape(-1, D)
        T = xf.shape[0]
        scores = jax.nn.softmax(xf @ gate_w.T, axis=-1)
        _, idx = jax.lax.top_k(scores + gate_b, K)
        weights = jnp.take_along_axis(scores, idx, axis=1) * ROUTE_SCALE
        flat_e = idx.reshape(-1)
        order = jnp.argsort(flat_e)
        se = flat_e[order]
        counts = jnp.bincount(flat_e, length=E)
        starts = jnp.cumsum(counts) - counts
        pos = jnp.arange(T * K) - starts[se]
        tok = order // K
        xb = jnp.zeros((E, CAP, D), xf.dtype).at[se, pos].set(xf[tok], mode='drop')
        h = jax.nn.silu(jnp.einsum('ecd,eid->eci', xb, w1)) * jnp.einsum('ecd,eid->eci', xb, w3)
        yb = jnp.einsum('eci,edi->ecd', h, w2)
        valid = (pos < CAP).astype(xf.dtype)
        contrib = yb[se, jnp.minimum(pos, CAP - 1)]
        wf = weights.reshape(-1)[order] * valid
        y = jnp.zeros_like(xf).at[tok].add(contrib * wf[:, None])
        z = jax.nn.silu(xf @ ws1.T) * (xf @ ws3.T) @ ws2.T
        return (y + z).reshape(shape)

    def _L2_attn_ref(x, W_qkv, W_out, b_out):
        import jax, jax.numpy as jnp
        import numpy as np
        DIM = 128
        B, N = (8, 512)
        EPS = 1e-06
        qkv = jnp.einsum('bnd,ed->bne', x, W_qkv)
        q, k, v = jnp.split(qkv, 3, axis=-1)
        q = jax.nn.relu(q) + EPS
        k = jax.nn.relu(k) + EPS
        kv = jnp.einsum('bnd,bne->bde', k, v)
        z = 1.0 / (jnp.einsum('bnd,bd->bn', q, k.sum(axis=1)) + EPS)
        attn = jnp.einsum('bnd,bde,bn->bne', q, kv, z)
        return jnp.einsum('bne,fe->bnf', attn, W_out) + b_out

    def _L2_xattn_ref(x_text, x_vision, text_mask, vision_mask, Wq, Wk, Wv, W_film_in, b_film_in, W_film_out, b_film_out, g_norm_in, b_norm_in, g_norm_out, b_norm_out, g_ffn, b_ffn, W1, b1, W2, b2, log_dt, A_re, A_im, C_re, C_im, D_skip, mod_gate):
        import jax, jax.numpy as jnp
        import numpy as np
        B, T, DT, G, DV = (16, 64, 128, 72, 96)
        H, DH = (4, 32)
        INNER = H * DH
        HID = 4 * DT
        N_STATE = 64
        K_TOP = 32

        def layernorm(x, g, b, eps=1e-05):
            m = x.mean(-1, keepdims=True)
            v = x.var(-1, keepdims=True)
            return (x - m) * jax.lax.rsqrt(v + eps) * g + b

        def s4d(x, log_dt, A_re, A_im, C_re, C_im, D_skip):
            Bb, L, D = x.shape
            dt = jnp.exp(log_dt)
            A = A_re + 1j * A_im
            C = C_re + 1j * C_im
            dtA = dt[:, None] * A
            dC = C * (jnp.exp(dtA) - 1.0) / A
            powers = jnp.exp(dtA[:, :, None] * jnp.arange(L))
            K = 2.0 * jnp.einsum('dn,dnl->dl', dC, powers).real
            n = 2 * L
            Kf = jnp.fft.rfft(K, n=n, axis=-1)
            xf = jnp.fft.rfft(x, n=n, axis=1)
            y = jnp.fft.irfft(xf * Kf.T[None], n=n, axis=1)[:, :L]
            return y + x * D_skip
        Bb, Tt, D = x_text.shape
        Gg = x_vision.shape[1]
        Q = (x_text @ Wq).reshape(Bb, Tt, H, DH)
        K = (x_vision @ Wk).reshape(Bb, Gg, H, DH)
        scores = jnp.einsum('bthd,bghd->bhtg', Q, K) / np.sqrt(DH).astype(np.float32)
        scores = jnp.where(vision_mask[:, None, None, :], scores, -jnp.inf)
        topv, topi = jax.lax.top_k(scores, K_TOP)
        probs = jax.nn.softmax(topv, axis=-1)
        bi = jnp.arange(Bb)[:, None, None, None]
        hi = jnp.arange(H)[None, :, None, None]
        ti = jnp.arange(Tt)[None, None, :, None]
        attn = jnp.zeros_like(scores).at[bi, hi, ti, topi].set(probs)
        attn_mean = attn.mean(axis=1)
        V = x_vision @ Wv
        c_t = jnp.einsum('btg,bgd->btd', attn_mean, V)
        c_t = c_t * text_mask[..., None]
        x = layernorm(x_text, g_norm_in, b_norm_in)
        scale_in, shift_in = jnp.split(c_t @ W_film_in + b_film_in, 2, axis=-1)
        x = x * (1.0 + mod_gate * scale_in) + mod_gate * shift_in
        y = s4d(x, log_dt, A_re, A_im, C_re, C_im, D_skip)
        scale_out, shift_out = jnp.split(c_t @ W_film_out + b_film_out, 2, axis=-1)
        y = y * (1.0 + mod_gate * scale_out) + mod_gate * shift_out
        xt = x_text + y
        h = layernorm(xt, g_ffn, b_ffn)
        h = jax.nn.gelu(h @ W1 + b1, approximate=False) @ W2 + b2
        xt = xt + h
        return layernorm(xt, g_norm_out, b_norm_out)

    def _L2_ffn_ref(hidden_states, router_w, actor_w1, actor_b1, actor_w2, actor_b2, gate_w, up_w, down_w):
        import jax, jax.numpy as jnp
        import numpy as np
        B, S, H, E, I, MAX_K, A_HID = (2, 256, 128, 8, 336, 6, 50)
        probs = jax.nn.softmax(jnp.einsum('bsh,eh->bse', hidden_states, router_w).astype(jnp.float32), axis=-1)
        a_h = jax.nn.gelu(jnp.einsum('bsh,ah->bsa', hidden_states, actor_w1) + actor_b1)
        actor_logits = jnp.clip(jnp.einsum('bsa,ka->bsk', a_h, actor_w2) + actor_b2, -30.0, 30.0)
        sampled_k = jnp.argmax(actor_logits, axis=-1) + 1
        order = jnp.argsort(-probs, axis=-1)
        rank = jnp.argsort(order, axis=-1)
        mask = rank < sampled_k[..., None]
        scores = jnp.where(mask, probs, 0.0).astype(hidden_states.dtype)
        out = jnp.zeros_like(hidden_states)
        for e in range(E):
            g = jnp.einsum('bsh,ih->bsi', hidden_states, gate_w[e])
            u = jnp.einsum('bsh,ih->bsi', hidden_states, up_w[e])
            y = jnp.einsum('bsi,hi->bsh', jax.nn.silu(g) * u, down_w[e])
            out = out + scores[..., e:e + 1] * y
        return out

    def _L3_attn_ref(x, gamma, w_qkv, w_out):
        import jax, jax.numpy as jnp
        import numpy as np
        HEADS = 16
        DIM_HEAD = 64
        RMS_EPS = 1e-12
        b, n, dim = x.shape
        h, d = (HEADS, DIM_HEAD)
        l2 = jnp.maximum(jnp.linalg.norm(x, axis=-1, keepdims=True), RMS_EPS)
        normed = x / l2 * dim ** 0.5 * gamma
        qkv = (normed @ w_qkv).reshape(b, n, 3, h, d)
        qkv = jnp.transpose(qkv, (2, 0, 3, 1, 4))
        q, k, v = (qkv[0], qkv[1], qkv[2])
        q = q * d ** (-0.5)
        sim = jnp.einsum('bhid,bhjd->bhij', q, k)
        mask_value = -jnp.finfo(sim.dtype).max
        causal_mask = jnp.triu(jnp.ones((n, n), dtype=bool), k=1)
        sim = jnp.where(causal_mask, mask_value, sim)
        attn = jax.nn.softmax(sim, axis=-1)
        out = jnp.einsum('bhij,bhjd->bhid', attn, v)
        out = jnp.transpose(out, (0, 2, 1, 3)).reshape(b, n, h * d)
        return out @ w_out

    def _L3_xattn_ref(x, cond, q_w, q_b, kv_w, kv_b, proj_w, proj_b):
        import jax, jax.numpy as jnp
        import numpy as np
        NUM_HEADS = 16
        B, N, C = x.shape
        condN = cond.shape[1]
        H = NUM_HEADS
        hd = C // H
        scale = hd ** (-0.5)
        q = (x @ q_w + q_b).reshape(B, N, H, hd).transpose(0, 2, 1, 3)
        kv = (cond @ kv_w + kv_b).reshape(B, condN, 2, H, hd)
        k = kv[:, :, 0].transpose(0, 2, 1, 3)
        v = kv[:, :, 1].transpose(0, 2, 1, 3)
        attn = jnp.einsum('bhnd,bhmd->bhnm', q * scale, k)
        attn = jax.nn.softmax(attn, axis=-1)
        out = jnp.einsum('bhnm,bhmd->bhnd', attn, v)
        out = out.transpose(0, 2, 1, 3).reshape(B, N, C)
        return out @ proj_w + proj_b

    def _L3_ffn_ref(hidden_states, W_up, W_down, W_q, keys, down_embed, up_embed):
        import jax, jax.numpy as jnp
        import numpy as np
        B, T, H = (2, 256, 128)
        I = 512
        HEADS = 4
        RET = 128
        NUM_EXPERTS = 512
        NUM_KEYS = 64
        K = 8
        b, t, hd = hidden_states.shape
        h, nk, _, n = keys.shape
        q = jnp.einsum('btd,ed->bte', hidden_states, W_q)
        q = q.reshape(b, t, 2, h, n).transpose(2, 0, 1, 3, 4)
        sim = jnp.einsum('pbthn,hkpn->pbthk', q, keys)
        scores_xy, idx_xy = jax.lax.top_k(sim, K)
        sx, sy = (scores_xy[0], scores_xy[1])
        ix, iy = (idx_xy[0], idx_xy[1])
        all_scores = (sx[..., :, None] + sy[..., None, :]).reshape(b, t, h, K * K)
        all_idx = (ix[..., :, None] * nk + iy[..., None, :]).reshape(b, t, h, K * K)
        scores, pk = jax.lax.top_k(all_scores, K)
        indices = jnp.take_along_axis(all_idx, pk, axis=-1)
        de = down_embed[indices]
        ue = up_embed[indices]
        w = jax.nn.silu(jnp.einsum('btd,bthkd->bthk', hidden_states, de) * jax.nn.softmax(scores, axis=-1))
        experts_states = jnp.einsum('bthk,bthkd->btd', w, ue)
        dense = jnp.einsum('bti,di->btd', jax.nn.silu(jnp.einsum('btd,id->bti', hidden_states, W_up)), W_down)
        return dense + experts_states
    x = x + _L0_attn_ref(_layernorm(x, axis=-1), L0_attn_in_proj, L0_attn_out_proj, L0_attn_frequencies, L0_attn_decays, L0_attn_ss_W, L0_attn_ss_b, L0_attn_gate_W, L0_attn_gate_b, L0_attn_fin_W, L0_attn_fin_b)
    x = x + _L0_xattn_ref(_layernorm(x, axis=-1), ctx_768, ctx_768, L0_xattn_Wq, L0_xattn_bq, L0_xattn_Wk, L0_xattn_bk, L0_xattn_Wv, L0_xattn_bv, L0_xattn_Wo, L0_xattn_bo, L0_xattn_ln_gamma, L0_xattn_ln_beta)
    x = x + _L0_ffn_ref(_layernorm(x, axis=-1), L0_ffn_router_w, L0_ffn_w_gate, L0_ffn_w_up, L0_ffn_w_down)
    x = x + _L1_attn_ref(_layernorm(x, axis=-1), L1_attn_Wproj, L1_attn_bproj, L1_attn_W0, L1_attn_ln_g, L1_attn_ln_b, L1_attn_gn_g, L1_attn_gn_b, L1_attn_Wout, L1_attn_bout)
    x = x + _L1_xattn_ref(ctx_768, _layernorm(x, axis=-1), mask_BxS2_bk0, L1_xattn_ln_x_g, L1_xattn_ln_x_b, L1_xattn_ln_l_g, L1_xattn_ln_l_b, L1_xattn_qn_g, L1_xattn_kn_g, L1_xattn_Wq, L1_xattn_Wkv, L1_xattn_Wlkv, L1_xattn_Wo, L1_xattn_bo)
    x = x + _L1_ffn_ref(_layernorm(x, axis=-1), L1_ffn_gate_w, L1_ffn_gate_b, L1_ffn_w1, L1_ffn_w2, L1_ffn_w3, L1_ffn_ws1, L1_ffn_ws2, L1_ffn_ws3)
    x = x + _L2_attn_ref(_layernorm(x, axis=-1), L2_attn_W_qkv, L2_attn_W_out, L2_attn_b_out)
    x = x + _L2_xattn_ref(_layernorm(x, axis=-1), ctx_768, mask_BxS_bf1, mask_BxS2_bf1, L2_xattn_Wq, L2_xattn_Wk, L2_xattn_Wv, L2_xattn_W_film_in, L2_xattn_b_film_in, L2_xattn_W_film_out, L2_xattn_b_film_out, L2_xattn_g_norm_in, L2_xattn_b_norm_in, L2_xattn_g_norm_out, L2_xattn_b_norm_out, L2_xattn_g_ffn, L2_xattn_b_ffn, L2_xattn_W1, L2_xattn_b1, L2_xattn_W2, L2_xattn_b2, L2_xattn_log_dt, L2_xattn_A_re, L2_xattn_A_im, L2_xattn_C_re, L2_xattn_C_im, L2_xattn_D_skip, L2_xattn_mod_gate)
    x = x + _L2_ffn_ref(_layernorm(x, axis=-1), L2_ffn_router_w, L2_ffn_actor_w1, L2_ffn_actor_b1, L2_ffn_actor_w2, L2_ffn_actor_b2, L2_ffn_gate_w, L2_ffn_up_w, L2_ffn_down_w)
    x = x + _L3_attn_ref(_layernorm(x, axis=-1), L3_attn_gamma, L3_attn_w_qkv, L3_attn_w_out)
    x = x + _L3_xattn_ref(_layernorm(x, axis=-1), ctx_768, L3_xattn_q_w, L3_xattn_q_b, L3_xattn_kv_w, L3_xattn_kv_b, L3_xattn_proj_w, L3_xattn_proj_b)
    x = x + _L3_ffn_ref(_layernorm(x, axis=-1), L3_ffn_W_up, L3_ffn_W_down, L3_ffn_W_q, L3_ffn_keys, L3_ffn_down_embed, L3_ffn_up_embed)
    return x

_drawn_inputs = setup_inputs


def setup_inputs(seed=0):
    import zlib

    import numpy as np

    out = dict(_drawn_inputs(seed))
    spreads = {'L0_attn_decays': (-0.6931471824645996, 0.2),
     'L0_xattn_bq': (0.0, 0.1),
     'L0_xattn_bk': (0.0, 2.0),
     'L0_xattn_bv': (0.0, 0.1),
     'L0_xattn_bo': (0.0, 0.1),
     'L0_xattn_ln_gamma': (1.0, 0.2),
     'L0_xattn_ln_beta': (0.0, 0.1),
     'L1_attn_ln_g': (1.0, 0.2),
     'L1_attn_ln_b': (0.0, 0.1),
     'L1_attn_gn_g': (1.0, 0.2),
     'L1_attn_gn_b': (0.0, 0.1),
     'L1_xattn_ln_x_g': (1.0, 0.6),
     'L1_xattn_ln_x_b': (0.0, 0.8),
     'L1_xattn_ln_l_g': (1.0, 0.2),
     'L1_xattn_ln_l_b': (0.0, 0.1),
     'L1_xattn_qn_g': (1.0, 0.6),
     'L1_xattn_kn_g': (1.0, 0.6),
     'L1_xattn_bo': (0.0, 0.1),
     'L1_ffn_gate_b': (0.0, 0.8),
     'L2_xattn_b_film_in': (0.0, 0.373),
     'L2_xattn_b_film_out': (0.0, 0.431),
     'L2_xattn_g_norm_in': (1.0, 0.2),
     'L2_xattn_b_norm_in': (0.0, 0.278),
     'L2_xattn_g_norm_out': (1.0, 0.2),
     'L2_xattn_b_norm_out': (0.0, 0.317),
     'L2_xattn_g_ffn': (1.0, 0.6),
     'L2_xattn_b_ffn': (0.0, 0.8),
     'L2_xattn_b1': (0.0, 0.8),
     'L2_xattn_b2': (0.0, 1.24),
     'L2_xattn_A_re': (-0.5, 0.6),
     'L2_ffn_actor_b1': (0.0, 0.1),
     'L2_ffn_actor_b2': (0.0, 0.8),
     'L3_attn_gamma': (1.0, 0.6),
     'L3_xattn_q_b': (0.0, 2.0),
     'L3_xattn_kv_b': (0.0, 0.551),
     'L3_xattn_proj_b': (0.0, 0.606)}
    factors = {'L0_attn_ss_b': 3.603,
     'L0_xattn_Wk': 47.054,
     'L1_attn_bout': 4.181,
     'L1_ffn_gate_w': 8.0,
     'L1_ffn_w1': 8.0,
     'L1_ffn_w2': 8.0,
     'L1_ffn_w3': 8.0,
     'L1_ffn_ws1': 8.0,
     'L1_ffn_ws2': 8.0,
     'L1_ffn_ws3': 8.0,
     'L2_xattn_Wq': 8.0,
     'L2_xattn_Wk': 8.0,
     'L2_xattn_Wv': 8.0,
     'L2_xattn_W_film_in': 8.0,
     'L2_xattn_W_film_out': 8.0,
     'L2_xattn_W1': 4.921,
     'L2_xattn_W2': 4.577,
     'L2_ffn_router_w': 8.0,
     'L2_ffn_gate_w': 8.0,
     'L2_ffn_up_w': 8.0,
     'L2_ffn_down_w': 8.0,
     'L3_ffn_W_up': 3.131,
     'L3_ffn_W_down': 3.148,
     'L3_ffn_W_q': 32.823,
     'L3_ffn_keys': 32.855,
     'L3_ffn_down_embed': 8.0,
     'L3_ffn_up_embed': 8.0,
     'L2_attn_b_out': 3.927}
    for name, (base, spread) in spreads.items():
        noise = np.random.default_rng([zlib.crc32(name.encode()), seed]).standard_normal(out[name].shape)
        drawn = base * np.exp(spread * noise) if base else spread * noise
        out[name] = jnp.asarray(drawn.astype(out[name].dtype))
    for name, factor in factors.items():
        out[name] = (out[name] * factor).astype(out[name].dtype)
    return out
```

```python
from collections import namedtuple
from contextlib import ExitStack, contextmanager

import numpy as np

import concourse.bass as bass
from concourse import mybir

F32 = mybir.dt.float32
BF16 = mybir.dt.bfloat16
I32 = mybir.dt.int32
U8 = mybir.dt.uint8
U32 = mybir.dt.uint32
ALU = mybir.AluOpType
ACT = mybir.ActivationFunctionType
AX = mybir.AxisListType

NB, S, D = 32, 128, 128
SC, DC = 120, 96
P = 128
EPS = 1e-5
DMA = 16


def row(t, i):
    return t[:, bass.ds(i, 1), :].rearrange("p a n -> p (a n)")


class Named:
    pass


class Chain:

    def __init__(self, eng, sem):
        self.eng, self.sem, self.n = eng, sem, 0

    def restart(self):
        self.eng.sem_clear(self.sem)
        self.n = 0

    def __call__(self, ins):
        self.n += 1
        ins.then_inc(self.sem, 1)
        self.eng.wait_ge(self.sem, self.n)


@contextmanager
def phase(nc, label, names):
    with ExitStack() as ctx:
        fields, start = [n.split("+")[0] for n in names.split()], [int((n + "+0").split("+")[1]) for n in names.split()]
        s = namedtuple("Semaphores", fields)(*(ctx.enter_context(nc.semaphore(f"{label}_{n}")) for n in fields))
        for sem, n in zip(s, start):
            if n:
                nc.gpsimd.sem_inc(sem, n)

        def sb(name, shape, dt=F32):
            return ctx.enter_context(nc.sbuf_tensor(f"{label}_{name}", shape, dt))

        def ps(name, shape, dt=F32):
            return ctx.enter_context(nc.psum_tensor(f"{label}_{name}", shape, dt))

        yield s, sb, ps
        nums = sorted(x.num for x in s)
        for n in nums:
            nc.gpsimd.sem_clear(range(n, n + 1))
        nc.all_engine_barrier()


def norm_vector(R, dve, s):
    dve.tensor_scalar(R.vareps[:], R.stats[:, :, 1], EPS, None, ALU.add).then_inc(s.var_ready, 1)
    dve.wait_ge(s.rstd_ready, 1)
    dve.scalar_tensor_tensor(out=R.shift[:], in0=R.stats[:, :, 0], scalar=-1.0, in1=R.rstd[:],
                             op0=ALU.mult, op1=ALU.mult).then_inc(s.shift_ready, 1)
    dve.wait_ge(s.shift_ready, 1)


def norm_pool(R, pool, s):
    pool.wait_ge(s.var_ready, 1)
    pool.tensor_tensor(R.rstd[:], R.vareps[:], R.minus_half[:], ALU.pow).then_inc(s.rstd_ready, 1)


def normalised(R, dve, i, out):
    return dve.tensor_scalar(out, row(R.x, i), R.rstd[:, bass.ds(i, 1)], R.shift[:, bass.ds(i, 1)],
                             ALU.mult, ALU.add)


def row_stats(R, dve, i, chain):
    chain(dve.bn_stats(R.bn[:, 0], row(R.x, i)))
    chain(dve.bn_aggr(R.aggr[:, 0], R.bn[:, 0]))
    return dve.tensor_copy(row(R.stats, i), R.aggr[:, 0])


def pair(t, i):
    return t[:, bass.ds(i * 2, 2), :]


def side(t):
    return t.rearrange("p (r n) -> p r n", r=2)


def both(t):
    return t[:].unsqueeze(1).broadcast_to((P, 2, P))


def pair_normalised(R, dve, i, out):
    normalised(R, dve, i * 2, out[:, 0])
    return normalised(R, dve, i * 2 + 1, out[:, 1])


def pair_stats(R, dve, i, chain):
    for r in range(2):
        last = dve.bn_stats(R.bn[:, r], row(R.x, i * 2 + r))
    chain(last)
    for r in range(2):
        last = dve.bn_aggr(R.aggr[:, r], R.bn[:, r])
    chain(last)
    return dve.tensor_copy(pair(R.stats, i), R.aggr[:, 0:2])


PHASES, LAYOUTS = [], []


def transposed(a, n, *axes):
    return np.ascontiguousarray(np.transpose(a[n], axes or None))


def repeated(a, n):
    return np.ascontiguousarray(np.broadcast_to(a[n].reshape(1, -1), (P, a[n].size)))


def column(a, n):
    return np.ascontiguousarray(a[n].reshape(-1, 1))


def load(sp, A, sem, pairs):
    for tile, name in pairs:
        sp.dma_start(tile[:], A[name]).then_inc(sem, DMA)


U = 2


def held(i, n=U):
    return [(u, i * n + u, i * n + (u + 1)) for u in range(n)]

TWO_PI = (6.28125, 0.0019340515136718750, 1.2556659146e-06)
ROUND = 12582912.0


def turns_removed(dve, chain, arg, n):
    chain(dve.tensor_scalar(n, arg, float(1 / (2 * np.pi)), ROUND, ALU.mult, ALU.add))
    chain(dve.tensor_scalar(n, n, ROUND, None, ALU.subtract))
    for part in TWO_PI:
        chain(dve.scalar_tensor_tensor(out=arg, in0=n, scalar=-part, in1=arg, op0=ALU.mult, op1=ALU.add))
    chain(dve.tensor_scalar(arg, arg, 3.1415925, -3.1415925, ALU.min, ALU.max))


def flip_vector(R, dve, s, T):
    E = T.router.shape[1]
    with dve.Fori(0, NB // 4 // U) as i:
        for u, b, n in held(i):
            for r in range(4):
                last = normalised(R, dve, b * 4 + r, T.xhat[:, u, r])
            last.then_inc(s.xhat_ready, 1)
        for u, b, n in held(i):
            dve.wait_ge(s.logits_psum, n)
            dve.tensor_copy(T.logits[:, bass.ds(b * 4, 4), :], T.p_r[:, u, 0:4 * E].rearrange("p (r e) -> p r e", r=4)).then_inc(s.logits_ready, 1)


def flip_tensor(R, pe, s, T):
    E = T.router.shape[1]
    with pe.Fori(0, NB // 4 // U) as i:
        for u, b, n in held(i):
            pe.wait_ge(s.xhat_ready, n)
            for r in range(4):
                mm = pe.transpose(T.p_t[:, u, r * P:(r + 1) * P], T.xhat[:, u, r], R.ident[:])
            mm.then_inc(s.xT_psum, 1)
        for u, b, n in held(i):
            pe.wait_ge(s.xT_ready, n)
            for r in range(4):
                mm = pe.matmul(T.p_r[:, u, r * E:(r + 1) * E], T.xT[:, u, r * P:(r + 1) * P], T.router[:], start=True, stop=True)
            mm.then_inc(s.logits_psum, 1)


def flip_scalar(R, act, s, T):
    with act.Fori(0, NB // 4 // U) as i:
        for u, b, n in held(i):
            act.wait_ge(s.xT_psum, n)
            act.activation(T.xT[:, u], T.p_t[:, u], ACT.Copy)
            act.activation(row(T.xTall[:].rearrange("p (g r) t -> p g (r t)", r=4), b), T.p_t[:, u], ACT.Copy).then_inc(s.xT_ready, 1)


FLIP = "var_ready rstd_ready shift_ready vchain w_in xhat_ready xT_psum xT_ready logits_psum logits_ready "


def flip_buffers(sb, ps, router, p_t, p_r):
    T = Named()
    T.router = router
    T.xhat = sb("f_xhat", [P, U, 4, P])
    T.xTall = sb("f_xTall", [P, NB, P])
    T.xT, T.logits = sb("f_xT", [P, U, 4 * P]), sb("f_logits", [P, NB, router.shape[1]])
    T.p_t, T.p_r = p_t, p_r
    return T


def all_row_stats(R, dve, chain):
    with dve.Fori(0, NB // 8) as i:
        chain.restart()
        for r in range(8):
            last = dve.bn_stats(R.bn[:, r], row(R.x, i * 8 + r))
        chain(last)
        for r in range(8):
            last = dve.bn_aggr(R.aggr[:, r], R.bn[:, r])
        chain(last)
        chain(dve.tensor_copy(R.stats[:, bass.ds(i * 8, 8), :], R.aggr[:]))


EXPERTS = "wexp_in0 wexp_in1 gate_psum up_psum silu_ready h_ready+2 down_psum out_added+2 "
G, NG = 4, NB // 4


def experts_buffers(sb, ps, E, FC, FP, names, cw):
    NW = min(E, 2)
    X = Named()
    X.E = E
    X.FC = FC
    X.FP = FP
    X.names = names
    X.cw = cw
    X.NW = NW
    X.wg = sb("wg", [P, NW, FC * FP])
    X.wu = sb("wu", [P, NW, FC * FP])
    X.wd = sb("wd", [FP, NW, FC * P])
    X.sg = sb("sg", [FP, 2, G * P])
    X.h = sb("h", [FP, 2, FC, G * P])
    X.p_g = ps("p_g", [P, 2, 512])
    X.p_u = ps("p_u", [P, 2, 512])
    X.p_o = ps("p_o", [P, 2, 512])
    X.landed = 3 * DMA
    return X


def experts_sync(sp, A, s, X):
    def expert(e, w):
        for dst, name in zip((X.wg, X.wu, X.wd), X.names):
            sp.dma_start(dst[:, w], A[name][bass.ds(e * X.NW + w, 1)].rearrange("a p n -> p (a n)")).then_inc(
                [s.wexp_in0, s.wexp_in1][w], DMA)

    for w in range(X.NW):
        expert(0, w)
    if X.E > 2:
        with sp.Fori(1, X.E // 2) as e:
            for w in range(2):
                sp.wait_ge(s.down_psum, (e * 2 + (w - 1)) * NG)
                expert(e, w)


def experts_tensor(R, pe, s, X, T):
    groups = T.xTall[:].rearrange("p (g r) t -> p g (r t)", r=G)
    with pe.Fori(0, X.E // X.NW) as e:
        for w in range(X.NW):
            with pe.Fori(0, NG // 2) as j:
                pe.wait_ge([s.wexp_in0, s.wexp_in1][w], (e + 1) * X.landed)
                group = (e * X.NW + w) * NG + j * 2
                for k in range(2 * X.FC):
                    v, f = divmod(k, X.FC)
                    x = row(groups, j * 2 + v)
                    if k >= 2:
                        pe.wait_ge(s.silu_ready, group * X.FC + (k - 1))
                    pe.matmul(X.p_g[0:X.FP, k % 2], X.wg[:, w, f * X.FP:(f + 1) * X.FP], x, start=True, stop=True).then_inc(s.gate_psum, 1)
                    if k >= 2:
                        pe.wait_ge(s.h_ready, group * X.FC + (k + 1))
                    pe.matmul(X.p_u[0:X.FP, k % 2], X.wu[:, w, f * X.FP:(f + 1) * X.FP], x, start=True, stop=True).then_inc(s.up_psum, 1)
                for v in range(2):
                    pe.wait_ge(s.h_ready, (group + (v + 1)) * X.FC + 2)
                    pe.wait_ge(s.out_added, group + (v + 1))
                    for q in range(G):
                        for f in range(X.FC):
                            mm = pe.matmul(X.p_o[:, v, q * P:(q + 1) * P], X.h[:, v, f, q * P:(q + 1) * P],
                                           X.wd[:, w, f * P:(f + 1) * P], start=(f == 0), stop=(f == X.FC - 1))
                    mm.then_inc(s.down_psum, 1)


def experts_scalar(act, s, X):
    with act.Fori(0, X.E * NG // 2) as g:
        for k in range(2 * X.FC):
            act.wait_ge(s.gate_psum, g * (2 * X.FC) + (k + 1))
            act.wait_ge(s.h_ready, g * (2 * X.FC) + (k + 1))
            act.activation(X.sg[:, k % 2], X.p_g[0:X.FP, k % 2], ACT.Silu).then_inc(s.silu_ready, 1)


def experts_vector(R, dve, s, X):
    with dve.Fori(0, X.E // X.NW) as e:
        for w in range(X.NW):
            with dve.Fori(0, NG // 2) as j:
                group = (e * X.NW + w) * NG + j * 2
                for k in range(2 * X.FC):
                    dve.wait_ge(s.silu_ready, group * X.FC + (k + 1))
                    dve.wait_ge(s.up_psum, group * X.FC + (k + 1))
                    dve.tensor_tensor(X.h[:, k // X.FC, k % X.FC], X.sg[:, k % 2], X.p_u[0:X.FP, k % 2], ALU.mult).then_inc(s.h_ready, 1)
                for v in range(2):
                    dve.wait_ge(s.down_psum, group + (v + 1))
                    for q in range(G):
                        b = (j * 2 + v) * G + q
                        if X.cw is None:
                            add = dve.tensor_tensor(row(R.x, b), X.p_o[:, v, q * P:(q + 1) * P], row(R.x, b), ALU.add)
                        else:
                            weight = X.cw[:, bass.ds(b, 1), bass.ds(e * X.NW + w, 1)].rearrange("p a c -> p (a c)")
                            add = dve.scalar_tensor_tensor(out=row(R.x, b), in0=X.p_o[:, v, q * P:(q + 1) * P], scalar=weight,
                                                           in1=row(R.x, b), op0=ALU.mult, op1=ALU.add)
                    add.then_inc(s.out_added, 1)

def l0_attn(nc, R, A):
    NS, GROUP = 64, 32
    kernel_rows = nc.dram_tensor("kernel_rows", (P, 2 * S), F32, kind="Internal").ap()
    with phase(nc, "l0_attn", "var_ready rstd_ready shift_ready w_in vchain decay_ready phase_ready trig_ready envelope_ready "
                   "kernel_ready kernel_psum padded kernel_out toeplitz_in all_normal conv_psum conv_copied "
                   "xhat_ready y_ready xyT_psum xyT_ready gates_psum gelu_ready prod_ready out_psum "
                   ) as (s, sb, ps):
        ssW, gateW, finW, finb = sb("ssW", [P, P]), sb("gateW", [P, P]), sb("finW", [P, P]), sb("finb", [P, P])
        ssb, gateb = sb("ssb", [P, 1]), sb("gateb", [P, 1])
        inT, outp = sb("inT", [NS, P]), sb("outp", [NS, P])
        freq, decay, times = sb("freq", [NS, 1]), sb("decay", [NS, 1]), sb("times", [NS, S])
        rate = sb("rate", [NS, 2])
        arg, turns, env, coef = sb("arg", [NS, S]), sb("turns", [NS, S]), sb("env", [NS, S]), sb("coef", [NS, P])
        kpad, toep = sb("kpad", [P, 2 * S]), sb("toep", [P, P, S])
        xall, y = sb("xall", [P, NB, D]), sb("y", [P, NB, D])
        xhat, yrow, xyT, gates, prod = sb("xhat", [P, U, 2, P]), sb("yrow", [P, U, 2, P]), sb("xyT", [P, U, 512]), sb("gates", [P, U, 512]), sb("prod", [P, U, 256])
        p_conv = ps("p_conv", [P, 2, GROUP, 32])
        p_t, p_g = ps("p_t", [P, U, 512]), ps("p_g", [P, U, 512])
        p_o = p_conv[:].rearrange("p g j b -> p (g j b)").rearrange("p (k c) -> p k c", c=512)[:, 0:U]
        toeplitz = bass.AP(kernel_rows.tensor, 0, [[1, P], [2 * S, P], [1, S]])
        with nc.Block() as block:
            @block.sync
            def _(sp):
                load(sp, A, s.w_in, [(freq, "L0_attn_frequencies"), (decay, "L0_attn_decays"), (times, "c_times"),
                                     (inT, "L0_attn_in_proj"), (outp, "L0_attn_out_proj"), (ssW, "L0_attn_ss_W"),
                                     (gateW, "L0_attn_gate_W"), (finW, "L0_attn_fin_W"), (finb, "L0_attn_fin_b"),
                                     (ssb, "L0_attn_ss_b"), (gateb, "L0_attn_gate_b")])
                sp.wait_ge(s.padded, 1)
                sp.dma_start(kernel_rows, kpad[:]).then_inc(s.kernel_out, DMA)
                sp.wait_ge(s.kernel_out, DMA)
                sp.dma_start(toep[:], toeplitz).then_inc(s.toeplitz_in, DMA)

            @block.gpsimd
            def _(pool):
                norm_pool(R, pool, s)
                pool.wait_ge(s.conv_copied, 4)
                with pool.Fori(0, NB // 2 // U) as i:
                    for u, b, n in held(i):
                        pool.wait_ge(s.xhat_ready, n)
                        pool.tensor_copy(yrow[:, u], pair(y, b)).then_inc(s.y_ready, 1)

            @block.vector
            def _(dve):
                chain = Chain(dve, s.vchain)
                dve.wait_ge(s.w_in, 11 * DMA)
                chain(dve.tensor_scalar(rate[:, 0:1], freq[:], float(np.float32(2 * np.pi)), None, ALU.mult))
                chain(dve.tensor_scalar(arg[:], times[:], rate[:, 0:1], None, ALU.mult))
                turns_removed(dve, chain, arg[:], turns[:])
                dve.tensor_tensor(coef[:], inT[:], outp[:], ALU.mult).then_inc(s.phase_ready, 1)
                dve.wait_ge(s.decay_ready, 1)
                dve.tensor_scalar(env[:], times[:], rate[:, 1:2], -1.0, ALU.mult, ALU.mult).then_inc(s.envelope_ready, 1)
                dve.wait_ge(s.trig_ready, 2)
                chain(dve.tensor_tensor(arg[:], arg[:], arg[:], ALU.mult))
                chain(dve.tensor_scalar(arg[:], arg[:], -2.0, 1.0, ALU.mult, ALU.add))
                dve.tensor_tensor(arg[:], arg[:], env[:], ALU.mult).then_inc(s.kernel_ready, 1)
                norm_vector(R, dve, s)
                chain(dve.memset(kpad[:, S:2 * S], 0.0))
                dve.wait_ge(s.kernel_psum, 1)
                dve.tensor_copy(kpad[:, 0:S], p_t[:, 0, 0:S]).then_inc(s.padded, 1)
                with dve.Fori(0, NB) as i:
                    normalised(R, dve, i, row(xall, i)).then_inc(s.all_normal, 1)
                with dve.Fori(0, NB // 2 // U) as i:
                    chain.restart()
                    for u, b, n in held(i):
                        pair_normalised(R, dve, b, xhat[:, u]).then_inc(s.xhat_ready, 1)
                    for u, b, n in held(i):
                        dve.wait_ge(s.gelu_ready, n)
                        dve.tensor_tensor(prod[:, u], gates[:, u, 0:256], gates[:, u, 256:512], ALU.mult).then_inc(s.prod_ready, 1)
                        chain(dve.tensor_tensor(pair(R.x, b), pair(R.x, b), finb[:].unsqueeze(1).broadcast_to((P, 2, P)), ALU.add))
                    for u, b, n in held(i):
                        dve.wait_ge(s.out_psum, n)
                        chain(dve.tensor_tensor(pair(R.x, b), pair(R.x, b), side(p_o[:, u, 0:256]), ALU.add))
                        chain(pair_stats(R, dve, b, chain))

            @block.scalar
            def _(act):
                act.wait_ge(s.w_in, 11 * DMA)
                act.activation(rate[:, 1:2], decay[:], ACT.Exp).then_inc(s.decay_ready, 1)
                act.wait_ge(s.envelope_ready, 1)
                act.activation(env[:], env[:], ACT.Exp).then_inc(s.trig_ready, 1)
                act.wait_ge(s.phase_ready, 1)
                act.activation(arg[:], arg[:], ACT.Sin, scale=0.5).then_inc(s.trig_ready, 1)
                for g in range(P // GROUP):
                    act.wait_ge(s.conv_psum, g + 1)
                    act.activation(y[:, :, g * GROUP:(g + 1) * GROUP].rearrange("p b h -> p h b"),
                                   p_conv[:, g % 2, :, 0:NB], ACT.Copy).then_inc(s.conv_copied, 1)
                with act.Fori(0, NB // 2 // U) as i:
                    for u, b, n in held(i):
                        act.wait_ge(s.xyT_psum, n)
                        act.activation(xyT[:, u, 0:256], p_t[:, u, 0:256], ACT.Copy)
                        act.activation(side(xyT[:, u, 256:512]), side(p_t[:, u, 256:512])[:, :, ::-1], ACT.Copy).then_inc(s.xyT_ready, 1)
                    for u, b, n in held(i):
                        act.wait_ge(s.gates_psum, n)
                        act.activation(gates[:, u, 0:256], p_g[:, u, 0:256], ACT.Gelu, bias=gateb[:])
                        act.activation(gates[:, u, 256:512], p_g[:, u, 256:512], ACT.Gelu, bias=ssb[:]).then_inc(s.gelu_ready, 1)

            @block.tensor
            def _(pe):
                pe.wait_ge(s.kernel_ready, 1)
                pe.matmul(p_t[:, 0, 0:S], coef[:], arg[:], start=True, stop=True).then_inc(s.kernel_psum, 1)
                pe.wait_ge(s.all_normal, NB)
                pe.wait_ge(s.toeplitz_in, DMA)
                for h in range(P):
                    g, j = divmod(h, GROUP)
                    if j == 0 and g >= 2:
                        pe.wait_ge(s.conv_copied, g - 1)
                    mm = pe.matmul(p_conv[:, g % 2, j, 0:NB], toep[:, h, :], xall[:, :, h], start=True, stop=True)
                    if j == GROUP - 1:
                        mm.then_inc(s.conv_psum, 1)
                pe.wait_ge(s.conv_copied, P // GROUP)
                with pe.Fori(0, NB // 2 // U) as i:
                    for u, b, n in held(i):
                        pe.wait_ge(s.xhat_ready, n)
                        pe.wait_ge(s.y_ready, n)
                        for k, rows in enumerate((xhat, yrow)):
                            for r in range(2):
                                mm = pe.transpose(p_t[:, u, k * 256 + r * P:k * 256 + (r + 1) * P], rows[:, u, r], R.ident[:])
                        mm.then_inc(s.xyT_psum, 1)
                    for u, b, n in held(i):
                        pe.wait_ge(s.xyT_ready, n)
                        pe.matmul(p_g[:, u, 0:256], gateW[:], xyT[:, u, 0:256], start=True, stop=True)
                        pe.matmul(p_g[:, u, 256:512], ssW[:], xyT[:, u, 256:512], start=True, stop=True).then_inc(s.gates_psum, 1)
                    for u, b, n in held(i):
                        pe.wait_ge(s.prod_ready, n)
                        for r in range(2):
                            mm = pe.matmul(p_o[:, u, r * P:(r + 1) * P], prod[:, u, r * P:(r + 1) * P], finW[:], start=True, stop=True)
                        mm.then_inc(s.out_psum, 1)


PHASES.append(l0_attn)
LAYOUTS.append(lambda a: {
    "L0_attn_frequencies": column(a, "L0_attn_frequencies"), "L0_attn_decays": column(a, "L0_attn_decays"),
    "c_times": np.ascontiguousarray(np.broadcast_to(np.arange(S - 1, -1, -1, dtype=np.float32), (64, S))),
    "L0_attn_in_proj": transposed(a, "L0_attn_in_proj"), "L0_attn_out_proj": a["L0_attn_out_proj"],
    "L0_attn_ss_W": transposed(a, "L0_attn_ss_W"), "L0_attn_gate_W": transposed(a, "L0_attn_gate_W"),
    "L0_attn_fin_W": transposed(a, "L0_attn_fin_W"), "L0_attn_fin_b": repeated(a, "L0_attn_fin_b"),
    "L0_attn_ss_b": column(a, "L0_attn_ss_b"), "L0_attn_gate_b": column(a, "L0_attn_gate_b")})

def l0_xattn(nc, R, A):
    H, HD = 16, 8
    SCALE = HD ** -0.5
    with phase(nc, "l0_xattn", "var_ready rstd_ready shift_ready w_in ones_set vchain xhat_ready ctx_ready xT_psum xT_ready q_psum kv_psum "
                   "kT_ready squares_q squares_k norms_ready powers_ready qn_ready qnT_psum qmask_ready scores_psum "
                   "exp_ready av_psum heads_ready headsT_psum headsT_ready out_psum lnvar_ready lnrstd_ready row_done "
                   ) as (s, sb, ps):
        wq, wo, wkv = sb("wq", [P, P]), sb("wo", [P, P]), sb("wkv", [DC + 1, 256])
        bq, bo, gam, bet = sb("bq", [P, P]), sb("bo", [P, P]), sb("gam", [P, P]), sb("bet", [P, P])
        xhat, xT, cT = sb("xhat", [P, U, P]), sb("xT", [P, U, P]), sb("cT", [DC + 1, U, SC])
        qp, qpo, qn, sq = sb("qp", [P, U, P]), sb("qpo", [P, U, P]), sb("qn", [P, U, P]), sb("sq", [P, U, P])
        kT, va = sb("kT", [P, U, SC]), sb("va", [P, U, H, HD + 1])
        sums, powers, kscale = sb("sums", [P, U, 2]), sb("powers", [P, U, 2]), sb("kscale", [P, U])
        qm, E = sb("qm", [P, U, H, P]), sb("E", [P, U, H, P])
        rden, heads, headsT = sb("rden", [P, U, H]), sb("heads", [P, U, P]), sb("headsT", [P, U, P])
        z, ln, bn = sb("z", [P, U, P]), sb("ln", [P, U, 6]), sb("bn6", [P, U, 6])
        p_s, p_m, p_t = ps("p_s", [P, U, 8, P]), ps("p_m", [P, U, 512]), ps("p_t", [P, U, 512])
        with nc.Block() as block:
            @block.sync
            def _(sp):
                load(sp, A, s.w_in, [(wq, "L0_xattn_Wq"), (wo, "L0_xattn_Wo"), (bq, "L0_xattn_bq"), (bo, "L0_xattn_bo"),
                                     (gam, "L0_xattn_ln_gamma"), (bet, "L0_xattn_ln_beta")])
                for n, c in (("k", 0), ("v", P)):
                    sp.dma_start(wkv[0:DC, c:c + P], A[f"L0_xattn_W{n}"]).then_inc(s.w_in, DMA)
                    sp.dma_start(wkv[DC:DC + 1, c:c + P], A[f"L0_xattn_b{n}"]).then_inc(s.w_in, DMA)

            @block.gpsimd
            def _(pool):
                norm_pool(R, pool, s)
                with pool.Fori(0, NB // U) as i:
                    for u, b, n in held(i):
                        pool.wait_ge(s.xhat_ready, n)
                        pool.tensor_copy(cT[:, u], row(R.ctxT, b)).then_inc(s.ctx_ready, 1)
                    for u, b, n in held(i):
                        pool.wait_ge(s.norms_ready, n)
                        pool.tensor_tensor(powers[:, u], sums[:, u], R.minus_half[:, 0:2], ALU.pow).then_inc(s.powers_ready, 1)
                    pool.wait_ge(s.lnvar_ready, i + 1)
                    pool.tensor_tensor(ln[:, :, 3], ln[:, :, 2], R.minus_half[:, 0:U], ALU.pow).then_inc(s.lnrstd_ready, 1)

            @block.vector
            def _(dve):
                chain = Chain(dve, s.vchain)
                norm_vector(R, dve, s)
                dve.memset(sums[:], 1.0)
                dve.memset(va[:, :, :, HD:HD + 1], 1.0).then_inc(s.ones_set, 1)
                dve.wait_ge(s.w_in, 10 * DMA)
                with dve.Fori(0, NB // U) as i:
                    chain.restart()
                    for u, b, n in held(i):
                        normalised(R, dve, b, xhat[:, u]).then_inc(s.xhat_ready, 1)
                    for u, b, n in held(i):
                        dve.wait_ge(s.q_psum, n)
                        chain(dve.tensor_tensor(qp[:, u], p_t[:, u, 384:512], bq[:], ALU.add))
                        chain(dve.tensor_tensor_reduce(sq[:, u], qp[:, u], qp[:, u], 1.0, 0.0, ALU.mult, ALU.add, sums[:, u, 0:1]))
                        dve.tensor_tensor(qpo[:, u], qp[:, u], bo[:], ALU.add)
                        dve.wait_ge(s.squares_k, n)
                        dve.tensor_scalar(sums[:, u], sums[:, u], 1e-24, None, ALU.max).then_inc(s.norms_ready, 1)
                    for u, b, n in held(i):
                        dve.wait_ge(s.powers_ready, n)
                        dve.tensor_scalar(kscale[:, u:u + 1], powers[:, u, 1:2], SCALE, None, ALU.mult)
                        dve.tensor_scalar(qn[:, u], qp[:, u], powers[:, u, 0:1], None, ALU.mult).then_inc(s.qn_ready, 1)
                    for u, b, n in held(i):
                        dve.wait_ge(s.qnT_psum, n)
                        dve.tensor_tensor(qm[:, u], p_t[:, u, P:256].unsqueeze(1).broadcast_to((P, H, P)),
                                          R.head8[:].unsqueeze(2).broadcast_to((P, H, P)), ALU.mult).then_inc(s.qmask_ready, 1)
                    for u, b, n in held(i):
                        dve.wait_ge(s.av_psum, n)
                        av = p_m[:, u, 0:H * (HD + 1)].rearrange("p (h e) -> p h e", h=H)
                        chain(dve.reciprocal(rden[:, u], av[:, :, HD]))
                        dve.tensor_tensor(heads[:, u].rearrange("p (h e) -> p h e", h=H), av[:, :, 0:HD],
                                          rden[:, u].unsqueeze(2).broadcast_to((P, H, HD)), ALU.mult).then_inc(s.heads_ready, 1)
                    dve.wait_ge(s.out_psum, (i + 1) * U)
                    chain(dve.tensor_tensor(z[:], p_m[:, :, 256:384], qpo[:], ALU.add))
                    for u in range(U):
                        last = dve.bn_stats(bn[:, u], z[:, u])
                    chain(last)
                    for u in range(U):
                        last = dve.bn_aggr(ln[:, u, 0:2], bn[:, u])
                    chain(last)
                    dve.tensor_scalar(ln[:, :, 2], ln[:, :, 1], EPS, None, ALU.add).then_inc(s.lnvar_ready, 1)
                    dve.wait_ge(s.lnrstd_ready, i + 1)
                    for u in range(U):
                        last = dve.tensor_scalar(z[:, u], z[:, u], ln[:, u, 0:1], ln[:, u, 3:4], ALU.subtract, ALU.mult)
                    chain(last)
                    chain(dve.tensor_tensor(z[:], z[:], both(gam), ALU.mult))
                    chain(dve.tensor_tensor(z[:], z[:], both(bet), ALU.add))
                    chain(dve.tensor_tensor(pair(R.x, i), pair(R.x, i), z[:], ALU.add))
                    chain(pair_stats(R, dve, i, chain))

            @block.scalar
            def _(act):
                act.wait_ge(s.ones_set, 1)
                with act.Fori(0, NB // U) as i:
                    for u, b, n in held(i):
                        act.wait_ge(s.xT_psum, n)
                        act.activation(xT[:, u], p_t[:, u, 0:P], ACT.Copy).then_inc(s.xT_ready, 1)
                    for u, b, n in held(i):
                        act.wait_ge(s.kv_psum, n)
                        act.activation(z[0:SC, u], p_m[0:SC, u, P:256], ACT.Square, accum_out=sums[0:SC, u, 1:2]).then_inc(s.squares_k, 1)
                        act.activation(kT[:, u], p_m[:, u, 384:384 + SC], ACT.Copy)
                        act.activation(va[0:SC, u, :, 0:HD], p_m[0:SC, u, 256:384].rearrange("p (h e) -> p h e", h=H),
                                       ACT.Copy).then_inc(s.kT_ready, 1)
                    for half in range(2):
                        for u, b, n in held(i):
                            act.wait_ge(s.scores_psum, i * (2 * U) + (half * U + u + 1))
                            act.activation(E[0:SC, u, 8 * half:8 * half + 8], p_s[0:SC, u], ACT.Exp,
                                           scale=kscale[0:SC, u:u + 1]).then_inc(s.exp_ready, 1)
                    for u, b, n in held(i):
                        act.wait_ge(s.headsT_psum, n)
                        act.activation(headsT[:, u], p_t[:, u, 256:384], ACT.Copy).then_inc(s.headsT_ready, 1)

            @block.tensor
            def _(pe):
                pe.wait_ge(s.w_in, 10 * DMA)
                with pe.Fori(0, NB // U) as i:
                    for u, b, n in held(i):
                        pe.wait_ge(s.xhat_ready, n)
                        pe.transpose(p_t[:, u, 0:P], xhat[:, u], R.ident[:]).then_inc(s.xT_psum, 1)
                    for u, b, n in held(i):
                        pe.wait_ge(s.ctx_ready, n)
                        pe.matmul(p_m[0:SC, u, P:384], cT[:, u], wkv[:], start=True, stop=True)
                        pe.matmul(p_m[:, u, 384:384 + SC], wkv[:, 0:P], cT[:, u], start=True, stop=True).then_inc(s.kv_psum, 1)
                        pe.wait_ge(s.xT_ready, n)
                        pe.matmul(p_t[:, u, 384:512], xT[:, u], wq[:], start=True, stop=True).then_inc(s.q_psum, 1)
                    for u, b, n in held(i):
                        pe.wait_ge(s.qn_ready, n)
                        pe.transpose(p_t[:, u, P:256], qn[:, u], R.ident[:]).then_inc(s.qnT_psum, 1)
                    for half in range(2):
                        for u, b, n in held(i):
                            if half == 0:
                                pe.wait_ge(s.qmask_ready, n)
                                pe.wait_ge(s.kT_ready, n)
                            else:
                                pe.wait_ge(s.exp_ready, i * (2 * U) + (u + 1))
                            for q in range(2):
                                h = 8 * half + 4 * q
                                mm = pe.matmul(p_s[0:SC, u, 4 * q:4 * q + 4], kT[:, u], qm[:, u, h:h + 4], start=True, stop=True)
                            mm.then_inc(s.scores_psum, 1)
                    for half in range(2):
                        for u, b, n in held(i):
                            pe.wait_ge(s.exp_ready, i * (2 * U) + (half * U + u + 1))
                            for h in range(8 * half, 8 * half + 8):
                                mm = pe.matmul(p_m[:, u, (HD + 1) * h:(HD + 1) * (h + 1)], E[0:SC, u, h], va[0:SC, u, h], start=True, stop=True)
                            if half == 1:
                                mm.then_inc(s.av_psum, 1)
                    for u, b, n in held(i):
                        pe.wait_ge(s.heads_ready, n)
                        pe.transpose(p_t[:, u, 256:384], heads[:, u], R.ident[:]).then_inc(s.headsT_psum, 1)
                    for u, b, n in held(i):
                        pe.wait_ge(s.headsT_ready, n)
                        pe.matmul(p_m[:, u, 256:384], headsT[:, u], wo[:], start=True, stop=True).then_inc(s.out_psum, 1)


PHASES.append(l0_xattn)
LAYOUTS.append(lambda a: {
    **{n: a[n] for n in ("L0_xattn_Wq", "L0_xattn_Wk", "L0_xattn_Wv", "L0_xattn_Wo")},
    **{n: a[n].reshape(1, -1) for n in ("L0_xattn_bk", "L0_xattn_bv")},
    **{n: repeated(a, n) for n in ("L0_xattn_bq", "L0_xattn_bo", "L0_xattn_ln_gamma", "L0_xattn_ln_beta")}})

def l0_ffn(nc, R, A):
    E = 8
    with phase(nc, "l0_ffn", FLIP + EXPERTS + "max_ready exps_ready") as (s, sb, ps):
        router = sb("router", [P, E])
        m1, m2, cw, tmp = sb("m1", [P, NB]), sb("m2", [P, NB]), sb("cw", [P, NB, E]), sb("tmp", [P, NB, E])
        X = experts_buffers(sb, ps, E, 4, P, ("L0_ffn_w_gate", "L0_ffn_w_up", "L0_ffn_w_down"), cw)
        T = flip_buffers(sb, ps, router, p_t=X.p_g, p_r=X.p_u)
        with nc.Block() as block:
            @block.sync
            def _(sp):
                load(sp, A, s.w_in, [(router, "L0_ffn_router_w")])
                experts_sync(sp, A, s, X)

            @block.gpsimd
            def _(pool):
                norm_pool(R, pool, s)

            @block.vector
            def _(dve):
                chain = Chain(dve, s.vchain)
                norm_vector(R, dve, s)
                flip_vector(R, dve, s, T)
                dve.wait_ge(s.logits_ready, NB // 4)
                wide = lambda t: t[:].unsqueeze(2).broadcast_to((P, NB, E))
                L = T.logits
                chain(dve.tensor_reduce(m1[:], L[:], AX.X, ALU.max))
                chain(dve.tensor_tensor(cw[:], L[:], wide(m1), ALU.is_equal))
                chain(dve.scalar_tensor_tensor(out=cw[:], in0=cw[:], scalar=-3e38, in1=L[:], op0=ALU.mult, op1=ALU.add))
                chain(dve.tensor_reduce(m2[:], cw[:], AX.X, ALU.max))
                dve.tensor_tensor(tmp[:], L[:], wide(m1), ALU.subtract).then_inc(s.max_ready, 1)
                chain(dve.tensor_tensor(cw[:], L[:], wide(m2), ALU.is_ge))
                dve.wait_ge(s.exps_ready, 1)
                chain(dve.tensor_tensor(cw[:], cw[:], tmp[:], ALU.mult))
                chain(dve.tensor_reduce(m1[:], cw[:], AX.X, ALU.add))
                chain(dve.reciprocal(m2[:], m1[:]))
                chain(dve.tensor_tensor(cw[:], cw[:], wide(m2), ALU.mult))
                experts_vector(R, dve, s, X)
                dve.wait_ge(s.out_added, E * NG + 2)
                all_row_stats(R, dve, chain)

            @block.scalar
            def _(act):
                flip_scalar(R, act, s, T)
                act.wait_ge(s.max_ready, 1)
                act.activation(tmp[:], tmp[:], ACT.Exp).then_inc(s.exps_ready, 1)
                experts_scalar(act, s, X)

            @block.tensor
            def _(pe):
                pe.wait_ge(s.w_in, DMA)
                flip_tensor(R, pe, s, T)
                pe.wait_ge(s.xT_ready, NB // 4)
                pe.wait_ge(s.logits_ready, NB // 4)
                experts_tensor(R, pe, s, X, T)


PHASES.append(l0_ffn)
LAYOUTS.append(lambda a: {
    "L0_ffn_router_w": transposed(a, "L0_ffn_router_w"), "L0_ffn_w_gate": a["L0_ffn_w_gate"], "L0_ffn_w_up": a["L0_ffn_w_up"],
    "L0_ffn_w_down": np.ascontiguousarray(a["L0_ffn_w_down"].reshape(8, 4, P, P).transpose(0, 2, 1, 3).reshape(8, P, 512))})

def l1_attn(nc, R, A):
    H, HD = 16, 8
    W = 2 * P
    USES = 3 * 2 * U
    with phase(nc, "l1_attn", "var_ready rstd_ready shift_ready w_in blocks_ready composed vchain xhat_ready xT_psum xT_ready slot_psum slot_read+2 "
                   "var1_ready std1_ready outer1_ready var2_ready std2_ready outer2_ready sums_ready mean_psum squares_ready sqmean_psum "
                   "gnvar_ready gnstd_ready ctx_ready ctxT_psum ctxT_ready out_psum") as (s, sb, ps):
        wproj, bproj = sb("wproj", [P, 5 * P]), sb("bproj", [P, 5 * P])
        wT, bqk, bwide = sb("wT", [P, W]), sb("bqk", [P, 2]), sb("bwide", [P, 2, P])
        wout, bd, bdm, bout, upper = (sb(n, [P, P]) for n in ("wout", "bd", "bdm", "bout", "upper"))
        g, lnb, gng, gnb = sb("g", [P, W]), sb("lnb", [P, P]), sb("gng", [P, W]), sb("gnb", [P, W])
        xhat, xT = sb("xhat", [P, U, 2, P]), sb("xT", [P, U, W])
        proj = sb("proj", [P, U, 5, 2, P])
        outer, part = sb("outer", [P, U, 2, P * HD]), sb("part", [P, 2, P * HD])
        step = sb("step", [P, U, W])
        n_, dn, t1, dz1, dz12 = (sb(x, [P, U, W]) for x in ("n", "dn", "t1", "dz1", "dz12"))
        st = sb("st", [P, U, 4, 2 * H])
        gs, cT = sb("gs", [P, U, 2 * H]), sb("cT", [P, U, W])
        p_s, p_m = ps("p_s", [P, 2, 2, 512]), ps("p_m", [P, U, 512])
        k_, minus_w, z, qw, q_ = ([proj[:, u, c].rearrange("p r t -> p (r t)") for u in range(U)] for c in (1, 2, 3, 4, 0))

        def heads(t):
            return t.rearrange("p (h e) -> p h e", e=HD)

        def wide(t):
            return t.unsqueeze(2).broadcast_to((P, 2 * H, HD))

        def over_rows(t):
            return heads(t).unsqueeze(3).broadcast_to((P, H, HD, HD))

        def over_columns(t):
            return heads(t).unsqueeze(2).broadcast_to((P, H, HD, HD))

        def square(t):
            return t.rearrange("p (h i j) -> p h i j", i=HD, j=HD)

        with nc.Block() as block:
            @block.sync
            def _(sp):
                load(sp, A, s.w_in, [(wT, "L1_attn_Wkq_T"), (bqk, "L1_attn_bkq"), (wout, "L1_attn_Wout"), (bd, "L1_attn_W0"),
                                     (bdm, "c_blocks8"), (bout, "L1_attn_bout"), (upper, "c_upper"),
                                     (g, "L1_attn_ln_g"), (lnb, "L1_attn_ln_b"), (gng, "L1_attn_gn_g"), (gnb, "L1_attn_gn_b")])
                sp.dma_start(wproj[:, 0:3 * P], A["L1_attn_Wproj"]).then_inc(s.w_in, DMA)
                sp.dma_start(bproj[:, 0:3 * P], A["L1_attn_bproj"]).then_inc(s.w_in, DMA)

            @block.gpsimd
            def _(pool):
                norm_pool(R, pool, s)

            @block.vector
            def _(dve):
                chain = Chain(dve, s.vchain)
                norm_vector(R, dve, s)
                dve.wait_ge(s.w_in, 13 * DMA)
                dve.tensor_copy(bwide[:], bqk[:].unsqueeze(2).broadcast_to((P, 2, P)))
                dve.tensor_tensor(bd[:], bd[:], bdm[:], ALU.mult).then_inc(s.blocks_ready, 1)
                dve.tensor_tensor(bproj[:, W:3 * P], bproj[:, W:3 * P], lnb[:], ALU.subtract)
                dve.wait_ge(s.composed, 1)
                chain(dve.tensor_copy(wproj[:, 3 * P:5 * P], p_m[:, 0, 0:W]))
                chain(dve.tensor_copy(bproj[:, 3 * P:5 * P], p_m[:, 0, W:2 * W]))

                def centred(u, var_ready):
                    chain(dve.tensor_reduce(st[:, u, 0], heads(z[u]), AX.X, ALU.add))
                    chain(dve.tensor_scalar(st[:, u, 0], st[:, u, 0], 1.0 / HD, None, ALU.mult))
                    chain(dve.tensor_tensor(heads(n_[:, u]), heads(z[u]), wide(st[:, u, 0]), ALU.subtract))
                    chain(dve.tensor_tensor(t1[:, u], n_[:, u], n_[:, u], ALU.mult))
                    chain(dve.tensor_reduce(st[:, u, 1], heads(t1[:, u]), AX.X, ALU.add))
                    dve.tensor_scalar(st[:, u, 1], st[:, u, 1], 1.0 / HD, EPS, ALU.mult, ALU.add).then_inc(var_ready, 1)

                def gradient(u):
                    n, d, t, m = n_[:, u], dn[:, u], t1[:, u], st[:, u]
                    chain(dve.reciprocal(m[:, 1], m[:, 1]))
                    chain(dve.tensor_tensor(heads(n), heads(n), wide(m[:, 1]), ALU.mult))
                    chain(dve.tensor_tensor(d, n, g[:], ALU.mult))
                    chain(dve.tensor_tensor(d, d, minus_w[u], ALU.subtract))
                    chain(dve.tensor_tensor(d, d, g[:], ALU.mult))
                    chain(dve.tensor_tensor(t, d, n, ALU.mult))
                    dve.tensor_reduce(m[:, 2], heads(d), AX.X, ALU.add)
                    chain(dve.tensor_reduce(m[:, 3], heads(t), AX.X, ALU.add))
                    chain(dve.tensor_scalar(m[:, 2:4], m[:, 2:4], 1.0 / HD, None, ALU.mult))
                    dve.tensor_tensor(heads(d), heads(d), wide(m[:, 2]), ALU.subtract)
                    chain(dve.tensor_tensor(heads(n), heads(n), wide(m[:, 3]), ALU.mult))
                    chain(dve.tensor_tensor(d, d, n, ALU.subtract))

                def outer_products(u, dz, ready):
                    for r in range(2):
                        dve.tensor_tensor(square(outer[:, u, r]), over_rows(k_[u][:, r * P:(r + 1) * P]),
                                          over_columns(dz[:, u, r * P:(r + 1) * P]), ALU.mult).then_inc(ready, 1)

                def applied(i, use, u, x):
                    for r in range(2):
                        dve.wait_ge(s.slot_psum, i * USES + (use + r + 1))
                        dve.tensor_tensor(square(part[:, r]), square(p_s[:, r].rearrange("p a n -> p (a n)")),
                                          over_rows(x[u][:, r * P:(r + 1) * P]), ALU.mult).then_inc(s.slot_read, 1)
                    dve.wait_ge(s.slot_read, i * USES + (use + 4))
                    chain(dve.tensor_reduce(step[:, u].rearrange("p (h j) -> p h j", j=HD),
                                            part[:].rearrange("p r (h i j) -> p (r h) j i", i=HD, j=HD), AX.X, ALU.add))

                with dve.Fori(0, NB // 2 // U) as i:
                    chain.restart()
                    for u, b, n in held(i):
                        pair_normalised(R, dve, b, xhat[:, u]).then_inc(s.xhat_ready, 1)
                    for u, b, n in held(i):
                        for r in range(2):
                            dve.wait_ge(s.slot_psum, i * USES + (2 * u + r + 1))
                            dve.tensor_tensor(proj[:, u, 0:3, r], p_s[:, r, 0, 0:3 * P].rearrange("p (c n) -> p c n", n=P),
                                              bproj[:, 0:3 * P].rearrange("p (c n) -> p c n", n=P), ALU.add)
                            dve.tensor_tensor(proj[:, u, 3:5, r], p_s[:, r, 1, 0:W].rearrange("p (c n) -> p c n", n=P),
                                              bproj[:, 3 * P:5 * P].rearrange("p (c n) -> p c n", n=P), ALU.add).then_inc(s.slot_read, 1)
                        dve.wait_ge(s.slot_read, i * USES + (2 * u + 4))
                        centred(u, s.var1_ready)
                    for u, b, n in held(i):
                        dve.wait_ge(s.std1_ready, n)
                        gradient(u)
                        chain(dve.tensor_tensor(heads(dz1[:, u]), heads(dn[:, u]), wide(st[:, u, 1]), ALU.mult))
                        outer_products(u, dz1, s.outer1_ready)
                    for u, b, n in held(i):
                        applied(i, 2 * U + 2 * u, u, k_)
                        chain(dve.tensor_tensor(z[u], z[u], step[:, u], ALU.subtract))
                        centred(u, s.var2_ready)
                    for u, b, n in held(i):
                        dve.wait_ge(s.std2_ready, n)
                        gradient(u)
                        chain(dve.tensor_tensor(heads(dn[:, u]), heads(dn[:, u]), wide(st[:, u, 1]), ALU.mult))
                        chain(dve.tensor_tensor(dz12[:, u], dn[:, u], dz1[:, u], ALU.add))
                        outer_products(u, dz12, s.outer2_ready)
                    for u, b, n in held(i):
                        applied(i, 4 * U + 2 * u, u, q_)
                        chain(dve.tensor_tensor(qw[u], qw[u], step[:, u], ALU.subtract))
                        dve.tensor_reduce(gs[:, u], heads(qw[u]), AX.X, ALU.add).then_inc(s.sums_ready, 1)
                    for u, b, n in held(i):
                        dve.wait_ge(s.mean_psum, n)
                        chain(dve.tensor_scalar(st[:, u, 0], p_m[:, u, 0:2 * H], 1.0 / (HD * S), None, ALU.mult))
                        chain(dve.tensor_tensor(heads(qw[u]), heads(qw[u]), wide(st[:, u, 0]), ALU.subtract))
                        chain(dve.tensor_tensor(t1[:, u], qw[u], qw[u], ALU.mult))
                        dve.tensor_reduce(gs[:, u], heads(t1[:, u]), AX.X, ALU.add).then_inc(s.squares_ready, 1)
                    for u, b, n in held(i):
                        dve.wait_ge(s.sqmean_psum, n)
                        dve.tensor_scalar(st[:, u, 1], p_m[:, u, 0:2 * H], 1.0 / (HD * S), EPS, ALU.mult, ALU.add).then_inc(s.gnvar_ready, 1)
                    for u, b, n in held(i):
                        dve.wait_ge(s.gnstd_ready, n)
                        chain(dve.reciprocal(st[:, u, 1], st[:, u, 1]))
                        chain(dve.tensor_tensor(heads(qw[u]), heads(qw[u]), wide(st[:, u, 1]), ALU.mult))
                        chain(dve.tensor_tensor(qw[u], qw[u], gng[:], ALU.mult))
                        dve.tensor_tensor(qw[u], qw[u], gnb[:], ALU.add).then_inc(s.ctx_ready, 1)
                        chain(dve.tensor_tensor(pair(R.x, b), pair(R.x, b), bout[:].unsqueeze(1).broadcast_to((P, 2, P)), ALU.add))
                    for u, b, n in held(i):
                        dve.wait_ge(s.out_psum, n)
                        chain(dve.tensor_tensor(pair(R.x, b), pair(R.x, b), side(p_m[:, u, 0:W]), ALU.add))
                        chain(pair_stats(R, dve, b, chain))

            @block.scalar
            def _(act):
                with act.Fori(0, NB // 2 // U) as i:
                    for u, b, n in held(i):
                        act.wait_ge(s.xT_psum, n)
                        act.activation(xT[:, u], p_m[:, u, 0:W], ACT.Copy).then_inc(s.xT_ready, 1)
                    for ready, done in ((s.var1_ready, s.std1_ready), (s.var2_ready, s.std2_ready), (s.gnvar_ready, s.gnstd_ready)):
                        for u, b, n in held(i):
                            act.wait_ge(ready, n)
                            act.activation(st[:, u, 1], st[:, u, 1], ACT.Sqrt).then_inc(done, 1)
                    for u, b, n in held(i):
                        act.wait_ge(s.ctxT_psum, n)
                        act.activation(cT[:, u], p_m[:, u, W:2 * W], ACT.Copy).then_inc(s.ctxT_ready, 1)

            @block.tensor
            def _(pe):
                def states(i, use, ready, count):
                    u = use // 2 % U
                    for r in range(2):
                        pe.wait_ge(ready, count + r)
                        pe.wait_ge(s.slot_read, i * USES + (use + r + 1))
                        for a in range(2):
                            mm = pe.matmul(p_s[:, r, a], upper[:], outer[:, u, r, a * 512:(a + 1) * 512], start=True, stop=True)
                        mm.then_inc(s.slot_psum, 1)

                pe.wait_ge(s.w_in, 13 * DMA)
                pe.wait_ge(s.blocks_ready, 1)
                for c in range(2):
                    pe.matmul(p_m[:, 0, c * P:(c + 1) * P], wT[:, c * P:(c + 1) * P], bd[:], start=True, stop=True)
                    mm = pe.matmul(p_m[:, 0, W + c * P:W + (c + 1) * P], bwide[:, c], bd[:], start=True, stop=True)
                mm.then_inc(s.composed, 1)
                with pe.Fori(0, NB // 2 // U) as i:
                    for u, b, n in held(i):
                        pe.wait_ge(s.xhat_ready, n)
                        for r in range(2):
                            mm = pe.transpose(p_m[:, u, r * P:(r + 1) * P], xhat[:, u, r], R.ident[:])
                        mm.then_inc(s.xT_psum, 1)
                    for u, b, n in held(i):
                        pe.wait_ge(s.xT_ready, n)
                        for r in range(2):
                            pe.wait_ge(s.slot_read, i * USES + (2 * u + r + 1))
                            pe.matmul(p_s[:, r, 0, 0:3 * P], xT[:, u, r * P:(r + 1) * P], wproj[:, 0:3 * P], start=True, stop=True)
                            pe.matmul(p_s[:, r, 1, 0:W], xT[:, u, r * P:(r + 1) * P], wproj[:, 3 * P:5 * P], start=True, stop=True
                                      ).then_inc(s.slot_psum, 1)
                    for u, b, n in held(i):
                        states(i, 2 * U + 2 * u, s.outer1_ready, i * (2 * U) + (2 * u + 1))
                    for u, b, n in held(i):
                        states(i, 4 * U + 2 * u, s.outer2_ready, i * (2 * U) + (2 * u + 1))
                    for ready, done in ((s.sums_ready, s.mean_psum), (s.squares_ready, s.sqmean_psum)):
                        for u, b, n in held(i):
                            pe.wait_ge(ready, n)
                            pe.matmul(p_m[:, u, 0:2 * H], R.ones[:], gs[:, u], start=True, stop=True).then_inc(done, 1)
                    for u, b, n in held(i):
                        pe.wait_ge(s.ctx_ready, n)
                        for r in range(2):
                            mm = pe.transpose(p_m[:, u, W + r * P:W + (r + 1) * P], qw[u][:, r * P:(r + 1) * P], R.ident[:])
                        mm.then_inc(s.ctxT_psum, 1)
                    for u, b, n in held(i):
                        pe.wait_ge(s.ctxT_ready, n)
                        for r in range(2):
                            mm = pe.matmul(p_m[:, u, r * P:(r + 1) * P], cT[:, u, r * P:(r + 1) * P], wout[:], start=True, stop=True)
                        mm.then_inc(s.out_psum, 1)


PHASES.append(l1_attn)


def layout_l1_attn(a):
    tiled = lambda v, n: np.ascontiguousarray(np.broadcast_to(np.tile(v, n)[None, :], (P, v.size * n)))
    W, b = a["L1_attn_Wproj"], a["L1_attn_bproj"]
    eighths = np.arange(P) // 8
    return {
        "L1_attn_Wproj": W, "L1_attn_bproj": repeated(a, "L1_attn_bproj"),
        "L1_attn_Wkq_T": np.ascontiguousarray(np.concatenate([W[:, P:2 * P].T, W[:, 0:P].T], 1)),
        "L1_attn_bkq": np.ascontiguousarray(np.stack([b[P:2 * P], b[0:P]], 1)),
        "L1_attn_W0": np.ascontiguousarray(np.tile(a["L1_attn_W0"], (16, 16))), "L1_attn_Wout": a["L1_attn_Wout"],
        "L1_attn_bout": repeated(a, "L1_attn_bout"), "c_upper": (np.arange(P)[None, :] >= np.arange(P)[:, None]).astype(np.float32),
        "c_blocks8": (eighths[:, None] == eighths[None, :]).astype(np.float32),
        "L1_attn_ln_g": tiled(a["L1_attn_ln_g"], 32), "L1_attn_ln_b": tiled(a["L1_attn_ln_b"], 16),
        "L1_attn_gn_g": tiled(a["L1_attn_gn_g"], 2), "L1_attn_gn_b": tiled(a["L1_attn_gn_b"], 2)}


LAYOUTS.append(layout_l1_attn)
def l1_xattn(nc, R, A):
    H, HD, K = 2, 64, P + SC
    with phase(nc, "l1_xattn", "var_ready rstd_ready shift_ready w_in set_ready gammas_ready vchain var2_ready rstd2_ready z_ready zT_psum zT_ready qkv_psum "
                   "qkv_ready ssq_ready rms_ready qkn_ready qkT_psum qkT_ready scores_psum max_ready exp_ready eT_psum eT_ready "
                   "av_psum heads_ready headsT_psum headsT_ready out_psum") as (s, sb, ps):
        wl, wc, wo, bo = sb("wl", [P, 3 * P]), sb("wc", [DC, 2 * P]), sb("wo", [P, P]), sb("bo", [P, P])
        gl, bl, gc, bc = sb("gl", [P, 1]), sb("bl", [P, 1]), sb("gc", [DC, 1]), sb("bc", [DC, 1])
        gq, gk, halves = sb("gq", [P, 2]), sb("gk", [P, 2]), sb("halves", [P, 2])
        ctxt, m4, mneg = sb("ctxt", [SC, NB, DC]), sb("m4", [1, NB, SC // 4], U32), sb("mneg", [1, NB, SC])
        z, zc, st, bn = sb("z", [P, U, P]), sb("zc", [SC, U, DC]), sb("st", [P, U, 2, 2]), sb("bn12", [P, U, 2, 6])
        rs = sb("rs", [P, U, 2])
        lT, cT = sb("lT", [P, U, P]), sb("cT", [DC, U, SC])
        qk, kc, sq = sb("qk", [P, U, 2 * P]), sb("kc", [SC, U, P]), sb("sq", [P, U, 3 * P])
        ssq, vl, vc = sb("ssq", [P, U, 6]), sb("vl", [P, U, H, HD + 1]), sb("vc", [SC, U, H, HD + 1])
        qT, kT = sb("qT", [P, U, H, P]), sb("kT", [P, U, K])
        nm, E, eT = sb("nm", [P, U, H]), sb("E", [P, U, H, K]), sb("eT", [P, U, 4, P])
        rden, heads, headsT = sb("rden", [P, U, H]), sb("heads", [P, U, P]), sb("headsT", [P, U, P])
        p_t, p_q, p_k, p_o = ps("p_t", [P, U, 512]), ps("p_q", [P, U, 512]), ps("p_k", [P, U, 512]), ps("p_o", [P, U, 512])
        with nc.Block() as block:
            @block.sync
            def _(sp):
                load(sp, A, s.w_in, [(wl, "L1_xattn_Wl"), (wc, "L1_xattn_Wkv"), (wo, "L1_xattn_Wo"), (bo, "L1_xattn_bo"),
                                     (gl, "L1_xattn_ln_l_g"), (bl, "L1_xattn_ln_l_b"), (gc, "L1_xattn_ln_x_g"), (bc, "L1_xattn_ln_x_b"),
                                     (gq, "L1_xattn_qn_g"), (gk, "L1_xattn_kn_g"), (ctxt, "ctx_tokens"), (m4, "mask_BxS2_bk0"),
                                     (halves, "c_halves")])

            @block.gpsimd
            def _(pool):
                norm_pool(R, pool, s)
                with pool.Fori(0, NB // U) as i:
                    for u, b, n in held(i):
                        pool.wait_ge(s.var2_ready, n)
                        pool.tensor_tensor(rs[:, u], rs[:, u], R.minus_half[:, 0:2], ALU.pow).then_inc(s.rstd2_ready, 1)
                    for u, b, n in held(i):
                        pool.wait_ge(s.ssq_ready, n)
                        pool.tensor_tensor(ssq[:, u], ssq[:, u], R.minus_half[:, 0:6], ALU.pow).then_inc(s.rms_ready, 1)

            @block.vector
            def _(dve):
                chain = Chain(dve, s.vchain)
                norm_vector(R, dve, s)
                dve.memset(vl[:, :, :, HD:HD + 1], 1.0)
                dve.memset(ssq[:], 1.0)
                dve.memset(rs[:], 1.0)
                dve.memset(st[:], 1.0)
                dve.memset(vc[:, :, :, HD:HD + 1], 1.0).then_inc(s.set_ready, 1)
                dve.wait_ge(s.set_ready, 1)
                dve.wait_ge(s.w_in, 13 * DMA)
                chain(dve.tensor_scalar(mneg[:], m4[:].bitcast(U8), 1.0, 1e30, ALU.subtract, ALU.mult))
                chain(dve.scalar_tensor_tensor(out=gq[:], in0=gq[:], scalar=HD ** -0.5, in1=gk[:], op0=ALU.mult, op1=ALU.mult))
                dve.tensor_tensor(gq[:], gq[:], halves[:], ALU.mult).then_inc(s.gammas_ready, 1)
                with dve.Fori(0, NB // U) as i:
                    chain.restart()
                    for u, b, n in held(i):
                        chain(normalised(R, dve, b, z[:, u]))
                        dve.bn_stats(bn[:, u, 0], z[:, u])
                        chain(dve.bn_stats(bn[0:SC, u, 1], row(ctxt, b)))
                        dve.bn_aggr(st[:, u, 0], bn[:, u, 0])
                        chain(dve.bn_aggr(st[0:SC, u, 1], bn[0:SC, u, 1]))
                        dve.tensor_scalar(rs[:, u], st[:, u, :, 1], EPS, None, ALU.add).then_inc(s.var2_ready, 1)
                    for u, b, n in held(i):
                        dve.wait_ge(s.rstd2_ready, n)
                        dve.tensor_scalar(z[:, u], z[:, u], st[:, u, 0, 0:1], rs[:, u, 0:1], ALU.subtract, ALU.mult)
                        dve.tensor_scalar(zc[:, u], row(ctxt, b), st[0:SC, u, 1, 0:1], rs[0:SC, u, 1:2], ALU.subtract,
                                          ALU.mult).then_inc(s.z_ready, 1)
                    for u, b, n in held(i):
                        dve.wait_ge(s.qkv_ready, n)
                        dve.tensor_tensor(sq[:, u, 0:2 * P], qk[:, u], qk[:, u], ALU.mult)
                        chain(dve.tensor_tensor(sq[0:SC, u, 2 * P:], kc[:, u], kc[:, u], ALU.mult))
                        dve.tensor_reduce(ssq[:, u, 0:4], sq[:, u, 0:2 * P].rearrange("p (h e) -> p h e", e=HD), AX.X, ALU.add)
                        chain(dve.tensor_reduce(ssq[0:SC, u, 4:6], sq[0:SC, u, 2 * P:].rearrange("p (h e) -> p h e", e=HD), AX.X, ALU.add))
                        dve.tensor_scalar(ssq[:, u], ssq[:, u], 1.0 / HD, 1e-16, ALU.mult, ALU.max).then_inc(s.ssq_ready, 1)
                    for u, b, n in held(i):
                        dve.wait_ge(s.rms_ready, n)
                        v = qk[:, u].rearrange("p (h e) -> p h e", e=HD)
                        dve.tensor_tensor(v, v, ssq[:, u, 0:4].unsqueeze(2).broadcast_to((P, 4, HD)), ALU.mult)
                        v = kc[:, u].rearrange("p (h e) -> p h e", e=HD)
                        dve.tensor_tensor(v, v, ssq[0:SC, u, 4:6].unsqueeze(2).broadcast_to((SC, 2, HD)), ALU.mult).then_inc(s.qkn_ready, 1)
                    for u, b, n in held(i):
                        dve.wait_ge(s.scores_psum, n)
                        dve.tensor_reduce(nm[:, u], p_k[:, u, 0:H * K].rearrange("p (h k) -> p h k", h=H), AX.X, ALU.max,
                                          negate=True).then_inc(s.max_ready, 1)
                    for u, b, n in held(i):
                        dve.wait_ge(s.eT_psum, n)
                        dve.tensor_copy(eT[:, u, 0:2], p_q[:, u, 0:256].rearrange("p (h t) -> p h t", h=H))
                        dve.tensor_copy(eT[0:SC, u, 2:4], p_q[0:SC, u, 256:512].rearrange("p (h t) -> p h t", h=H)).then_inc(s.eT_ready, 1)
                    for u, b, n in held(i):
                        dve.wait_ge(s.av_psum, n)
                        av = p_o[:, u, 0:H * (HD + 1)].rearrange("p (h e) -> p h e", h=H)
                        chain(dve.reciprocal(rden[:, u], av[:, :, HD]))
                        dve.tensor_tensor(heads[:, u].rearrange("p (h e) -> p h e", h=H), av[:, :, 0:HD],
                                          rden[:, u].unsqueeze(2).broadcast_to((P, H, HD)), ALU.mult).then_inc(s.heads_ready, 1)
                    chain(dve.tensor_tensor(pair(R.x, i), pair(R.x, i), both(bo), ALU.add))
                    dve.wait_ge(s.out_psum, (i + 1) * U)
                    chain(dve.tensor_tensor(pair(R.x, i), pair(R.x, i), p_o[:, :, 256:384], ALU.add))
                    chain(pair_stats(R, dve, i, chain))

            @block.scalar
            def _(act):
                act.wait_ge(s.w_in, 13 * DMA)
                act.wait_ge(s.gammas_ready, 1)
                with act.Fori(0, NB // U) as i:
                    for u, b, n in held(i):
                        act.wait_ge(s.zT_psum, n)
                        act.activation(lT[:, u], p_t[:, u, 0:P], ACT.Identity, scale=gl[:], bias=bl[:])
                        act.activation(cT[:, u], p_t[0:DC, u, P:P + SC], ACT.Identity, scale=gc[:], bias=bc[:]).then_inc(s.zT_ready, 1)
                    for u, b, n in held(i):
                        act.wait_ge(s.qkv_psum, n)
                        act.activation(qk[:, u], p_q[:, u, 0:2 * P], ACT.Copy)
                        act.activation(kc[:, u], p_k[0:SC, u, 0:P], ACT.Copy)
                        act.activation(vl[:, u, :, 0:HD], p_q[:, u, 2 * P:3 * P].rearrange("p (h e) -> p h e", h=H), ACT.Copy)
                        act.activation(vc[:, u, :, 0:HD], p_k[0:SC, u, P:2 * P].rearrange("p (h e) -> p h e", h=H), ACT.Copy
                                       ).then_inc(s.qkv_ready, 1)
                    for u, b, n in held(i):
                        act.wait_ge(s.qkT_psum, n)
                        for h in range(H):
                            act.activation(qT[:, u, h], p_t[:, u, 0:P], ACT.Copy, scale=gq[:, h:h + 1])
                        act.activation(kT[:, u], p_t[:, u, P:P + K], ACT.Copy).then_inc(s.qkT_ready, 1)
                    for u, b, n in held(i):
                        act.wait_ge(s.max_ready, n)
                        for h in range(H):
                            e = act.activation(E[:, u, h], p_k[:, u, h * K:(h + 1) * K], ACT.Exp, bias=nm[:, u, h:h + 1])
                        e.then_inc(s.exp_ready, 1)
                    for u, b, n in held(i):
                        act.wait_ge(s.headsT_psum, n)
                        act.activation(headsT[:, u], p_t[:, u, 0:P], ACT.Copy).then_inc(s.headsT_ready, 1)

            @block.tensor
            def _(pe):
                pe.wait_ge(s.w_in, 13 * DMA)
                with pe.Fori(0, NB // U) as i:
                    for u, b, n in held(i):
                        pe.wait_ge(s.z_ready, n)
                        pe.transpose(p_t[:, u, 0:P], z[:, u], R.ident[:])
                        pe.transpose(p_t[0:DC, u, P:P + SC], zc[:, u], R.ident[0:SC, 0:SC]).then_inc(s.zT_psum, 1)
                    for u, b, n in held(i):
                        pe.wait_ge(s.zT_ready, n)
                        pe.matmul(p_k[0:SC, u, 0:2 * P], cT[:, u], wc[:], start=True, stop=True)
                        pe.matmul(p_q[:, u, 0:3 * P], lT[:, u], wl[:], start=True, stop=True).then_inc(s.qkv_psum, 1)
                    for u, b, n in held(i):
                        pe.wait_ge(s.qkn_ready, n)
                        pe.transpose(p_t[:, u, 0:P], qk[:, u, 0:P], R.ident[:])
                        pe.transpose(p_t[:, u, P:2 * P], qk[:, u, P:2 * P], R.ident[:])
                        pe.transpose(p_t[:, u, 2 * P:2 * P + SC], kc[:, u], R.ident[0:SC, 0:SC]).then_inc(s.qkT_psum, 1)
                    for u, b, n in held(i):
                        pe.wait_ge(s.qkT_ready, n)
                        for h in range(H):
                            pe.matmul(p_k[:, u, h * K:(h + 1) * K], qT[:, u, h], kT[:, u], start=True, stop=False, skip_group_check=True)
                            mm = pe.matmul(p_k[:, u, h * K + P:(h + 1) * K], R.ones[0:1, :], row(mneg, b), start=False, stop=True,
                                           skip_group_check=True)
                        mm.then_inc(s.scores_psum, 1)
                    for u, b, n in held(i):
                        pe.wait_ge(s.exp_ready, n)
                        for h in range(H):
                            pe.transpose(p_q[:, u, h * P:(h + 1) * P], E[:, u, h, 0:P], R.ident[:])
                            mm = pe.transpose(p_q[0:SC, u, (2 + h) * P:(3 + h) * P], E[:, u, h, P:K], R.ident[:])
                        mm.then_inc(s.eT_psum, 1)
                    for u, b, n in held(i):
                        pe.wait_ge(s.eT_ready, n)
                        for h in range(H):
                            o = p_o[:, u, h * (HD + 1):(h + 1) * (HD + 1)]
                            pe.matmul(o, eT[:, u, h], vl[:, u, h], start=True, stop=False)
                            mm = pe.matmul(o, eT[0:SC, u, 2 + h], vc[:, u, h], start=False, stop=True)
                        mm.then_inc(s.av_psum, 1)
                    for u, b, n in held(i):
                        pe.wait_ge(s.heads_ready, n)
                        pe.transpose(p_t[:, u, 0:P], heads[:, u], R.ident[:]).then_inc(s.headsT_psum, 1)
                    for u, b, n in held(i):
                        pe.wait_ge(s.headsT_ready, n)
                        pe.matmul(p_o[:, u, 256:384], headsT[:, u], wo[:], start=True, stop=True).then_inc(s.out_psum, 1)


PHASES.append(l1_xattn)


def layout_l1_xattn(a):
    return {
        "L1_xattn_Wl": np.ascontiguousarray(np.concatenate([a["L1_xattn_Wq"], a["L1_xattn_Wlkv"]], 0).T),
        "L1_xattn_Wkv": transposed(a, "L1_xattn_Wkv"), "L1_xattn_Wo": transposed(a, "L1_xattn_Wo"), "L1_xattn_bo": repeated(a, "L1_xattn_bo"),
        **{n: column(a, n) for n in ("L1_xattn_ln_l_g", "L1_xattn_ln_l_b", "L1_xattn_ln_x_g", "L1_xattn_ln_x_b")},
        "c_halves": (np.arange(P)[:, None] // 64 == np.arange(2)[None, :]).astype(np.float32),
        **{n: np.ascontiguousarray(np.broadcast_to(np.tile(a[n], 2).reshape(P, 1), (P, 2))) for n in ("L1_xattn_qn_g", "L1_xattn_kn_g")},
        "ctx_tokens": transposed(a, "ctx_768", 1, 0, 2), "mask_BxS2_bk0": a["mask_BxS2_bk0"].view(np.uint32).reshape(1, NB, SC // 4)}


LAYOUTS.append(layout_l1_xattn)

SSM = "ssm_in dt_ready half_ready small_args small_trig args_ready trig_ready padded rows_out "
SSM_N, LAGS, COARSE = 64, 16, S // 16
SSM_NAMES = ("log_dt", "D_skip", "A_re", "A_im", "C_re", "C_im")


def ssm_buffers(sb):
    M, NS, N = Named(), SSM_N, LAGS + COARSE
    M.logdt, M.skip, M.are, M.aim, M.cre, M.cim = (sb(f"ssm_{n}", [P, 1 if n in ("log_dt", "D_skip") else NS]) for n in SSM_NAMES)
    M.times, M.dt, M.quarter, M.kpad = sb("times", [P, N]), sb("dt", [P, 1]), sb("quarter", [P, 1]), sb("kpad", [P, 2 * S])
    M.re, M.im, M.er, M.ei, M.q, M.t1, M.t2 = (sb(f"t_{n}", [P, NS]) for n in ("re", "im", "er", "ei", "q", "t1", "t2"))
    M.wre, M.wim = sb("wre", [P, NS]), sb("wim", [P, NS])
    M.env, M.arg, M.turns, M.cosine = (sb(n, [P, N, NS]) for n in ("env", "arg", "turns", "cosine"))
    M.fine, M.coarse = sb("fine", [P, LAGS, 2, NS]), sb("coarse", [P, COARSE, 2, NS])
    M.terms, M.sums = sb("terms", [P, LAGS, 2 * NS]), sb("sums", [P, LAGS])
    return M


def ssm_sync(sp, A, s, M):
    load(sp, A, s.ssm_in, [(t, f"L2_xattn_{n}") for t, n in zip((M.logdt, M.skip, M.are, M.aim, M.cre, M.cim), SSM_NAMES)]
         + [(M.times, "c_lags")])


def ssm_tables(dve, chain, s, M):
    NS, N = SSM_N, LAGS + COARSE
    re, im, er, ei, q, t1, t2, wre, wim = M.re, M.im, M.er, M.ei, M.q, M.t1, M.t2, M.wre, M.wim
    tt = lambda o, a, b, op: chain(dve.tensor_tensor(o, a, b, op))
    dve.wait_ge(s.ssm_in, 7 * DMA)
    chain(dve.memset(M.kpad[:], 0.0))
    dve.memset(M.quarter[:], float(np.pi / 2)).then_inc(s.half_ready, 1)
    dve.wait_ge(s.dt_ready, 1)
    chain(dve.tensor_scalar(re[:], M.are[:], M.dt[:], None, ALU.mult))
    chain(dve.tensor_scalar(im[:], M.aim[:], M.dt[:], None, ALU.mult))
    chain(dve.tensor_copy(ei[:], im[:]))
    turns_removed(dve, chain, ei[:], t1[:])
    dve.scalar_tensor_tensor(out=q[:], in0=ei[:], scalar=-1.0, in1=ei[:], op0=ALU.mult, op1=ALU.max).then_inc(s.small_args, 1)
    over = lambda t, n: t[:].unsqueeze(1).broadcast_to((P, n, NS))
    lags = M.times[:].unsqueeze(2).broadcast_to((P, N, NS))
    tt(M.env[:], over(re, N), lags, ALU.mult)
    tt(M.arg[:], over(im, N), lags, ALU.mult)
    turns_removed(dve, chain, M.arg[:], M.turns[:])
    dve.scalar_tensor_tensor(out=M.cosine[:], in0=M.arg[:], scalar=-1.0, in1=M.arg[:], op0=ALU.mult, op1=ALU.max).then_inc(s.args_ready, 1)
    dve.wait_ge(s.small_trig, 1)
    tt(er[:], t1[:], q[:], ALU.mult)
    tt(ei[:], t1[:], ei[:], ALU.mult)
    chain(dve.tensor_scalar(er[:], er[:], 1.0, None, ALU.subtract))
    tt(t1[:], M.cre[:], er[:], ALU.mult)
    tt(t2[:], M.cim[:], ei[:], ALU.mult)
    tt(wre[:], t1[:], t2[:], ALU.subtract)
    tt(t1[:], M.cre[:], ei[:], ALU.mult)
    tt(t2[:], M.cim[:], er[:], ALU.mult)
    tt(wim[:], t1[:], t2[:], ALU.add)
    tt(t1[:], M.are[:], M.are[:], ALU.mult)
    tt(t2[:], M.aim[:], M.aim[:], ALU.mult)
    tt(t1[:], t1[:], t2[:], ALU.add)
    chain(dve.reciprocal(q[:], t1[:]))
    tt(t1[:], wre[:], M.are[:], ALU.mult)
    tt(t2[:], wim[:], M.aim[:], ALU.mult)
    tt(er[:], t1[:], t2[:], ALU.add)
    tt(t1[:], wim[:], M.are[:], ALU.mult)
    tt(t2[:], wre[:], M.aim[:], ALU.mult)
    tt(ei[:], t1[:], t2[:], ALU.subtract)
    chain(dve.scalar_tensor_tensor(out=wre[:], in0=er[:], scalar=2.0, in1=q[:], op0=ALU.mult, op1=ALU.mult))
    chain(dve.scalar_tensor_tensor(out=wim[:], in0=ei[:], scalar=2.0, in1=q[:], op0=ALU.mult, op1=ALU.mult))
    dve.wait_ge(s.trig_ready, 1)
    tt(M.cosine[:], M.cosine[:], M.env[:], ALU.mult)
    tt(M.arg[:], M.arg[:], M.env[:], ALU.mult)
    chain(dve.tensor_copy(M.fine[:, :, 0], M.cosine[:, 0:LAGS]))
    chain(dve.tensor_copy(M.fine[:, :, 1], M.arg[:, 0:LAGS]))
    cos, sin, u, v = M.cosine[:, LAGS:N], M.arg[:, LAGS:N], M.turns[:, 0:COARSE], M.env[:, 0:COARSE]
    tt(u, cos, over(wre, COARSE), ALU.mult)
    tt(v, sin, over(wim, COARSE), ALU.mult)
    tt(M.coarse[:, :, 0], u, v, ALU.subtract)
    tt(u, cos, over(wim, COARSE), ALU.mult)
    tt(v, sin, over(wre, COARSE), ALU.mult)
    tt(u, u, v, ALU.add)
    chain(dve.tensor_scalar(M.coarse[:, :, 1], u, -1.0, None, ALU.mult))


def ssm_lags(dve, chain, M, i):
    power = M.coarse[:, bass.ds(i, 1)].rearrange("p a c n -> p a (c n)").broadcast_to((P, LAGS, 2 * SSM_N))
    chain(dve.tensor_tensor(M.terms[:], M.fine[:].rearrange("p l c n -> p l (c n)"), power, ALU.mult))
    chain(dve.tensor_reduce(M.sums[:], M.terms[:], AX.X, ALU.add))
    chain(dve.tensor_copy(M.kpad[:, bass.ds(i * LAGS + (S - 1), LAGS)], M.sums[:]))


def ssm_scalar(act, s, M):
    act.wait_ge(s.ssm_in, 7 * DMA)
    act.activation(M.dt[:], M.logdt[:], ACT.Exp).then_inc(s.dt_ready, 1)
    act.wait_ge(s.small_args, 1)
    act.wait_ge(s.half_ready, 1)
    act.activation(M.t1[:], M.re[:], ACT.Exp)
    act.activation(M.ei[:], M.ei[:], ACT.Sin)
    act.activation(M.q[:], M.q[:], ACT.Sin, scale=-1.0, bias=M.quarter[:]).then_inc(s.small_trig, 1)
    act.wait_ge(s.args_ready, 1)
    act.activation(M.arg[:], M.arg[:], ACT.Sin)
    act.activation(M.cosine[:], M.cosine[:], ACT.Sin, scale=-1.0, bias=M.quarter[:])
    act.activation(M.env[:], M.env[:], ACT.Exp).then_inc(s.trig_ready, 1)


LAYOUTS.append(lambda a: {
    **{"L2_xattn_" + k: column(a, "L2_xattn_" + k) for k in ("log_dt", "D_skip")},
    **{"L2_xattn_" + k: a["L2_xattn_" + k] for k in ("A_re", "A_im", "C_re", "C_im")},
    "c_lags": np.ascontiguousarray(np.broadcast_to(np.concatenate([np.arange(16), np.arange(0, S, 16)]).astype(np.float32), (P, 24)))})

def l1_ffn(nc, R, A):
    E, K, CAP, FP = 64, 6, 64, 88
    SLOTS, FAR = E * CAP, 8192
    xb = nc.dram_tensor("slots_in", (SLOTS, D), F32, kind="Internal").ap()
    yb = nc.dram_tensor("slots_out", (SLOTS, D), F32, kind="Internal").ap()
    with ExitStack() as ctx:
        slot = ctx.enter_context(nc.sbuf_tensor("l1_slot", [P, NB, 8], U32))
        share = ctx.enter_context(nc.sbuf_tensor("l1_share", [P, NB, 8], F32))
        prob, sel = (ctx.enter_context(nc.sbuf_tensor(f"l1_{n}", [P, NB, E], F32)) for n in ("prob", "sel"))
        best = ctx.enter_context(nc.sbuf_tensor("l1_best", [P, NB, 8], F32))
        l1_route(nc, R, A, xb, slot, prob, sel, best)
        l1_slots(nc, R, A, xb, yb, prob, sel, best, share)
        l1_combine(nc, R, A, yb, slot, share)


def l1_route(nc, R, A, xb, slot, prob, sel, best):
    E, K, CAP, FP, FAR = 64, 6, 64, 88, 8192
    SLOTS = E * CAP
    with phase(nc, "l1_route", FLIP + EXPERTS + "cleared pchain zero_ready max_ready exps_ready picks_ready cum_psum cum_ready slot_ready x_ready "
                               "") as (s, sb, ps):
        router, gb, lower, far = sb("router", [P, E]), sb("gb", [P, E]), sb("lower", [P, P]), sb("far", [P, E])
        lowerb, onesb = sb("lowerb", [P, P], BF16), sb("onesb", [P, P], BF16)
        zero = sb("zero", [P, SLOTS // P * D])
        m1, m2, eight, these = sb("m1", [P, NB]), sb("m2", [P, NB]), sb("eight", [P, 8, 8]), sb("these", [P, 8, E])
        pos, tot = sb("pos", [P, NB, E]), sb("tot", [P, NB, E])
        picks = sb("picks", [P, NB, E], BF16)
        xd, at = sb("xd", [P, U, D]), sb("at", [P, U, 8], U32)
        X = experts_buffers(sb, ps, 1, 2, FP, ("L1_ffn_ws1", "L1_ffn_ws3", "L1_ffn_ws2"), None)
        T = flip_buffers(sb, ps, router, p_t=X.p_g, p_r=X.p_u)
        blocks = 512 // E
        with nc.Block() as block:
            @block.sync
            def _(sp):
                load(sp, A, s.w_in, [(router, "L1_ffn_gate_w"), (gb, "L1_ffn_gate_b"), (lower, "c_before"), (far, "c_far")])
                sp.wait_ge(s.zero_ready, 1)
                sp.dma_start(xb.rearrange("(p a) d -> p (a d)", p=P), zero[:]).then_inc(s.cleared, DMA)
                experts_sync(sp, A, s, X)

            @block.gpsimd
            def _(pool):
                norm_pool(R, pool, s)
                chain = Chain(pool, s.pchain)
                last = pool.to_reg(SLOTS - 1)
                with pool.Fori(0, NB // U) as i:
                    chain.restart()
                    for u, b, n in held(i):
                        pool.wait_ge(s.x_ready, n)
                        chain(pool.tensor_copy(at[:, u], row(slot, b)))
                        pool.wait_ge(s.cleared, DMA)
                        for k in range(K):
                            pool.indirect_dma_start(xb, bass.IndirectOffsetOnAxis(ap=at[:, u, k:k + 1], axis=0), xd[:, u], None,
                                                    bounds_check=last, oob_is_err=False).then_inc(R.scattered[u], DMA)
                for u in range(U):
                    pool.wait_ge(R.scattered[u], NB // U * K * DMA)

            @block.vector
            def _(dve):
                chain = Chain(dve, s.vchain)
                dve.memset(zero[:], 0.0).then_inc(s.zero_ready, 1)
                norm_vector(R, dve, s)
                flip_vector(R, dve, s, T)
                dve.wait_ge(s.logits_ready, NB // 4)
                dve.wait_ge(s.w_in, 4 * DMA)
                wide = lambda t: t[:].unsqueeze(2).broadcast_to((P, NB, E))
                rows = lambda t: t[:].unsqueeze(1).broadcast_to((P, NB, E))
                L = T.logits

                def largest(i):
                    chain.restart()
                    chain(dve.tensor_copy(these[:], sel[:, bass.ds(i * 8, 8), :]))
                    for r in range(8):
                        last = dve.max(eight[:, r], these[:, r])
                    chain(last)

                dve.tensor_copy(lowerb[:], lower[:])
                dve.tensor_copy(onesb[:], R.ones[:])
                chain(dve.tensor_reduce(m1[:], L[:], AX.X, ALU.max))
                dve.tensor_tensor(prob[:], L[:], wide(m1), ALU.subtract).then_inc(s.max_ready, 1)
                dve.wait_ge(s.exps_ready, 1)
                chain(dve.tensor_reduce(m1[:], prob[:], AX.X, ALU.add))
                chain(dve.reciprocal(m2[:], m1[:]))
                chain(dve.tensor_tensor(prob[:], prob[:], wide(m2), ALU.mult))
                chain(dve.tensor_tensor(sel[:], prob[:], rows(gb), ALU.add))
                with dve.Fori(0, NB // 8) as i:
                    largest(i)
                    dve.tensor_copy(m1[:, bass.ds(i * 8, 8)], eight[:, :, K - 1]).then_inc(s.slot_ready, 1)
                dve.wait_ge(s.slot_ready, NB // 8)
                chain(dve.tensor_tensor(sel[:], sel[:], wide(m1), ALU.is_ge))
                dve.tensor_copy(picks[:], sel[:]).then_inc(s.picks_ready, 1)
                dve.tensor_tensor(prob[:], prob[:], sel[:], ALU.mult)
                for c in range(NB // blocks):
                    dve.wait_ge(s.cum_psum, c + 1)
                    dve.tensor_copy(pos[:, c * blocks:(c + 1) * blocks].rearrange("p b e -> p (b e)"), X.p_g[:, c % 2])
                    dve.tensor_copy(tot[:, c * blocks:(c + 1) * blocks].rearrange("p b e -> p (b e)"), X.p_u[:, c % 2]).then_inc(s.cum_ready, 1)
                dve.wait_ge(s.cum_ready, NB // blocks)
                src, dst = tot, L
                for step in (1, 2, 4, 8, 16):
                    dve.tensor_copy(dst[:, 0:step], src[:, 0:step])
                    chain(dve.tensor_tensor(dst[:, step:NB], src[:, step:NB], src[:, 0:NB - step], ALU.add))
                    src, dst = dst, src
                chain(dve.tensor_tensor(pos[:, 1:NB], pos[:, 1:NB], src[:, 0:NB - 1], ALU.add))
                chain(dve.tensor_scalar(tot[:], pos[:], float(CAP), None, ALU.is_lt))
                chain(dve.tensor_tensor(sel[:], sel[:], tot[:], ALU.mult))
                chain(dve.tensor_tensor(pos[:], rows(far), pos[:], ALU.subtract))
                chain(dve.tensor_tensor(sel[:], sel[:], pos[:], ALU.mult))
                with dve.Fori(0, NB // 8) as i:
                    largest(i)
                    dve.tensor_copy(best[:, bass.ds(i * 8, 8), :], eight[:]).then_inc(s.slot_ready, 1)
                dve.wait_ge(s.slot_ready, NB // 4)
                dve.tensor_scalar(slot[:], best[:], -1.0, float(FAR), ALU.mult, ALU.add)
                for u in range(U):
                    normalised(R, dve, u, xd[:, u]).then_inc(s.x_ready, 1)
                with dve.Fori(1, NB // U) as i:
                    for u, b, n in held(i):
                        dve.wait_ge(R.scattered[u], i * (K * DMA))
                        normalised(R, dve, b, xd[:, u]).then_inc(s.x_ready, 1)
                experts_vector(R, dve, s, X)

            @block.scalar
            def _(act):
                flip_scalar(R, act, s, T)
                act.wait_ge(s.max_ready, 1)
                act.activation(prob[:], prob[:], ACT.Exp).then_inc(s.exps_ready, 1)
                experts_scalar(act, s, X)

            @block.tensor
            def _(pe):
                pe.wait_ge(s.w_in, 4 * DMA)
                flip_tensor(R, pe, s, T)
                pe.wait_ge(s.picks_ready, 1)
                for c in range(NB // blocks):
                    if c >= 2:
                        pe.wait_ge(s.cum_ready, c - 1)
                    chosen = picks[:, c * blocks:(c + 1) * blocks].rearrange("p b e -> p (b e)")
                    pe.matmul(X.p_g[:, c % 2], lowerb[:], chosen, start=True, stop=True)
                    pe.matmul(X.p_u[:, c % 2], onesb[:], chosen, start=True, stop=True).then_inc(s.cum_psum, 1)
                pe.wait_ge(s.cum_ready, NB // blocks)
                experts_tensor(R, pe, s, X, T)


def l1_slots(nc, R, A, xb, yb, prob, sel, best, share):
    E, K, CAP, FP, W = 64, 6, 64, 88, 2
    NP = E // 2
    with phase(nc, "l1_slots", "vchain x0 x1 up0 up1 down0 down1 xT_psum+2 xT_ready hid_psum+2 silu_ready h_ready y_psum+2 y_ready+2 out0+16 out1+16") as (s, sb, ps):
        x, w13, w2 = sb("x", [P, W, P]), sb("w13", [P, W, 4 * FP]), sb("w2", [FP, W, 2 * P])
        xT, sg, h, y = sb("xT", [P, W, P]), sb("sg", [FP, W, P]), sb("h", [FP, W, P]), sb("y", [CAP, W, 2 * P])
        hit, shares, kept = sb("hit", [P, 2, K, E]), sb("shares", [P, 2, 8]), sb("kept", [P, 2, 8])
        p_x, p_h, p_y = ps("p_x", [P, W, 512]), ps("p_h", [P, W, 512]), ps("p_y", [P, W, 512])
        x_in, up_in, down_in, stored = [s.x0, s.x1], [s.up0, s.up1], [s.down0, s.down1], [s.out0, s.out1]
        xs = xb.rearrange("(n p) d -> n p d", p=P)
        ys = yb.rearrange("(n e c) d -> n c e d", e=2, c=CAP)
        with nc.Block() as block:
            @block.sync
            def _(sp):
                with sp.Fori(0, NP // W) as i:
                    for u in range(W):
                        p = i * W + u
                        sp.wait_ge(s.xT_psum, p + 1)
                        sp.dma_start(x[:, u], xs[bass.ds(p, 1)].rearrange("a p d -> p (a d)")).then_inc(x_in[u], DMA)
                    for u in range(W):
                        sp.wait_ge(s.hid_psum, i * W + (u + 1))
                        sp.dma_start(w13[:, u], A["L1_ffn_w13"][bass.ds(i * W + u, 1)].rearrange("a p n -> p (a n)")).then_inc(up_in[u], DMA)
                    for u in range(W):
                        sp.wait_ge(s.y_psum, i * W + (u + 1))
                        sp.dma_start(w2[:, u], A["L1_ffn_w2"][bass.ds(i * W + u, 1)].rearrange("a p n -> p (a n)")).then_inc(down_in[u], DMA)

            @block.scalar
            def _(act):
                with act.Fori(0, NP // W) as i:
                    for u in range(W):
                        n = i * W + (u + 1)
                        act.wait_ge(s.xT_psum, n + W)
                        act.activation(xT[:, u], p_x[:, u, 0:P], ACT.Copy).then_inc(s.xT_ready, 1)
                    for u in range(W):
                        n = i * W + (u + 1)
                        act.wait_ge(s.hid_psum, n + W)
                        act.activation(sg[:, u], p_h[0:FP, u, 0:P], ACT.Silu).then_inc(s.silu_ready, 1)
                    for u in range(W):
                        n = i * W + (u + 1)
                        act.wait_ge(s.y_psum, n + W)
                        act.wait_ge(stored[u], (i + 1) * DMA)
                        act.activation(y[:, u], p_y[0:CAP, u, 0:2 * P], ACT.Copy).then_inc(s.y_ready, 1)
                    for u in range(W):
                        act.wait_ge(s.y_ready, (i + 1) * W + (u + 1))
                        act.dma_start(ys[bass.ds(i * W + u, 1)].rearrange("a c e d -> c (a e) d"),
                                      y[:, u].rearrange("c (e d) -> c e d", e=2)).then_inc(stored[u], DMA)
                for u in range(W):
                    act.wait_ge(stored[u], (NP // W + 1) * DMA)

            @block.vector
            def _(dve):
                chain = Chain(dve, s.vchain)
                chain(dve.memset(shares[:], 0.0))
                with dve.Fori(0, NP // W) as i:
                    for u in range(W):
                        n = i * W + (u + 1)
                        dve.wait_ge(s.silu_ready, n)
                        dve.tensor_tensor(h[:, u], sg[:, u], p_h[0:FP, u, P:2 * P], ALU.mult).then_inc(s.h_ready, 1)
                    chain.restart()
                    two = lambda t: t[:, bass.ds(i * 2, 2), :]
                    each = lambda t: two(t).unsqueeze(2).broadcast_to((P, 2, K, E))
                    chain(dve.tensor_tensor(hit[:], each(sel), two(best)[:, :, 0:K].unsqueeze(3).broadcast_to((P, 2, K, E)), ALU.is_equal))
                    chain(dve.tensor_tensor(hit[:], hit[:], each(prob), ALU.mult))
                    chain(dve.tensor_reduce(shares[:, :, 0:K], hit[:], AX.X, ALU.add))
                    chain(dve.tensor_scalar(kept[:], two(best), 0.0, None, ALU.is_gt))
                    chain(dve.tensor_tensor(two(share), shares[:], kept[:], ALU.mult))

            @block.tensor
            def _(pe):
                with pe.Fori(0, NP // W) as i:
                    for u in range(W):
                        pe.wait_ge(x_in[u], (i + 1) * DMA)
                        pe.transpose(p_x[:, u, 0:P], x[:, u], R.ident[:]).then_inc(s.xT_psum, 1)
                    for u in range(W):
                        pe.wait_ge(s.xT_ready, i * W + (u + 1))
                        pe.wait_ge(up_in[u], (i + 1) * DMA)
                        for g in range(2):
                            for e in range(2):
                                w = (2 * e + g) * FP
                                mm = pe.matmul(p_h[0:FP, u, g * P + e * CAP:g * P + (e + 1) * CAP], w13[:, u, w:w + FP],
                                               xT[:, u, e * CAP:(e + 1) * CAP], start=True, stop=True)
                        mm.then_inc(s.hid_psum, 1)
                    for u in range(W):
                        pe.wait_ge(s.h_ready, i * W + (u + 1))
                        pe.wait_ge(s.y_ready, (i + 1) * W)
                        pe.wait_ge(down_in[u], (i + 1) * DMA)
                        for e in range(2):
                            mm = pe.matmul(p_y[0:CAP, u, e * P:(e + 1) * P], h[:, u, e * CAP:(e + 1) * CAP], w2[:, u, e * P:(e + 1) * P],
                                           start=True, stop=True)
                        mm.then_inc(s.y_psum, 1)


def l1_combine(nc, R, A, yb, slot, share):
    K, SLOTS, V = 6, 64 * 64, 4
    with phase(nc, "l1_combine", SSM + "vchain pchain zeroed got_added+4") as (s, sb, ps):
        M = ssm_buffers(sb)
        got, at = sb("got", [P, V, K, D]), sb("at", [P, V, 8], U32)
        with nc.Block() as block:
            @block.sync
            def _(sp):
                ssm_sync(sp, A, s, M)
                sp.wait_ge(s.padded, 1)
                sp.dma_start(R.ssm_rows, M.kpad[:]).then_inc(s.rows_out, DMA)
                sp.wait_ge(s.rows_out, DMA)

            @block.scalar
            def _(act):
                ssm_scalar(act, s, M)

            @block.gpsimd
            def _(pool):
                chain = Chain(pool, s.pchain)
                last = pool.to_reg(SLOTS - 1)
                with pool.Fori(0, NB // V) as i:
                    chain.restart()
                    for u, b, n in held(i, V):
                        pool.wait_ge(s.got_added, n)
                        chain(pool.tensor_copy(at[:, u], row(slot, b)))
                        pool.wait_ge(s.zeroed, 1)
                        for k in range(K):
                            pool.indirect_dma_start(got[:, u, k], None, yb, bass.IndirectOffsetOnAxis(ap=at[:, u, k:k + 1], axis=0),
                                                    bounds_check=last, oob_is_err=False).then_inc(R.fetched[u], DMA)

            @block.vector
            def _(dve):
                chain = Chain(dve, s.vchain)
                dve.memset(got[:], 0.0).then_inc(s.zeroed, 1)
                ssm_tables(dve, chain, s, M)
                with dve.Fori(0, NB // V) as i:
                    chain.restart()
                    for u, b, n in held(i, V):
                        dve.wait_ge(R.fetched[u], (i + 1) * (K * DMA))
                        for k in range(K):
                            chain(dve.scalar_tensor_tensor(out=row(R.x, b), in0=got[:, u, k],
                                                           scalar=share[:, bass.ds(b, 1), k:k + 1].rearrange("p a c -> p (a c)"),
                                                           in1=row(R.x, b), op0=ALU.mult, op1=ALU.add))
                        row_stats(R, dve, b, chain).then_inc(s.got_added, 1)
                    ssm_lags(dve, chain, M, i)
                dve.tensor_tensor(M.kpad[:, S - 1:S], M.kpad[:, S - 1:S], M.skip[:], ALU.add).then_inc(s.padded, 1)


PHASES.append(l1_ffn)
LAYOUTS.append(lambda a: {
    "L1_ffn_gate_w": transposed(a, "L1_ffn_gate_w"), "L1_ffn_gate_b": repeated(a, "L1_ffn_gate_b"),
    "c_far": np.ascontiguousarray(np.broadcast_to((8192 - 64 * np.arange(64)).astype(np.float32), (P, 64))),
    "c_before": (np.arange(P)[:, None] < np.arange(P)[None, :]).astype(np.float32),
    "L1_ffn_ws1": transposed(a, "L1_ffn_ws1")[None], "L1_ffn_ws3": transposed(a, "L1_ffn_ws3")[None],
    "L1_ffn_ws2": np.ascontiguousarray(a["L1_ffn_ws2"].reshape(P, 2, 88).transpose(2, 1, 0).reshape(1, 88, 2 * P)),
    "L1_ffn_w13": np.ascontiguousarray(np.stack([a["L1_ffn_w1"], a["L1_ffn_w3"]], 1).reshape(32, 4 * 88, P).transpose(0, 2, 1)),
    "L1_ffn_w2": np.ascontiguousarray(a["L1_ffn_w2"].reshape(32, 2, P, 88).transpose(0, 3, 1, 2).reshape(32, 88, 2 * P))})

def l2_attn(nc, R, A):
    eps = 1e-6
    with phase(nc, "l2_attn", "var_ready rstd_ready shift_ready w_in vchain xhat_ready xT_psum xT_ready kv_psum qT_psum "
                   "k_ready v_ready q_ready mem_psum memT_ready memW_psum memW_ready out_psum") as (s, sb, ps):
        wqkv, wout, bout = sb("wqkv", [P, 384]), sb("wout", [P, P]), sb("bout", [P, P])
        xhat, xT = sb("xhat", [P, U, 2, P]), sb("xT", [P, U, 256])
        k, v, qT = sb("k", [P, U, 2, P]), sb("v", [P, U, 2, P]), sb("qT", [P, U, 256])
        memT, memW, z = sb("memT", [P, U, 2, P]), sb("memW", [P, U, 2, P + 1]), sb("z", [P, U, 2, 2])
        p_t, p_kv, p_m, p_o = (ps(n, [P, U, 512]) for n in ("p_t", "p_kv", "p_m", "p_o"))
        M = P + 1
        with nc.Block() as block:
            @block.sync
            def _(sp):
                load(sp, A, s.w_in, [(wqkv, "L2_attn_W_qkv"), (wout, "L2_attn_W_out"), (bout, "L2_attn_b_out")])

            @block.gpsimd
            def _(pool):
                norm_pool(R, pool, s)

            @block.vector
            def _(dve):
                chain = Chain(dve, s.vchain)
                norm_vector(R, dve, s)
                dve.wait_ge(s.w_in, 3 * DMA)
                with dve.Fori(0, NB // 2 // U) as i:
                    chain.restart()
                    for u, b, n in held(i):
                        pair_normalised(R, dve, b, xhat[:, u]).then_inc(s.xhat_ready, 1)
                    for u, b, n in held(i):
                        dve.wait_ge(s.kv_psum, n)
                        dve.tensor_scalar(k[:, u], p_kv[:, u].rearrange("p (r c) -> p r c", c=256)[:, :, 0:P], 0.0, eps,
                                          ALU.max, ALU.add).then_inc(s.k_ready, 1)
                        dve.wait_ge(s.qT_psum, n)
                        dve.tensor_scalar(qT[:, u], p_t[:, u, 256:512], 0.0, eps, ALU.max, ALU.add).then_inc(s.q_ready, 1)
                        dve.tensor_tensor(pair(R.x, b), pair(R.x, b), bout[:].unsqueeze(1).broadcast_to((P, 2, P)), ALU.add)
                    for u, b, n in held(i):
                        dve.wait_ge(s.out_psum, n)
                        sums = p_o[:, u, 0:2 * M].rearrange("p (r c) -> p r c", c=M)[:, :, P]
                        chain(dve.tensor_scalar(z[:, u, 0], sums, eps, None, ALU.add))
                        chain(dve.reciprocal(z[:, u, 1], z[:, u, 0]))
                        for r in range(2):
                            last = dve.scalar_tensor_tensor(out=row(R.x, b * 2 + r), in0=p_o[:, u, r * M:r * M + P], scalar=z[:, u, 1, r:r + 1],
                                                            in1=row(R.x, b * 2 + r), op0=ALU.mult, op1=ALU.add)
                        chain(last)
                        chain(pair_stats(R, dve, b, chain))

            @block.scalar
            def _(act):
                with act.Fori(0, NB // 2 // U) as i:
                    for u, b, n in held(i):
                        act.wait_ge(s.xT_psum, n)
                        act.activation(xT[:, u], p_t[:, u, 0:256], ACT.Copy).then_inc(s.xT_ready, 1)
                    for u, b, n in held(i):
                        act.wait_ge(s.k_ready, n)
                        act.activation(v[:, u], p_kv[:, u].rearrange("p (r c) -> p r c", c=256)[:, :, P:256], ACT.Copy).then_inc(s.v_ready, 1)
                    for u, b, n in held(i):
                        act.wait_ge(s.mem_psum, n)
                        mem = p_m[:, u, 0:2 * M].rearrange("p (r c) -> p r c", c=M)
                        act.activation(memW[:, u, :, P], mem[:, :, P], ACT.Copy)
                        act.activation(memT[:, u], mem[:, :, 0:P], ACT.Copy).then_inc(s.memT_ready, 1)
                    for u, b, n in held(i):
                        act.wait_ge(s.memW_psum, n)
                        act.activation(memW[:, u, :, 0:P], side(p_t[:, u, 0:256]), ACT.Copy).then_inc(s.memW_ready, 1)

            @block.tensor
            def _(pe):
                pe.wait_ge(s.w_in, 3 * DMA)
                with pe.Fori(0, NB // 2 // U) as i:
                    for u, b, n in held(i):
                        pe.wait_ge(s.xhat_ready, n)
                        for r in range(2):
                            mm = pe.transpose(p_t[:, u, r * P:(r + 1) * P], xhat[:, u, r], R.ident[:])
                        mm.then_inc(s.xT_psum, 1)
                    for u, b, n in held(i):
                        pe.wait_ge(s.xT_ready, n)
                        for r in range(2):
                            mm = pe.matmul(p_kv[:, u, r * 256:(r + 1) * 256], xT[:, u, r * P:(r + 1) * P], wqkv[:, P:384], start=True, stop=True)
                        mm.then_inc(s.kv_psum, 1)
                        pe.matmul(p_t[:, u, 256:512], wqkv[:, 0:P], xT[:, u], start=True, stop=True).then_inc(s.qT_psum, 1)
                    for u, b, n in held(i):
                        pe.wait_ge(s.v_ready, n)
                        for r in range(2):
                            pe.matmul(p_m[:, u, r * M:r * M + P], v[:, u, r], k[:, u, r], start=True, stop=True)
                            mm = pe.matmul(p_m[:, u, r * M + P:(r + 1) * M], k[:, u, r], R.ones[:, 0:1], start=True, stop=True)
                        mm.then_inc(s.mem_psum, 1)
                    for u, b, n in held(i):
                        pe.wait_ge(s.memT_ready, n)
                        pe.wait_ge(s.q_ready, n)
                        for r in range(2):
                            mm = pe.matmul(p_t[:, u, r * P:(r + 1) * P], memT[:, u, r], wout[:], start=True, stop=True)
                        mm.then_inc(s.memW_psum, 1)
                    for u, b, n in held(i):
                        pe.wait_ge(s.memW_ready, n)
                        for r in range(2):
                            mm = pe.matmul(p_o[:, u, r * M:(r + 1) * M], qT[:, u, r * P:(r + 1) * P], memW[:, u, r], start=True, stop=True)
                        mm.then_inc(s.out_psum, 1)


PHASES.append(l2_attn)
LAYOUTS.append(lambda a: {"L2_attn_W_qkv": transposed(a, "L2_attn_W_qkv"), "L2_attn_W_out": transposed(a, "L2_attn_W_out"),
                          "L2_attn_b_out": repeated(a, "L2_attn_b_out")})

def l2_xattn(nc, R, A):
    with ExitStack() as ctx:
        toep = ctx.enter_context(nc.sbuf_tensor("ssm_toep", [P, P, S], F32))
        xin = ctx.enter_context(nc.sbuf_tensor("ssm_in", [P, NB, D], F32))
        film = ctx.enter_context(nc.sbuf_tensor("film_out", [P, NB, 2 * D], F32))
        l2_film(nc, R, A, toep, xin, film)
        l2_mix(nc, R, A, toep, xin, film)


def l2_film(nc, R, A, toep, xin, film):
    H, TOP, HD = 4, 32, 32
    with phase(nc, "l2_film", "toeplitz_in var_ready rstd_ready shift_ready w_in vchain set_ready xhat_ready ctx_ready rstd2_ready xT_psum xT_ready qkv_psum qkv_ready "
                   "kexp_ready scores_psum scores_ready top_ready exp_ready mean_ready mT_psum mT_ready c_psum c_ready film_psum film_ready"
               ) as (s, sb, ps):
        wq, wkv, wf, bf, gate = sb("wq", [P, P]), sb("wkv", [DC, 256]), sb("wf", [P, 512]), sb("bf", [P, 512]), sb("gate", [P, 1])
        gam, bet, head32 = sb("gam", [P, P]), sb("bet", [P, P]), sb("head32", [P, H])
        m4, mneg = sb("m4", [1, NB, SC // 4], U32), sb("mneg", [1, NB, SC])
        tm4, tm = sb("tm4", [P, NB // 4], U32), sb("tm", [P, NB])
        xhat, xT, cT = sb("xhat", [P, U, P]), sb("xT", [P, U, P]), sb("cT", [DC, U, SC])
        bn, st, rs = sb("bn6", [P, U, 6]), sb("st", [P, U, 2]), sb("rs", [P, U])
        kT, qT, kexp, V = sb("kT", [P, U, SC]), sb("qT", [P, U, P]), sb("kexp", [P, U, H, SC]), sb("V", [SC, U, P])
        sc, wk, e = sb("sc", [P, U, H, SC]), sb("wk", [P, U, H, SC]), sb("e", [P, U, H, SC])
        top, nm, z = sb("top", [P, U, H, TOP]), sb("nm", [P, U, H]), sb("z", [P, U, 2, H])
        mean, mT, cc = sb("mean", [P, U, SC]), sb("mT", [SC, U, P]), sb("cc", [P, U, P])
        f = sb("f", [P, U, 256])
        p_a, p_s, p_f = ps("p_a", [P, U, 512]), ps("p_s", [P, U, 512]), ps("p_f", [P, U, 512])
        with nc.Block() as block:
            @block.sync
            def _(sp):
                load(sp, A, s.w_in, [(wq, "L2_xattn_Wq"), (wkv, "L2_xattn_Wkv"), (wf, "L2_xattn_W_film"), (bf, "L2_xattn_b_film"),
                                     (gate, "L2_xattn_mod_gate"), (gam, "L2_xattn_g_norm_in"), (bet, "L2_xattn_b_norm_in"),
                                     (head32, "c_head32"), (m4, "mask_BxS2_bf1"), (tm4, "mask_BxS_bf1")])
                sp.dma_start(toep[:], bass.AP(R.ssm_rows.tensor, 0, [[1, P], [2 * S, P], [1, S]])).then_inc(s.toeplitz_in, DMA)
                sp.wait_ge(s.toeplitz_in, DMA)

            @block.gpsimd
            def _(pool):
                norm_pool(R, pool, s)
                with pool.Fori(0, NB // U) as i:
                    for u, b, n in held(i):
                        pool.wait_ge(s.xhat_ready, n)
                        pool.tensor_copy(cT[:, u], row(R.ctxT, b)[0:DC]).then_inc(s.ctx_ready, 1)
                        pool.wait_ge(s.ctx_ready, n)
                        pool.tensor_tensor(rs[:, u:u + 1], rs[:, u:u + 1], R.minus_half[:, 0:1], ALU.pow).then_inc(s.rstd2_ready, 1)

            @block.vector
            def _(dve):
                chain = Chain(dve, s.vchain)
                norm_vector(R, dve, s)
                dve.wait_ge(s.w_in, 10 * DMA)
                chain(dve.tensor_copy(tm[:], tm4[:].bitcast(U8)))
                chain(dve.tensor_scalar(bf[:], bf[:], gate[:], None, ALU.mult))
                scales = bf[:].rearrange("p (k a d) -> p k a d", k=2, a=2)[:, :, 0]
                chain(dve.tensor_scalar(scales, scales, 1.0, None, ALU.add))
                dve.tensor_scalar(mneg[:], m4[:].bitcast(U8), 1.0, 1e30, ALU.subtract, ALU.mult).then_inc(s.set_ready, 1)
                with dve.Fori(0, NB // U) as i:
                    chain.restart()
                    for u, b, n in held(i):
                        chain(normalised(R, dve, b, xhat[:, u]))
                        chain(dve.bn_stats(bn[:, u], xhat[:, u]))
                        chain(dve.bn_aggr(st[:, u], bn[:, u]))
                        dve.tensor_scalar(rs[:, u:u + 1], st[:, u, 1:2], EPS, None, ALU.add).then_inc(s.xhat_ready, 1)
                    for u, b, n in held(i):
                        dve.wait_ge(s.qkv_ready, n)
                        dve.tensor_tensor(kexp[:, u], kT[:, u].unsqueeze(1).broadcast_to((P, H, SC)),
                                          head32[:].unsqueeze(2).broadcast_to((P, H, SC)), ALU.mult).then_inc(s.kexp_ready, 1)
                    for u, b, n in held(i):
                        dve.wait_ge(s.scores_psum, n)
                        chain(dve.tensor_copy(sc[:, u].rearrange("p h k -> p (h k)"), p_s[:, u, 0:H * SC]))
                        for r in range(TOP // 8):
                            src = sc if r == 0 else wk
                            for h in range(H):
                                last = dve.max(top[:, u, h, 8 * r:8 * r + 8], src[:, u, h])
                            chain(last)
                            if r == 0:
                                dve.tensor_scalar(nm[:, u], top[:, u, :, 0], -1.0, None, ALU.mult).then_inc(s.top_ready, 1)
                            if r < TOP // 8 - 1:
                                for h in range(H):
                                    last = dve.match_replace(wk[:, u, h], top[:, u, h, 8 * r:8 * r + 8], src[:, u, h], -3e38)
                                chain(last)
                    for u, b, n in held(i):
                        dve.wait_ge(s.exp_ready, n)
                        for h in range(H):
                            last = dve.scalar_tensor_tensor(out=e[:, u, h], in0=sc[:, u, h], scalar=top[:, u, h, TOP - 1:TOP],
                                                            in1=e[:, u, h], op0=ALU.is_ge, op1=ALU.mult)
                        chain(last)
                        chain(dve.tensor_reduce(z[:, u, 0], e[:, u], AX.X, ALU.add))
                        chain(dve.reciprocal(z[:, u, 1], z[:, u, 0]))
                        chain(dve.tensor_scalar(z[:, u, 1], z[:, u, 1], 1.0 / H, tm[:, bass.ds(b, 1)], ALU.mult, ALU.mult))
                        chain(dve.tensor_scalar(mean[:, u], e[:, u, 0], z[:, u, 1, 0:1], None, ALU.mult))
                        for h in range(1, H - 1):
                            chain(dve.scalar_tensor_tensor(out=mean[:, u], in0=e[:, u, h], scalar=z[:, u, 1, h:h + 1], in1=mean[:, u],
                                                           op0=ALU.mult, op1=ALU.add))
                        dve.scalar_tensor_tensor(out=mean[:, u], in0=e[:, u, H - 1], scalar=z[:, u, 1, H - 1:H], in1=mean[:, u],
                                                 op0=ALU.mult, op1=ALU.add).then_inc(s.mean_ready, 1)
                    for u, b, n in held(i):
                        dve.wait_ge(s.rstd2_ready, n)
                        chain(dve.tensor_scalar(xhat[:, u], xhat[:, u], st[:, u, 0:1], rs[:, u:u + 1], ALU.subtract, ALU.mult))
                        chain(dve.tensor_tensor(xhat[:, u], xhat[:, u], gam[:], ALU.mult))
                        chain(dve.tensor_tensor(xhat[:, u], xhat[:, u], bet[:], ALU.add))
                    for u, b, n in held(i):
                        dve.wait_ge(s.film_psum, n)
                        chain(dve.scalar_tensor_tensor(out=f[:, u], in0=p_f[:, u, 0:256], scalar=gate[:], in1=bf[:, 0:256],
                                                       op0=ALU.mult, op1=ALU.add))
                        dve.scalar_tensor_tensor(out=row(film, b), in0=p_f[:, u, 256:512], scalar=gate[:], in1=bf[:, 256:512],
                                                 op0=ALU.mult, op1=ALU.add)
                        chain(dve.tensor_tensor(xhat[:, u], xhat[:, u], f[:, u, 0:P], ALU.mult))
                        chain(dve.tensor_tensor(row(xin, b), xhat[:, u], f[:, u, P:256], ALU.add))

            @block.scalar
            def _(act):
                with act.Fori(0, NB // U) as i:
                    for u, b, n in held(i):
                        act.wait_ge(s.xT_psum, n)
                        act.activation(xT[:, u], p_a[:, u, 0:P], ACT.Copy).then_inc(s.xT_ready, 1)
                    for u, b, n in held(i):
                        act.wait_ge(s.qkv_psum, n)
                        act.activation(kT[:, u], p_a[:, u, P:P + SC], ACT.Copy)
                        act.activation(V[:, u], p_a[0:SC, u, 256:384], ACT.Copy)
                        act.activation(qT[:, u], p_a[:, u, 384:512], ACT.Copy, scale=HD ** -0.5).then_inc(s.qkv_ready, 1)
                    for u, b, n in held(i):
                        act.wait_ge(s.top_ready, n)
                        for h in range(H):
                            x = act.activation(e[:, u, h], sc[:, u, h], ACT.Exp, bias=nm[:, u, h:h + 1])
                        x.then_inc(s.exp_ready, 1)
                    for u, b, n in held(i):
                        act.wait_ge(s.mT_psum, n)
                        act.activation(mT[:, u], p_a[0:SC, u, 0:P], ACT.Copy).then_inc(s.mT_ready, 1)
                    for u, b, n in held(i):
                        act.wait_ge(s.c_psum, n)
                        act.activation(cc[:, u], p_a[:, u, P:256], ACT.Copy).then_inc(s.c_ready, 1)

            @block.tensor
            def _(pe):
                pe.wait_ge(s.w_in, 10 * DMA)
                pe.wait_ge(s.set_ready, 1)
                with pe.Fori(0, NB // U) as i:
                    for u, b, n in held(i):
                        pe.wait_ge(s.xhat_ready, n)
                        pe.transpose(p_a[:, u, 0:P], xhat[:, u], R.ident[:]).then_inc(s.xT_psum, 1)
                    for u, b, n in held(i):
                        pe.wait_ge(s.xT_ready, n)
                        pe.wait_ge(s.ctx_ready, n)
                        pe.matmul(p_a[:, u, P:P + SC], wkv[:, 0:P], cT[:, u], start=True, stop=True)
                        pe.matmul(p_a[0:SC, u, 256:384], cT[:, u], wkv[:, P:256], start=True, stop=True)
                        pe.matmul(p_a[:, u, 384:512], wq[:], xT[:, u], start=True, stop=True).then_inc(s.qkv_psum, 1)
                    for u, b, n in held(i):
                        pe.wait_ge(s.kexp_ready, n)
                        pe.matmul(p_s[:, u, 0:H * SC], qT[:, u], kexp[:, u].rearrange("p h k -> p (h k)"), start=True, stop=False,
                                  skip_group_check=True)
                        for h in range(H):
                            mm = pe.matmul(p_s[:, u, h * SC:(h + 1) * SC], R.ones[0:1, :], row(mneg, b), start=False, stop=True,
                                           skip_group_check=True)
                        mm.then_inc(s.scores_psum, 1)
                    for u, b, n in held(i):
                        pe.wait_ge(s.mean_ready, n)
                        pe.transpose(p_a[0:SC, u, 0:P], mean[:, u], R.ident[:]).then_inc(s.mT_psum, 1)
                    for u, b, n in held(i):
                        pe.wait_ge(s.mT_ready, n)
                        pe.matmul(p_a[:, u, P:256], V[:, u], mT[:, u], start=True, stop=True).then_inc(s.c_psum, 1)
                    for u, b, n in held(i):
                        pe.wait_ge(s.c_ready, n)
                        pe.matmul(p_f[:, u], cc[:, u], wf[:], start=True, stop=True).then_inc(s.film_psum, 1)


def l2_mix(nc, R, A, toep, xin, film):
    GROUP, FC = 32, 4
    with phase(nc, "l2_mix", "w_in vchain turned_psum turned+2 conv_psum conv_copied var1_ready rstd1_ready h_ready hT_psum hT_ready hid_psum hid_ready mlp_psum var2_ready rstd2_ready"
               ) as (s, sb, ps):
        w1, w2, b1, b2 = sb("w1", [P, 512]), sb("w2", [P, FC, P]), sb("b1", [P, FC]), sb("b2", [P, P])
        gf, bff, go, bo = (sb(n, [P, P]) for n in ("gf", "bff", "go", "bo"))
        y, turn = sb("y", [P, NB, D]), sb("turn", [P, P])
        xrows = xin[:].rearrange("p (g r) d -> p g (r d)", r=4)
        xt, h, bn, st, rs = sb("xt", [P, U, 2, P]), sb("h", [P, U, 2, P]), sb("bn6", [P, U, 2, 6]), sb("st", [P, U, 2, 2]), sb("rs", [P, U, 2])
        hT, hid = sb("hT", [P, U, 256]), sb("hid", [P, U, FC, 256])
        p_conv = ps("p_conv", [P, 2, GROUP, 32])
        p_h, p_o = ps("p_h", [P, 2, 512]), ps("p_o", [P, 2, 512])
        with nc.Block() as block:
            @block.sync
            def _(sp):
                load(sp, A, s.w_in, [(w1, "L2_xattn_W1"), (w2, "L2_xattn_W2"), (b1, "L2_xattn_b1"), (b2, "L2_xattn_b2"), (gf, "L2_xattn_g_ffn"),
                                     (bff, "L2_xattn_b_ffn"), (go, "L2_xattn_g_norm_out"), (bo, "L2_xattn_b_norm_out"), (turn, "c_turn")])

            @block.gpsimd
            def _(pool):
                with pool.Fori(0, NB // 2 // U) as i:
                    for ready, done in ((s.var1_ready, s.rstd1_ready), (s.var2_ready, s.rstd2_ready)):
                        for u, b, n in held(i):
                            pool.wait_ge(ready, n)
                            pool.tensor_tensor(rs[:, u], rs[:, u], R.minus_half[:, 0:2], ALU.pow).then_inc(done, 1)

            @block.vector
            def _(dve):
                chain = Chain(dve, s.vchain)
                dve.wait_ge(s.w_in, 9 * DMA)
                dve.wait_ge(s.conv_copied, P // GROUP)
                def variances(u, ready):
                    for r in range(2):
                        last = dve.bn_stats(bn[:, u, r], xt[:, u, r])
                    chain(last)
                    for r in range(2):
                        last = dve.bn_aggr(st[:, u, r], bn[:, u, r])
                    chain(last)
                    dve.tensor_scalar(rs[:, u], st[:, u, :, 1], EPS, None, ALU.add).then_inc(ready, 1)

                def normal(u, out, gamma):
                    for r in range(2):
                        last = dve.tensor_scalar(out[:, u, r], xt[:, u, r], st[:, u, r, 0:1], rs[:, u, r:r + 1], ALU.subtract, ALU.mult)
                    chain(last)
                    chain(dve.tensor_tensor(out[:, u], out[:, u], both(gamma), ALU.mult))

                with dve.Fori(0, NB // 2 // U) as i:
                    chain.restart()
                    for u, b, n in held(i):
                        dve.tensor_tensor(xt[:, u], pair(y, b), pair(film, b)[:, :, 0:P], ALU.mult)
                        chain(pair_normalised(R, dve, b, h[:, u]))
                        chain(dve.tensor_tensor(xt[:, u], xt[:, u], pair(film, b)[:, :, P:256], ALU.add))
                        chain(dve.tensor_tensor(xt[:, u], xt[:, u], h[:, u], ALU.add))
                        variances(u, s.var1_ready)
                    for u, b, n in held(i):
                        dve.wait_ge(s.rstd1_ready, n)
                        normal(u, h, gf)
                        dve.tensor_tensor(h[:, u], h[:, u], both(bff), ALU.add).then_inc(s.h_ready, 1)
                    for u, b, n in held(i):
                        chain(dve.tensor_tensor(xt[:, u], xt[:, u], both(b2), ALU.add))
                        dve.wait_ge(s.hT_psum, n)
                        dve.tensor_copy(hT[:, u], p_o[:, u, 256:512]).then_inc(s.hT_ready, 1)
                    for u, b, n in held(i):
                        dve.wait_ge(s.mlp_psum, n)
                        chain(dve.tensor_tensor(xt[:, u], xt[:, u], side(p_o[:, u, 0:256]), ALU.add))
                        variances(u, s.var2_ready)
                    for u, b, n in held(i):
                        dve.wait_ge(s.rstd2_ready, n)
                        normal(u, xt, go)
                        chain(dve.tensor_tensor(xt[:, u], xt[:, u], both(bo), ALU.add))
                        chain(dve.tensor_tensor(pair(R.x, b), pair(R.x, b), xt[:, u], ALU.add))
                        chain(pair_stats(R, dve, b, chain))

            @block.scalar
            def _(act):
                with act.Fori(0, NB // 8) as i:
                    for k in range(2):
                        act.wait_ge(s.turned_psum, i * 2 + (k + 1))
                        act.activation(row(xrows, i * 2 + k), p_h[:, k], ACT.Copy).then_inc(s.turned, 1)
                for g in range(P // GROUP):
                    act.wait_ge(s.conv_psum, g + 1)
                    act.activation(y[:, :, g * GROUP:(g + 1) * GROUP].rearrange("p b h -> p h b"),
                                   p_conv[:, g % 2, :, 0:NB], ACT.Copy).then_inc(s.conv_copied, 1)
                act.wait_ge(s.w_in, 9 * DMA)
                with act.Fori(0, NB // 2 // U) as i:
                    for u, b, n in held(i):
                        for c in range(FC):
                            act.wait_ge(s.hid_psum, i * (U * FC) + (u * FC + c + 1))
                            act.activation(hid[:, u, c], p_h[:, c % 2, 0:256], ACT.Gelu, bias=b1[:, c:c + 1]).then_inc(s.hid_ready, 1)

            @block.tensor
            def _(pe):
                pe.wait_ge(s.w_in, 9 * DMA)
                with pe.Fori(0, NB // 8) as i:
                    for k in range(2):
                        pe.wait_ge(s.turned, (i + 1) * 2)
                        pe.matmul(p_h[:, k], turn[:], row(xrows, i * 2 + k), start=True, stop=True).then_inc(s.turned_psum, 1)
                pe.wait_ge(s.turned, NB // 4 + 2)
                for h_ in range(P):
                    g, j = divmod(h_, GROUP)
                    if j == 0 and g >= 2:
                        pe.wait_ge(s.conv_copied, g - 1)
                    mm = pe.matmul(p_conv[:, g % 2, j, 0:NB], toep[:, h_, :], xin[:, :, h_], start=True, stop=True)
                    if j == GROUP - 1:
                        mm.then_inc(s.conv_psum, 1)
                with pe.Fori(0, NB // 2 // U) as i:
                    for u, b, n in held(i):
                        pe.wait_ge(s.h_ready, n)
                        for r in range(2):
                            mm = pe.transpose(p_o[:, u, 256 + r * P:256 + (r + 1) * P], h[:, u, r], R.ident[:])
                        mm.then_inc(s.hT_psum, 1)
                    for u, b, n in held(i):
                        pe.wait_ge(s.hT_ready, n)
                        for c in range(FC):
                            if u * FC + c >= 2:
                                pe.wait_ge(s.hid_ready, i * (U * FC) + (u * FC + c - 1))
                            pe.matmul(p_h[:, c % 2, 0:256], w1[:, c * P:(c + 1) * P], hT[:, u], start=True, stop=True).then_inc(s.hid_psum, 1)
                    for u, b, n in held(i):
                        pe.wait_ge(s.hid_ready, i * (U * FC) + (u + 1) * FC)
                        for r in range(2):
                            for c in range(FC):
                                mm = pe.matmul(p_o[:, u, r * P:(r + 1) * P], hid[:, u, c, r * P:(r + 1) * P], w2[:, c], start=(c == 0),
                                               stop=(c == FC - 1))
                        mm.then_inc(s.mlp_psum, 1)


PHASES.append(l2_xattn)


def layout_l2_xattn(a):
    n = "L2_xattn_"
    return {
        **{n + k: a[n + k] for k in ("Wq", "W1")},
        "c_turn": np.ascontiguousarray(np.eye(P, dtype=np.float32)[::-1]),
        n + "Wkv": np.ascontiguousarray(np.concatenate([a[n + "Wk"], a[n + "Wv"]], 1)),
        n + "W_film": np.ascontiguousarray(np.concatenate([a[n + "W_film_in"], a[n + "W_film_out"]], 1)),
        n + "b_film": np.ascontiguousarray(np.broadcast_to(np.concatenate([a[n + "b_film_in"], a[n + "b_film_out"]])[None], (P, 512))),
        n + "mod_gate": np.ascontiguousarray(np.broadcast_to(a[n + "mod_gate"].reshape(1, 1), (P, 1))),
        **{n + k: repeated(a, n + k) for k in ("g_norm_in", "b_norm_in", "g_norm_out", "b_norm_out", "g_ffn", "b_ffn", "b2")},
        "c_head32": (np.arange(P)[:, None] // 32 == np.arange(4)[None, :]).astype(np.float32),
        "mask_BxS2_bf1": a["mask_BxS2_bf1"].view(np.uint32).reshape(1, NB, SC // 4), "mask_BxS_bf1": np.ascontiguousarray(a["mask_BxS_bf1"].T).view(np.uint32),
        n + "W2": np.ascontiguousarray(a[n + "W2"].reshape(4, P, P).transpose(1, 0, 2)), n + "b1": np.ascontiguousarray(a[n + "b1"].reshape(4, P).T)}


LAYOUTS.append(layout_l2_xattn)

def l2_ffn(nc, R, A):
    E, AH, K = 8, 50, 6
    with phase(nc, "l2_ffn", FLIP + EXPERTS + "max_ready exps_ready ah_psum ah_ready+2 al_psum+2 al_ready+2") as (s, sb, ps):
        router, w1, w2 = sb("router", [P, E]), sb("w1", [P, AH]), sb("w2", [AH, K])
        b1, b2, order = sb("b1", [AH, 1]), sb("b2", [P, K]), sb("order", [P, K])
        m1, m2, k, cw, tmp = sb("m1", [P, NB]), sb("m2", [P, NB]), sb("k", [P, NB]), sb("cw", [P, NB, E]), sb("tmp", [P, NB, E])
        ah, al, rank = sb("ah", [AH, U, P]), sb("al", [P, NB, K]), sb("rank", [P, NB, E])
        X = experts_buffers(sb, ps, E, 3, 112, ("L2_ffn_gate_w", "L2_ffn_up_w", "L2_ffn_down_w"), cw)
        T = flip_buffers(sb, ps, router, p_t=X.p_g, p_r=X.p_u)
        with nc.Block() as block:
            @block.sync
            def _(sp):
                load(sp, A, s.w_in, [(router, "L2_ffn_router_w"), (w1, "L2_ffn_actor_w1"), (w2, "L2_ffn_actor_w2"),
                                     (b1, "L2_ffn_actor_b1"), (b2, "L2_ffn_actor_b2"), (order, "c_order6")])
                experts_sync(sp, A, s, X)

            @block.gpsimd
            def _(pool):
                norm_pool(R, pool, s)

            @block.vector
            def _(dve):
                chain = Chain(dve, s.vchain)
                norm_vector(R, dve, s)
                flip_vector(R, dve, s, T)
                with dve.Fori(0, NB // U) as i:
                    for u, b, n in held(i):
                        dve.wait_ge(s.al_psum, n + U)
                        dve.tensor_copy(row(al, b), X.p_o[:, u, 0:K]).then_inc(s.al_ready, 1)
                dve.wait_ge(s.al_ready, NB + U)
                dve.wait_ge(s.logits_ready, NB // 4)
                dve.wait_ge(s.w_in, 6 * DMA)
                wide = lambda t, n=E: t[:].unsqueeze(2).broadcast_to((P, NB, n))
                rows = lambda t: t[:].unsqueeze(1).broadcast_to((P, NB, K))
                L = T.logits
                chain(dve.tensor_reduce(m1[:], L[:], AX.X, ALU.max))
                dve.tensor_tensor(tmp[:], L[:], wide(m1), ALU.subtract).then_inc(s.max_ready, 1)
                chain(dve.tensor_tensor(al[:], al[:], rows(b2), ALU.add))
                chain(dve.tensor_scalar(al[:], al[:], 30.0, -30.0, ALU.min, ALU.max))
                chain(dve.tensor_reduce(m2[:], al[:], AX.X, ALU.max))
                chain(dve.tensor_tensor(al[:], al[:], wide(m2, K), ALU.is_equal))
                chain(dve.tensor_tensor(al[:], al[:], rows(order), ALU.mult))
                chain(dve.tensor_reduce(k[:], al[:], AX.X, ALU.max))
                chain(dve.tensor_scalar(k[:], k[:], -1.0, K + 1.0, ALU.mult, ALU.add))
                dve.wait_ge(s.exps_ready, 1)
                chain(dve.tensor_reduce(m1[:], tmp[:], AX.X, ALU.add))
                chain(dve.reciprocal(m2[:], m1[:]))
                chain(dve.tensor_tensor(cw[:], tmp[:], wide(m2), ALU.mult))
                chain(dve.memset(rank[:], 0.0))
                for e in range(E):
                    one = cw[:, :, e:e + 1]
                    if e:
                        dve.tensor_tensor(tmp[:, :, 0:e], one.broadcast_to((P, NB, e)), cw[:, :, 0:e], ALU.is_gt)
                    if e < E - 1:
                        dve.tensor_tensor(tmp[:, :, e + 1:E], one.broadcast_to((P, NB, E - 1 - e)), cw[:, :, e + 1:E], ALU.is_ge)
                    chain(dve.memset(tmp[:, :, e:e + 1], 0.0))
                    chain(dve.tensor_tensor(rank[:], rank[:], tmp[:], ALU.add))
                chain(dve.tensor_tensor(rank[:], rank[:], wide(k), ALU.is_lt))
                chain(dve.tensor_tensor(cw[:], cw[:], rank[:], ALU.mult))
                experts_vector(R, dve, s, X)
                dve.wait_ge(s.out_added, E * NG + 2)
                all_row_stats(R, dve, chain)

            @block.scalar
            def _(act):
                flip_scalar(R, act, s, T)
                act.wait_ge(s.w_in, 6 * DMA)
                with act.Fori(0, NB // U) as i:
                    for u, b, n in held(i):
                        act.wait_ge(s.ah_psum, n)
                        act.wait_ge(s.al_psum, (i + 1) * U)
                        act.activation(ah[:, u], X.p_g[0:AH, u, 0:P], ACT.Gelu_apprx_tanh, bias=b1[:]).then_inc(s.ah_ready, 1)
                act.wait_ge(s.max_ready, 1)
                act.activation(tmp[:], tmp[:], ACT.Exp).then_inc(s.exps_ready, 1)
                experts_scalar(act, s, X)

            @block.tensor
            def _(pe):
                pe.wait_ge(s.w_in, 6 * DMA)
                flip_tensor(R, pe, s, T)
                with pe.Fori(0, NB // U) as i:
                    for u, b, n in held(i):
                        pe.wait_ge(s.xT_ready, NB // 4)
                        pe.wait_ge(s.ah_ready, (i + 1) * U)
                        pe.matmul(X.p_g[0:AH, u, 0:P], w1[:], row(T.xTall, b), start=True, stop=True).then_inc(s.ah_psum, 1)
                    for u, b, n in held(i):
                        pe.wait_ge(s.ah_ready, n + U)
                        pe.wait_ge(s.al_ready, (i + 1) * U)
                        pe.matmul(X.p_o[:, u, 0:K], ah[:, u], w2[:], start=True, stop=True).then_inc(s.al_psum, 1)
                pe.wait_ge(s.al_ready, NB + U)
                pe.wait_ge(s.logits_ready, NB // 4)
                experts_tensor(R, pe, s, X, T)


PHASES.append(l2_ffn)
LAYOUTS.append(lambda a: {
    "L2_ffn_router_w": transposed(a, "L2_ffn_router_w"), "L2_ffn_actor_w1": transposed(a, "L2_ffn_actor_w1"),
    "L2_ffn_actor_w2": transposed(a, "L2_ffn_actor_w2"), "L2_ffn_actor_b1": column(a, "L2_ffn_actor_b1"),
    "L2_ffn_actor_b2": repeated(a, "L2_ffn_actor_b2"),
    "c_order6": np.ascontiguousarray(np.broadcast_to(np.arange(6, 0, -1, dtype=np.float32), (P, 6))),
    "L2_ffn_gate_w": transposed(a, "L2_ffn_gate_w", 0, 2, 1), "L2_ffn_up_w": transposed(a, "L2_ffn_up_w", 0, 2, 1),
    "L2_ffn_down_w": np.ascontiguousarray(a["L2_ffn_down_w"].reshape(8, P, 3, 112).transpose(0, 3, 2, 1).reshape(8, 112, 3 * P))})

def l3_attn(nc, R, A):
    HD, NH, HALF = 64, 16, 8
    HC = HALF * HD // P
    with phase(nc, "l3_attn", "var_ready rstd_ready shift_ready w_in vchain squares_ready rms_ready mask_ready xhat_ready xT_psum xT_ready proj_psum "
                   "qv_ready k_ready scores_psum max_ready exp_ready eT_psum eT_ready av_psum heads_ready headsT_psum headsT_ready "
                   "out_psum") as (s, sb, ps):
        wqkv, wout, gam = sb("wqkv", [P, 3 * NH * HD]), sb("wout", [P, 2 * HC, P]), sb("gam", [P, 1])
        maskb, identb = sb("maskb", [P, 4, P], BF16), sb("identb", [P, P], BF16)
        xhat, xT, ssq, rows8 = sb("xhat", [P, U, P]), sb("xT", [P, U, P]), sb("ssq", [P, NB]), sb("rows8", [P, 8, P])
        qT, kT, v = sb("qT", [P, U, 2, HC, P]), sb("kT", [P, U, 2, HC, P]), sb("v", [P, U, NH, HD])
        nm, sums, rden = sb("nm", [P, U, 2, HALF]), sb("sums", [P, U, 2, HALF]), sb("rden", [P, U, HALF])
        E, eT = sb("E", [P, U, HALF, P]), sb("eT", [P, U, HALF, P])
        heads, headsT = sb("heads", [P, U, HALF * HD]), sb("headsT", [P, U, 2 * HC, P])
        p_s, p_w = ps("p_s", [P, U, 2, 512]), ps("p_w", [P, U, 2, 512])

        def halves(i):
            for hf in range(2):
                yield hf, [(u, i * (2 * U) + (hf * U + u + 1)) for u in range(U)]

        with nc.Block() as block:
            @block.sync
            def _(sp):
                load(sp, A, s.w_in, [(wqkv, "L3_attn_w_qkv"), (wout, "L3_attn_w_out"), (gam, "L3_attn_gamma")])

            @block.gpsimd
            def _(pool):
                norm_pool(R, pool, s)
                pool.wait_ge(s.squares_ready, 1)
                pool.tensor_tensor(ssq[:], ssq[:], R.minus_half[:], ALU.pow).then_inc(s.rms_ready, 1)

            @block.vector
            def _(dve):
                chain = Chain(dve, s.vchain)
                norm_vector(R, dve, s)
                dve.tensor_copy(identb[:], R.ident[:])
                dve.tensor_copy(maskb[:], R.causal[:].unsqueeze(1).broadcast_to((P, 4, P))).then_inc(s.mask_ready, 1)
                with dve.Fori(0, NB // 8) as i:
                    chain.restart()
                    for r in range(8):
                        last = normalised(R, dve, i * 8 + r, rows8[:, r])
                    chain(last)
                    chain(dve.tensor_tensor(rows8[:], rows8[:], rows8[:], ALU.mult))
                    chain(dve.tensor_reduce(ssq[:, bass.ds(i * 8, 8)], rows8[:], AX.X, ALU.add))
                dve.tensor_scalar(ssq[:], ssq[:], 1e-24, None, ALU.max).then_inc(s.squares_ready, 1)
                dve.wait_ge(s.rms_ready, 1)
                for t in (R.rstd, R.shift):
                    chain(dve.scalar_tensor_tensor(out=t[:], in0=ssq[:], scalar=float(D) ** 0.5, in1=t[:], op0=ALU.mult, op1=ALU.mult))

                def maxima(rows, hf):
                    for u, n in rows:
                        dve.wait_ge(s.scores_psum, n)
                        dve.tensor_reduce(nm[:, u, hf], p_s[:, u].rearrange("p a (h t) -> p (a h) t", t=P), AX.X, ALU.max,
                                          negate=True).then_inc(s.max_ready, 1)

                def exps_transposed(rows):
                    for u, n in rows:
                        dve.wait_ge(s.eT_psum, n)
                        dve.tensor_copy(eT[:, u].rearrange("p h t -> p (h t)"), p_w[:, u].rearrange("p a t -> p (a t)")).then_inc(s.eT_ready, 1)

                def divided(rows, hf):
                    for u, n in rows:
                        dve.wait_ge(s.av_psum, n)
                        chain(dve.reciprocal(rden[:, u], sums[:, u, hf]))
                        dve.tensor_tensor(heads[:, u].rearrange("p (h e) -> p h e", e=HD), p_w[:, u, 0].rearrange("p (h e) -> p h e", e=HD),
                                          rden[:, u].unsqueeze(2).broadcast_to((P, HALF, HD)), ALU.mult).then_inc(s.heads_ready, 1)

                with dve.Fori(0, NB // U) as i:
                    chain.restart()
                    for u, b, n in held(i):
                        normalised(R, dve, b, xhat[:, u]).then_inc(s.xhat_ready, 1)
                    for u, b, n in held(i):
                        dve.wait_ge(s.proj_psum, i * (2 * U) + (u + 1))
                        dve.tensor_copy(kT[:, u, 0].rearrange("p c t -> p (c t)"), p_w[:, u, 1]).then_inc(s.k_ready, 1)
                    first, second = ([(u, i * (2 * U) + (hf * U + u + 1)) for u in range(U)] for hf in range(2))
                    maxima(first, 0)
                    for u, n in second:
                        dve.wait_ge(s.proj_psum, n)
                        dve.tensor_scalar(qT[:, u, 1].rearrange("p c t -> p (c t)"), p_w[:, u, 0], HD ** -0.5, None, ALU.mult)
                        dve.tensor_copy(kT[:, u, 1].rearrange("p c t -> p (c t)"), p_w[:, u, 1]).then_inc(s.k_ready, 1)
                    exps_transposed(first)
                    maxima(second, 1)
                    divided(first, 0)
                    exps_transposed(second)
                    divided(second, 1)
                    dve.wait_ge(s.out_psum, (i + 1) * U)
                    chain(dve.tensor_tensor(pair(R.x, i), pair(R.x, i), p_w[:, :, 0, 0:P], ALU.add))
                    chain(pair_stats(R, dve, i, chain))

            @block.scalar
            def _(act):
                act.wait_ge(s.w_in, 3 * DMA)
                with act.Fori(0, NB // U) as i:
                    for u, b, n in held(i):
                        act.wait_ge(s.xT_psum, n)
                        act.activation(xT[:, u], p_w[:, u, 0, 0:P], ACT.Copy, scale=gam[:]).then_inc(s.xT_ready, 1)
                    for u, b, n in held(i):
                        act.wait_ge(s.proj_psum, i * (2 * U) + (u + 1))
                        act.activation(qT[:, u, 0].rearrange("p c t -> p (c t)"), p_w[:, u, 0], ACT.Copy, scale=HD ** -0.5)
                        act.activation(v[:, u].rearrange("p h e -> p (h e)"), p_s[:, u].rearrange("p a n -> p (a n)"), ACT.Copy).then_inc(s.qv_ready, 1)
                    for hf, rows in halves(i):
                        for u, n in rows:
                            act.wait_ge(s.max_ready, n)
                            for h in range(HALF):
                                e = act.activation(E[:, u, h], p_s[:, u, h // 4, (h % 4) * P:(h % 4 + 1) * P], ACT.Exp,
                                                   bias=nm[:, u, hf, h:h + 1], accum_out=sums[:, u, hf, h // 4 + 2 * (h % 4):h // 4 + 2 * (h % 4) + 1])
                            e.then_inc(s.exp_ready, 1)
                    for hf, rows in halves(i):
                        for u, n in rows:
                            act.wait_ge(s.headsT_psum, n)
                            act.activation(headsT[:, u, hf * HC:(hf + 1) * HC].rearrange("p c t -> p (c t)"), p_w[:, u, 1], ACT.Copy
                                           ).then_inc(s.headsT_ready, 1)

            @block.tensor
            def _(pe):
                def queries_and_keys(u, hf):
                    for qk in range(2):
                        for c in range(HC):
                            w = qk * NH * HD + (hf * HC + c) * P
                            mm = pe.matmul(p_w[:, u, qk, c * P:(c + 1) * P], wqkv[:, w:w + P], xT[:, u], start=True, stop=True)
                    return mm

                def scores(rows, hf):
                    for u, n in rows:
                        pe.wait_ge(s.k_ready, n)
                        for odd in range(2):
                            pe.matmul(p_s[:, u, odd], identb[:], maskb[:].rearrange("p h t -> p (h t)"), start=True, stop=False,
                                      skip_group_check=True)
                        for c in range(HC):
                            for odd in range(2):
                                f = slice(odd * HD, (odd + 1) * HD)
                                mm = pe.matmul(p_s[:, u, odd, c * P:(c + 1) * P], qT[f, u, hf, c], kT[f, u, hf, c], start=False, stop=True,
                                               skip_group_check=True)
                        mm.then_inc(s.scores_psum, 1)

                def exps_transposed(rows):
                    for u, n in rows:
                        pe.wait_ge(s.exp_ready, n)
                        for h in range(HALF):
                            mm = pe.transpose(p_w[:, u, h // 4, (h % 4) * P:(h % 4 + 1) * P], E[:, u, h], R.ident[:])
                        mm.then_inc(s.eT_psum, 1)

                def weighted(rows, hf):
                    for u, n in rows:
                        pe.wait_ge(s.eT_ready, n)
                        for h in range(HALF):
                            e = (h % 2) * 4 + h // 2
                            mm = pe.matmul(p_w[:, u, 0, h * HD:(h + 1) * HD], eT[:, u, e], v[:, u, hf * HALF + h], start=True, stop=True)
                        mm.then_inc(s.av_psum, 1)
                    for u, n in rows:
                        pe.wait_ge(s.heads_ready, n)
                        for c in range(HC):
                            mm = pe.transpose(p_w[:, u, 1, c * P:(c + 1) * P], heads[:, u, c * P:(c + 1) * P], R.ident[:])
                        mm.then_inc(s.headsT_psum, 1)

                pe.wait_ge(s.w_in, 3 * DMA)
                pe.wait_ge(s.mask_ready, 1)
                with pe.Fori(0, NB // U) as i:
                    for u, b, n in held(i):
                        pe.wait_ge(s.xhat_ready, n)
                        pe.transpose(p_w[:, u, 0, 0:P], xhat[:, u], R.ident[:]).then_inc(s.xT_psum, 1)
                    for u, b, n in held(i):
                        pe.wait_ge(s.xT_ready, n)
                        for a in range(2):
                            w = (2 * NH + a * HALF) * HD
                            pe.matmul(p_s[:, u, a], xT[:, u], wqkv[:, w:w + HALF * HD], start=True, stop=True)
                        queries_and_keys(u, 0).then_inc(s.proj_psum, 1)
                    first, second = ([(u, i * (2 * U) + (hf * U + u + 1)) for u in range(U)] for hf in range(2))
                    for u, b, n in held(i):
                        pe.wait_ge(s.qv_ready, n)
                    scores(first, 0)
                    for u, b, n in held(i):
                        queries_and_keys(u, 1).then_inc(s.proj_psum, 1)
                    for u, n in second:
                        pe.wait_ge(s.k_ready, n)
                    exps_transposed(first)
                    scores(second, 1)
                    weighted(first, 0)
                    for u, n in first:
                        pe.wait_ge(s.headsT_ready, n)
                    exps_transposed(second)
                    weighted(second, 1)
                    for u, b, n in held(i):
                        pe.wait_ge(s.headsT_ready, i * (2 * U) + (U + u + 1))
                        for c in range(2 * HC):
                            mm = pe.matmul(p_w[:, u, 0, 0:P], headsT[:, u, c], wout[:, c], start=(c == 0), stop=(c == 2 * HC - 1))
                        mm.then_inc(s.out_psum, 1)


PHASES.append(l3_attn)
LAYOUTS.append(lambda a: {
    "L3_attn_w_qkv": a["L3_attn_w_qkv"], "L3_attn_w_out": np.ascontiguousarray(a["L3_attn_w_out"].reshape(8, P, P).transpose(1, 0, 2)),
    "L3_attn_gamma": column(a, "L3_attn_gamma")})

def l3_xattn(nc, R, A):
    H, HD, HALF = 16, 8, 8
    with phase(nc, "l3_xattn", "var_ready rstd_ready shift_ready w_in ones_set vchain xhat_ready ctx_ready xT_psum xT_ready kv_psum kv_ready q_psum q_ready kexp_ready "
                   "scores_psum max_ready exp_ready eT_psum eT_ready av_psum heads_ready headsT_psum headsT_ready out_psum"
               ) as (s, sb, ps):
        wq, wo, wkv, bq, bo = sb("wq", [P, P]), sb("wo", [P, P]), sb("wkv", [DC + 1, 256]), sb("bq", [P, 1]), sb("bo", [P, P])
        xhat, xT, cT = sb("xhat", [P, U, P]), sb("xT", [P, U, P]), sb("cT", [DC + 1, U, SC])
        qT, kT, kexp, va = sb("qT", [P, U, P]), sb("kT", [P, U, SC]), sb("kexp", [P, U, H, SC]), sb("va", [SC, U, H, HD + 1])
        nm, E, eT = sb("nm", [P, U, H]), sb("E", [P, U, HALF, SC]), sb("eT", [SC, U, HALF, P])
        rden, heads, headsT = sb("rden", [P, U, H]), sb("heads", [P, U, P]), sb("headsT", [P, U, P])
        p_s, p_e = ps("p_s", [P, U, 2, 512]), ps("p_e", [P, U, 2, 512])

        def halves(i):
            for hf in range(2):
                yield hf, [(u, i * (2 * U) + (hf * U + u + 1)) for u in range(U)]

        with nc.Block() as block:
            @block.sync
            def _(sp):
                load(sp, A, s.w_in, [(wq, "L3_xattn_q_w"), (wo, "L3_xattn_proj_w"), (bq, "L3_xattn_q_b"), (bo, "L3_xattn_proj_b")])
                sp.dma_start(wkv[0:DC], A["L3_xattn_kv_w"]).then_inc(s.w_in, DMA)
                sp.dma_start(wkv[DC:DC + 1], A["L3_xattn_kv_b"]).then_inc(s.w_in, DMA)

            @block.gpsimd
            def _(pool):
                norm_pool(R, pool, s)
                with pool.Fori(0, NB // U) as i:
                    for u, b, n in held(i):
                        pool.wait_ge(s.xhat_ready, n)
                        pool.tensor_copy(cT[:, u], row(R.ctxT, b)).then_inc(s.ctx_ready, 1)

            @block.vector
            def _(dve):
                chain = Chain(dve, s.vchain)
                norm_vector(R, dve, s)
                dve.wait_ge(s.w_in, 6 * DMA)
                dve.tensor_scalar(bq[:], bq[:], HD ** -0.5, None, ALU.mult)
                dve.memset(va[:, :, :, HD:HD + 1], 1.0).then_inc(s.ones_set, 1)

                def maxima(rows, hf):
                    for u, n in rows:
                        dve.wait_ge(s.scores_psum, n)
                        for q in range(2):
                            h = hf * HALF + 4 * q
                            m = dve.tensor_reduce(nm[:, u, h:h + 4], p_s[:, u, q, 0:4 * SC].rearrange("p (h k) -> p h k", h=4), AX.X,
                                                  ALU.max, negate=True)
                        m.then_inc(s.max_ready, 1)

                def exps_transposed(rows):
                    for u, n in rows:
                        dve.wait_ge(s.eT_psum, n)
                        dve.tensor_copy(eT[:, u].rearrange("p h t -> p (h t)"), p_e[0:SC, u].rearrange("p a t -> p (a t)")).then_inc(s.eT_ready, 1)

                def divided(rows, hf):
                    for u, n in rows:
                        dve.wait_ge(s.av_psum, n)
                        h = slice(hf * HALF, (hf + 1) * HALF)
                        av = p_e[:, u, 0, 0:HALF * (HD + 1)].rearrange("p (h e) -> p h e", h=HALF)
                        chain(dve.reciprocal(rden[:, u, h], av[:, :, HD]))
                        dve.tensor_tensor(heads[:, u].rearrange("p (h e) -> p h e", h=H)[:, h], av[:, :, 0:HD],
                                          rden[:, u, h].unsqueeze(2).broadcast_to((P, HALF, HD)), ALU.mult).then_inc(s.heads_ready, 1)

                with dve.Fori(0, NB // U) as i:
                    chain.restart()
                    for u, b, n in held(i):
                        normalised(R, dve, b, xhat[:, u]).then_inc(s.xhat_ready, 1)
                    for u, b, n in held(i):
                        dve.wait_ge(s.kv_ready, n)
                        dve.tensor_tensor(kexp[:, u], kT[:, u].unsqueeze(1).broadcast_to((P, H, SC)),
                                          R.head8[:].unsqueeze(2).broadcast_to((P, H, SC)), ALU.mult).then_inc(s.kexp_ready, 1)
                    first, second = (rows for _, rows in halves(i))
                    maxima(first, 0)
                    exps_transposed(first)
                    maxima(second, 1)
                    divided(first, 0)
                    exps_transposed(second)
                    divided(second, 1)
                    for u, b, n in held(i):
                        chain(dve.tensor_tensor(row(R.x, b), row(R.x, b), bo[:], ALU.add))
                    for u, b, n in held(i):
                        dve.wait_ge(s.out_psum, n)
                        chain(dve.tensor_tensor(row(R.x, b), row(R.x, b), p_e[:, u, 0, 0:P], ALU.add))
                        chain(row_stats(R, dve, b, chain))

            @block.scalar
            def _(act):
                act.wait_ge(s.w_in, 6 * DMA)
                act.wait_ge(s.ones_set, 1)
                with act.Fori(0, NB // U) as i:
                    for u, b, n in held(i):
                        act.wait_ge(s.xT_psum, n)
                        act.activation(xT[:, u], p_e[:, u, 0, 0:P], ACT.Copy).then_inc(s.xT_ready, 1)
                    for u, b, n in held(i):
                        act.wait_ge(s.kv_psum, n)
                        act.activation(kT[:, u], p_s[:, u, 0, 0:SC], ACT.Copy)
                        act.activation(va[:, u, :, 0:HD], p_s[0:SC, u, 0, P:256].rearrange("p (h e) -> p h e", h=H), ACT.Copy
                                       ).then_inc(s.kv_ready, 1)
                        act.wait_ge(s.q_psum, n)
                        act.activation(qT[:, u], p_e[:, u, 0, P:256], ACT.Identity, scale=HD ** -0.5, bias=bq[:]).then_inc(s.q_ready, 1)
                    for hf, rows in halves(i):
                        for u, n in rows:
                            act.wait_ge(s.max_ready, n)
                            for h in range(HALF):
                                e = act.activation(E[:, u, h], p_s[:, u, h // 4, (h % 4) * SC:(h % 4 + 1) * SC], ACT.Exp,
                                                   bias=nm[:, u, hf * HALF + h:hf * HALF + h + 1])
                            e.then_inc(s.exp_ready, 1)
                    for u, b, n in held(i):
                        act.wait_ge(s.headsT_psum, n)
                        act.activation(headsT[:, u], p_s[:, u, 1, 0:P], ACT.Copy).then_inc(s.headsT_ready, 1)

            @block.tensor
            def _(pe):
                def scores(rows, hf):
                    for u, n in rows:
                        for q in range(2):
                            h = hf * HALF + 4 * q
                            mm = pe.matmul(p_s[:, u, q, 0:4 * SC], qT[:, u], kexp[:, u, h:h + 4].rearrange("p h k -> p (h k)"), start=True, stop=True)
                        mm.then_inc(s.scores_psum, 1)

                def exps_transposed(rows):
                    for u, n in rows:
                        pe.wait_ge(s.exp_ready, n)
                        for h in range(HALF):
                            mm = pe.transpose(p_e[0:SC, u, h // 4, (h % 4) * P:(h % 4 + 1) * P], E[:, u, h], R.ident[:])
                        mm.then_inc(s.eT_psum, 1)

                def weighted(rows, hf):
                    for u, n in rows:
                        pe.wait_ge(s.eT_ready, n)
                        for h in range(HALF):
                            mm = pe.matmul(p_e[:, u, 0, h * (HD + 1):(h + 1) * (HD + 1)], eT[:, u, h], va[:, u, hf * HALF + h], start=True, stop=True)
                        mm.then_inc(s.av_psum, 1)

                pe.wait_ge(s.w_in, 6 * DMA)
                with pe.Fori(0, NB // U) as i:
                    for u, b, n in held(i):
                        pe.wait_ge(s.xhat_ready, n)
                        pe.transpose(p_e[:, u, 0, 0:P], xhat[:, u], R.ident[:]).then_inc(s.xT_psum, 1)
                    for u, b, n in held(i):
                        pe.wait_ge(s.ctx_ready, n)
                        pe.matmul(p_s[:, u, 0, 0:SC], wkv[:, 0:P], cT[:, u], start=True, stop=True)
                        pe.matmul(p_s[0:SC, u, 0, P:256], cT[:, u], wkv[:, P:256], start=True, stop=True).then_inc(s.kv_psum, 1)
                        pe.wait_ge(s.xT_ready, n)
                        pe.matmul(p_e[:, u, 0, P:256], wq[:], xT[:, u], start=True, stop=True).then_inc(s.q_psum, 1)
                    first, second = (rows for _, rows in halves(i))
                    pe.wait_ge(s.kexp_ready, (i + 1) * U)
                    pe.wait_ge(s.q_ready, (i + 1) * U)
                    scores(first, 0)
                    exps_transposed(first)
                    scores(second, 1)
                    weighted(first, 0)
                    pe.wait_ge(s.heads_ready, i * (2 * U) + U)
                    exps_transposed(second)
                    weighted(second, 1)
                    for u, b, n in held(i):
                        pe.wait_ge(s.heads_ready, i * (2 * U) + (U + u + 1))
                        pe.transpose(p_s[:, u, 1, 0:P], heads[:, u], R.ident[:]).then_inc(s.headsT_psum, 1)
                    for u, b, n in held(i):
                        pe.wait_ge(s.headsT_ready, n)
                        pe.matmul(p_e[:, u, 0, 0:P], headsT[:, u], wo[:], start=True, stop=True).then_inc(s.out_psum, 1)


PHASES.append(l3_xattn)
LAYOUTS.append(lambda a: {
    "L3_xattn_q_w": a["L3_xattn_q_w"], "L3_xattn_proj_w": a["L3_xattn_proj_w"], "L3_xattn_q_b": column(a, "L3_xattn_q_b"),
    "L3_xattn_proj_b": repeated(a, "L3_xattn_proj_b"), "L3_xattn_kv_w": a["L3_xattn_kv_w"], "L3_xattn_kv_b": a["L3_xattn_kv_b"].reshape(1, -1)})

def l3_ffn(nc, R, A):
    H, NK, K, NE, HF = 4, 64, 8, 512, 4
    NA, NG_ = H * K * K, H * NE
    with phase(nc, "l3_ffn", "var_ready rstd_ready shift_ready w_in vchain xhat_ready xT_psum xT_ready q_psum q_ready sim_psum sums_ready exp_ready "
                   "weights_ready silu_ready picks_ready up_psum h_ready wT_psum wT_ready out_psum") as (s, sb, ps):
        wq, keys, down = sb("wq", [P, NE]), sb("keys", [P, HF, P]), sb("down", [P, NE])
        up, wup, wdn = sb("up", [P, HF, P]), sb("wup", [P, NE]), sb("wdn", [P, HF, P])
        xhat, xT, qT = sb("xhat", [P, U, P]), sb("xT", [P, U, P]), sb("qT", [P, U, HF, P])
        top, idx, other = sb("top", [P, U, 2, H, K]), sb("idx", [P, U, H, K], U32), sb("other", [P, U, H, K])
        m, bestx, gridx = sb("m", [P, U, H]), sb("bestx", [P, U, H, K]), sb("gridx", [P, U, H, K])
        sums, w = sb("sums", [P, U, NA + NG_]), sb("w", [P, U, NA + NG_])
        cut, z, rest = sb("cut", [P, U, H, K]), sb("z", [P, U, 2, H]), sb("rest", [P, U])
        hT, wT = sb("hT", [P, U, HF, P]), sb("wT", [P, U, HF, P])
        p_x, p_sim, p_dot = ps("p_x", [P, U, 512]), ps("p_sim", [P, U, 512]), ps("p_dot", [P, U, 512])
        with nc.Block() as block:
            @block.sync
            def _(sp):
                load(sp, A, s.w_in, [(wq, "L3_ffn_W_q"), (keys, "L3_ffn_keys"), (down, "L3_ffn_down_embed"), (up, "L3_ffn_up_embed"),
                                     (wup, "L3_ffn_W_up"), (wdn, "L3_ffn_W_down")])

            @block.gpsimd
            def _(pool):
                norm_pool(R, pool, s)

            @block.vector
            def _(dve):
                chain = Chain(dve, s.vchain)
                norm_vector(R, dve, s)

                def four(t):
                    return t.rearrange("p (h i j) -> p h i j", h=H, i=K)

                with dve.Fori(0, NB // U) as i:
                    chain.restart()
                    for u, b, n in held(i):
                        normalised(R, dve, b, xhat[:, u]).then_inc(s.xhat_ready, 1)
                    for u, b, n in held(i):
                        dve.wait_ge(s.sim_psum, n)
                        sim = p_sim[:, u].rearrange("p (a h k) -> p a h k", a=2, h=H)
                        chain(dve.tensor_copy(gridx[:, u], sim[:, 0, :, 0:K]))
                        for xy in range(2):
                            for h in range(H):
                                last = dve.max(top[:, u, xy, h], sim[:, xy, h])
                        chain(last)
                        for h in range(H):
                            dve.max_index(idx[:, u, h], top[:, u, 0, h], sim[:, 0, h])
                        chain(dve.tensor_tensor(m[:, u], top[:, u, 0, :, 0], top[:, u, 1, :, 0], ALU.add))
                        wide = m[:, u].unsqueeze(2).broadcast_to((P, H, K))
                        dve.tensor_tensor(bestx[:, u], top[:, u, 0], wide, ALU.subtract)
                        chain(dve.tensor_tensor(gridx[:, u], gridx[:, u], wide, ALU.subtract))
                        for h in range(H):
                            dve.tensor_tensor(sums[:, u, h * K * K:(h + 1) * K * K].rearrange("p (i j) -> p i j", i=K),
                                              bestx[:, u, h].unsqueeze(2).broadcast_to((P, K, K)),
                                              top[:, u, 1, h].unsqueeze(1).broadcast_to((P, K, K)), ALU.add)
                            g = NA + h * NE
                            last = dve.tensor_tensor(sums[:, u, g:g + NE].rearrange("p (i j) -> p i j", i=K),
                                                     gridx[:, u, h].unsqueeze(2).broadcast_to((P, K, NK)),
                                                     sim[:, 1, h].unsqueeze(1).broadcast_to((P, K, NK)), ALU.add)
                        last.then_inc(s.sums_ready, 1)
                        dve.wait_ge(s.sums_ready, n)
                        dve.tensor_scalar(other[:, u], idx[:, u], float(K), None, ALU.is_ge)
                        for h in range(H):
                            last = dve.max(cut[:, u, h], sums[:, u, h * K * K:(h + 1) * K * K])
                        chain(last)
                    for u, b, n in held(i):
                        dve.wait_ge(s.exp_ready, n)
                        for h in range(H):
                            a = slice(h * K * K, (h + 1) * K * K)
                            last = dve.scalar_tensor_tensor(out=w[:, u, a], in0=sums[:, u, a], scalar=cut[:, u, h, K - 1:K], in1=w[:, u, a],
                                                            op0=ALU.is_ge, op1=ALU.mult)
                            g = slice(NA + h * NE, NA + (h + 1) * NE)
                            last = dve.scalar_tensor_tensor(out=w[:, u, g], in0=sums[:, u, g], scalar=cut[:, u, h, K - 1:K], in1=w[:, u, g],
                                                            op0=ALU.is_ge, op1=ALU.mult)
                        chain(last)
                        chain(dve.tensor_reduce(z[:, u, 0], w[:, u, 0:NA].rearrange("p (h k) -> p h k", h=H), AX.X, ALU.add))
                        chain(dve.reciprocal(z[:, u, 1], z[:, u, 0]))
                        for h in range(H):
                            a = slice(h * K * K, (h + 1) * K * K)
                            dve.tensor_scalar(w[:, u, a], w[:, u, a], z[:, u, 1, h:h + 1], p_dot[:, u, NE - 1:NE], ALU.mult, ALU.mult)
                            g = slice(NA + h * NE, NA + (h + 1) * NE)
                            last = dve.scalar_tensor_tensor(out=w[:, u, g], in0=w[:, u, g], scalar=z[:, u, 1, h:h + 1], in1=p_dot[:, u],
                                                            op0=ALU.mult, op1=ALU.mult)
                        last.then_inc(s.weights_ready, 1)
                    for u, b, n in held(i):
                        dve.wait_ge(s.silu_ready, n)
                        chain(dve.tensor_tensor(w[:, u, 0:NA].rearrange("p (h k) -> p h k", k=K), w[:, u, 0:NA].rearrange("p (h k) -> p h k", k=K),
                                                other[:, u].rearrange("p h i -> p (h i)").unsqueeze(2).broadcast_to((P, H * K, K)), ALU.mult))
                        chain(dve.tensor_reduce(rest[:, u:u + 1], w[:, u, 0:NA], AX.X, ALU.add))
                        e = slice(NA + NE - 1, NA + NE)
                        chain(dve.tensor_tensor(w[:, u, e], w[:, u, e], rest[:, u:u + 1], ALU.add))
                        a, b_ = NA, NA + 2 * NE
                        chain(dve.tensor_tensor(w[:, u, a:a + 2 * NE], w[:, u, a:a + 2 * NE], w[:, u, b_:b_ + 2 * NE], ALU.add))
                        dve.tensor_tensor(w[:, u, a:a + NE], w[:, u, a:a + NE], w[:, u, a + NE:a + 2 * NE], ALU.add).then_inc(s.picks_ready, 1)
                    for u, b, n in held(i):
                        dve.wait_ge(s.out_psum, n)
                        chain(dve.tensor_tensor(row(R.x, b), row(R.x, b), p_dot[:, u, 0:P], ALU.add))

            @block.scalar
            def _(act):
                with act.Fori(0, NB // U) as i:
                    for u, b, n in held(i):
                        act.wait_ge(s.xT_psum, n)
                        act.activation(xT[:, u], p_x[:, u, 0:P], ACT.Copy).then_inc(s.xT_ready, 1)
                    for u, b, n in held(i):
                        act.wait_ge(s.q_psum, n)
                        act.activation(qT[:, u].rearrange("p c t -> p (c t)"), p_x[:, u], ACT.Copy).then_inc(s.q_ready, 1)
                    for u, b, n in held(i):
                        act.wait_ge(s.sums_ready, n)
                        act.activation(w[:, u], sums[:, u], ACT.Exp).then_inc(s.exp_ready, 1)
                    for u, b, n in held(i):
                        act.wait_ge(s.up_psum, n)
                        act.activation(hT[:, u].rearrange("p c t -> p (c t)"), p_x[:, u], ACT.Silu).then_inc(s.h_ready, 1)
                    for u, b, n in held(i):
                        act.wait_ge(s.weights_ready, n)
                        act.activation(w[:, u], w[:, u], ACT.Silu).then_inc(s.silu_ready, 1)
                    for u, b, n in held(i):
                        act.wait_ge(s.wT_psum, n)
                        act.activation(wT[:, u].rearrange("p c t -> p (c t)"), p_sim[:, u], ACT.Copy).then_inc(s.wT_ready, 1)

            @block.tensor
            def _(pe):
                pe.wait_ge(s.w_in, 6 * DMA)
                with pe.Fori(0, NB // U) as i:
                    for u, b, n in held(i):
                        pe.wait_ge(s.xhat_ready, n)
                        pe.transpose(p_x[:, u, 0:P], xhat[:, u], R.ident[:]).then_inc(s.xT_psum, 1)
                    for u, b, n in held(i):
                        pe.wait_ge(s.xT_ready, n)
                        for c in range(HF):
                            mm = pe.matmul(p_x[:, u, c * P:(c + 1) * P], wq[:, c * P:(c + 1) * P], xT[:, u], start=True, stop=True)
                        mm.then_inc(s.q_psum, 1)
                    for u, b, n in held(i):
                        pe.matmul(p_dot[:, u], xT[:, u], down[:], start=True, stop=True)
                        pe.wait_ge(s.q_ready, n)
                        for c in range(HF):
                            mm = pe.matmul(p_sim[:, u, c * P:(c + 1) * P], qT[:, u, c], keys[:, c], start=True, stop=True)
                        mm.then_inc(s.sim_psum, 1)
                    for u, b, n in held(i):
                        for c in range(HF):
                            mm = pe.matmul(p_x[:, u, c * P:(c + 1) * P], wup[:, c * P:(c + 1) * P], xT[:, u], start=True, stop=True)
                        mm.then_inc(s.up_psum, 1)
                    for u, b, n in held(i):
                        pe.wait_ge(s.picks_ready, n)
                        for c in range(HF):
                            mm = pe.transpose(p_sim[:, u, c * P:(c + 1) * P], w[:, u, NA + c * P:NA + (c + 1) * P], R.ident[:])
                        mm.then_inc(s.wT_psum, 1)
                    for u, b, n in held(i):
                        pe.wait_ge(s.h_ready, n)
                        pe.wait_ge(s.wT_ready, n)
                        for c in range(HF):
                            pe.matmul(p_dot[:, u, 0:P], hT[:, u, c], wdn[:, c], start=(c == 0), stop=False)
                        for c in range(HF):
                            mm = pe.matmul(p_dot[:, u, 0:P], wT[:, u, c], up[:, c], start=False, stop=(c == HF - 1))
                        mm.then_inc(s.out_psum, 1)


PHASES.append(l3_ffn)


def layout_l3_ffn(a):
    keys = np.zeros((4, 2, 64, 2, 64), np.float32)
    for c in range(4):
        for j in range(2):
            keys[c, j, :, j] = a["L3_ffn_keys"][2 * (c % 2) + j, :, c // 2].T
    chunks = lambda w: np.ascontiguousarray(w.reshape(4, P, P).transpose(1, 0, 2))
    return {
        "L3_ffn_W_q": transposed(a, "L3_ffn_W_q"), "L3_ffn_keys": chunks(keys.reshape(4, P, P)),
        "L3_ffn_down_embed": transposed(a, "L3_ffn_down_embed"), "L3_ffn_up_embed": chunks(a["L3_ffn_up_embed"]),
        "L3_ffn_W_up": transposed(a, "L3_ffn_W_up"), "L3_ffn_W_down": chunks(transposed(a, "L3_ffn_W_down"))}


LAYOUTS.append(layout_l3_ffn)

def decoder(nc, A, out):
    with ExitStack() as ctx:
        def sb(name, shape, dt=F32):
            return ctx.enter_context(nc.sbuf_tensor(name, shape, dt))

        R = Named()
        R.x = sb("x", [P, NB, D])
        R.stats = sb("stats", [P, NB, 2])
        R.vareps = sb("vareps", [P, NB])
        R.rstd = sb("rstd", [P, NB])
        R.shift = sb("shift", [P, NB])
        R.minus_half = sb("minus_half", [P, NB])
        R.bn = sb("bn", [P, 8, 6])
        R.aggr = sb("aggr", [P, 8, 2])
        R.ident = sb("ident", [P, P])
        R.ones = sb("ones", [P, P])
        R.ctxT = sb("ctxT", [DC + 1, NB, SC])
        R.causal = sb("causal", [P, P])
        R.head8 = sb("head8", [P, 16])
        R.cap = sb("cap", [P, P])
        R.ssm_rows = nc.dram_tensor("ssm_rows", (P, 2 * S), F32, kind="Internal").ap()
        R.scattered = [ctx.enter_context(nc.semaphore(f"scattered{u}")) for u in range(U)]
        R.fetched = [ctx.enter_context(nc.semaphore(f"fetched{u}")) for u in range(4)]
        with phase(nc, "load", "x_in consts_in fills_done row_done vchain") as (s, _, _):
            with nc.Block() as block:
                @block.sync
                def _(sp):
                    sp.dma_start(R.x[:], A["x"]).then_inc(s.x_in, DMA)
                    sp.dma_start(R.ctxT[0:DC], A["ctx_768"]).then_inc(s.consts_in, DMA)
                    sp.dma_start(R.ident[:], A["c_ident"]).then_inc(s.consts_in, DMA)
                    sp.dma_start(R.causal[:], A["c_causal"]).then_inc(s.consts_in, DMA)
                    sp.dma_start(R.head8[:], A["c_head8"]).then_inc(s.consts_in, DMA)
                    sp.wait_ge(s.consts_in, 4 * DMA)

                @block.gpsimd
                def _(pool):
                    pool.memset(R.ones[:], 1.0)
                    pool.memset(R.minus_half[:], -0.5).then_inc(s.fills_done, 1)

                @block.vector
                def _(dve):
                    dve.memset(R.ctxT[DC:DC + 1], 1.0)
                    dve.wait_ge(s.x_in, DMA)
                    all_row_stats(R, dve, Chain(dve, s.vchain))
        for p in PHASES:
            p(nc, R, A)
        with phase(nc, "store", "stored") as (s, _, _):
            with nc.Block() as block:
                @block.sync
                def _(sp):
                    sp.dma_start(out, R.x[:]).then_inc(s.stored, DMA)
                    sp.wait_ge(s.stored, DMA)


def constants():
    return {
        "c_ident": np.eye(P, dtype=np.float32),
        "c_causal": np.where(np.arange(P)[None, :] <= np.arange(P)[:, None], 0.0, -3e38).astype(np.float32),
        "c_head8": (np.arange(P)[:, None] // 8 == np.arange(16)[None, :]).astype(np.float32),
    }


def laid_out(a):
    out = {"x": transposed(a, "x", 1, 0, 2), "ctx_768": transposed(a, "ctx_768", 2, 0, 1)}
    for layout in LAYOUTS:
        out.update(layout(a))
    return out


def kernel(**inputs):
    import concourse.bacc as _bacc
    from concourse.bass_utils import run_bass_kernel_spmd as _run

    arrays = laid_out({k: np.asarray(v) for k, v in inputs.items()})
    arrays.update(constants())
    nc = _bacc.Bacc("TRN2", target_bir_lowering=False, num_devices=1)
    A = {n: nc.dram_tensor(f"in_{n}", a.shape, mybir.dt.from_np(a.dtype), kind="ExternalInput").ap()
         for n, a in arrays.items()}
    out = nc.dram_tensor("out", (P, NB, D), F32, kind="ExternalOutput").ap()
    decoder(nc, A, out)
    r = _run(nc, [{f"in_{n}": a for n, a in arrays.items()}], core_ids=[0])
    return np.ascontiguousarray(np.transpose(r.results[0]["out"], (1, 0, 2)))
```
